# Optimizing a Trainium2 kernel written in Bass

```python
import numpy as np
import jax
import jax.numpy as jnp

def _softmax(x, axis=-1):
    return jax.nn.softmax(x, axis=axis)

def _gelu(x):
    return jax.nn.gelu(x, approximate=True)

def _silu(x):
    return jax.nn.silu(x)

def _sigmoid(x):
    return jax.nn.sigmoid(x)

def _layernorm(x, axis=-1, eps=1e-05):
    m = jnp.mean(x, axis=axis, keepdims=True)
    v = jnp.var(x, axis=axis, keepdims=True)
    return (x - m) / jnp.sqrt(v + eps)

def _scatter_add(tgt, idx, src, axis=0):
    return tgt.at[idx].add(src)

def _segment_sum(src, seg, n):
    return jax.ops.segment_sum(src, seg, n)
kernel_name = 'mk_gnn_preln_d4_gnn_r8_85c12c'

def setup_inputs(seed: int=0):
    np.random.seed(seed)
    _w = jnp.asarray

    def _rec_inputs():
        import jax
        import jax.numpy as jnp
        _gk = jax.random.key(seed)
        x = -0.0003713 + 1 * jax.random.normal(jax.random.fold_in(_gk, 1), (6250, 128), jnp.float32)
        src = jax.random.randint(jax.random.fold_in(_gk, 2), (100000,), 0, 6250, jnp.int32)
        dst = jax.random.randint(jax.random.fold_in(_gk, 3), (100000,), 0, 6250, jnp.int32)
        _o = jnp.argsort(dst, stable=True)
        src = src[_o]
        dst = dst[_o]
        edge_attr_128 = 5.93493e-05 + 1.00006 * jax.random.normal(jax.random.fold_in(_gk, 11), (100000, 128), jnp.float32)
        return (x, src, dst, edge_attr_128)
    x, src, dst, edge_attr_128 = _rec_inputs()

    def _L0_gnn_setup():
        import jax, jax.numpy as jnp
        import numpy as np
        ALPHA = 0.2
        LN_EPS = 1e-05
        key = jax.random.key(seed)
        ks = jax.random.split(key, 6)
        N, E, D = (12500, 75000, 128)
        x = jax.random.normal(ks[0], (N, D), dtype=jnp.float32)
        edge_index = jax.random.randint(ks[1], (2, E), 0, N, dtype=jnp.int64)
        W1 = jax.random.normal(ks[2], (D, D // 2), dtype=jnp.float32) * (1.0 / np.sqrt(D))
        b1 = jnp.zeros((D // 2,), dtype=jnp.float32)
        W2 = jax.random.normal(ks[3], (D // 2, D), dtype=jnp.float32) * (1.0 / np.sqrt(D // 2))
        b2 = jnp.zeros((D,), dtype=jnp.float32)
        gamma = jnp.ones((D,), dtype=jnp.float32)
        beta = jnp.zeros((D,), dtype=jnp.float32)
        return {'x': x, 'edge_index': edge_index, 'W1': W1, 'b1': b1, 'W2': W2, 'b2': b2, 'gamma': gamma, 'beta': beta}
    _L0_gnn_all = _L0_gnn_setup()
    _L0_gnn_in = {k: v for k, v in _L0_gnn_all.items() if k in ('W1', 'b1', 'W2', 'b2', 'gamma', 'beta')}
    del _L0_gnn_all

    def _L1_gnn_setup():
        import jax, jax.numpy as jnp
        import numpy as np
        N, E = (6250, 75000)
        ND, ED, HD = (128, 128, 128)
        EPS = 1e-05
        key = jax.random.key(seed)
        ks = jax.random.split(key, 8)
        w = lambda k, shape: jax.random.normal(k, shape, jnp.float32) * 0.05
        return {'node_features': jax.random.normal(ks[0], (N, ND), jnp.float32), 'edge_index': jax.random.randint(ks[1], (2, E), 0, N, jnp.int32), 'edge_attr': jax.random.normal(ks[2], (E, ED), jnp.float32), 'W1': w(ks[3], (2 * ND + ED, HD)), 'b1': jnp.zeros((HD,), jnp.float32), 'W2': w(ks[4], (HD, HD)), 'b2': jnp.zeros((HD,), jnp.float32), 'U1': w(ks[5], (ND + HD, HD)), 'ub1': jnp.zeros((HD,), jnp.float32), 'U2': w(ks[6], (HD, HD)), 'ub2': jnp.zeros((HD,), jnp.float32), 'gamma': jnp.ones((HD,), jnp.float32), 'beta': jnp.zeros((HD,), jnp.float32)}
    _L1_gnn_all = _L1_gnn_setup()
    _L1_gnn_in = {k: v for k, v in _L1_gnn_all.items() if k in ('W1', 'b1', 'W2', 'b2', 'U1', 'ub1', 'U2', 'ub2', 'gamma', 'beta')}
    del _L1_gnn_all

    def _L2_gnn_setup():
        import jax, jax.numpy as jnp
        import numpy as np
        N_NODES = 12500
        N_EDGES = 200000
        IN_DIM = 128
        OUT_DIM = 128
        ALPHA = 0.2
        EPS = 9e-15
        key = jax.random.key(seed)
        k1, k2, k3, k4, k5 = jax.random.split(key, 5)
        x = jax.random.normal(k1, (N_NODES, IN_DIM), dtype=jnp.float32)
        src = jax.random.randint(k2, (N_EDGES,), 0, N_NODES)
        dst = jax.random.randint(k3, (N_EDGES,), 0, N_NODES)
        edge_index = jnp.stack([src, dst]).astype(jnp.int64)
        W = jax.random.normal(k4, (IN_DIM, OUT_DIM), dtype=jnp.float32) * (1.414 * np.sqrt(2.0 / (IN_DIM + OUT_DIM)))
        attn = jax.random.normal(k5, (1, 2 * OUT_DIM), dtype=jnp.float32) * (1.414 * np.sqrt(2.0 / (1 + 2 * OUT_DIM)))
        return {'x': x, 'edge_index': edge_index, 'W': W, 'attn': attn}
    _L2_gnn_all = _L2_gnn_setup()
    _L2_gnn_in = {k: v for k, v in _L2_gnn_all.items() if k in ('W', 'attn')}
    del _L2_gnn_all

    def _L3_gnn_setup():
        import jax, jax.numpy as jnp
        import numpy as np
        N_NODES = 12500
        N_EDGES = 200000
        IN_CH = 128
        OUT_CH = 32
        HEADS = 4
        NEG_SLOPE = 0.2
        key = jax.random.key(seed)
        k1, k2, k3, k4 = jax.random.split(key, 4)
        x = jax.random.normal(k1, (N_NODES, IN_CH), dtype=jnp.float32)
        weight = jax.random.normal(k2, (IN_CH, HEADS * OUT_CH), dtype=jnp.float32) * 0.1
        att = jax.random.normal(k3, (1, HEADS, 2 * OUT_CH), dtype=jnp.float32) * 0.1
        edge_index = jax.random.randint(k4, (2, N_EDGES), 0, N_NODES, dtype=jnp.int64)
        return {'x': x, 'weight': weight, 'att': att, 'edge_index': edge_index}
    _L3_gnn_all = _L3_gnn_setup()
    _L3_gnn_in = {k: v for k, v in _L3_gnn_all.items() if k in ('weight', 'att')}
    del _L3_gnn_all
    return {'x': x, 'src': src, 'dst': dst, 'edge_attr_128': edge_attr_128, 'L0_gnn_W1': _L0_gnn_in['W1'], 'L0_gnn_b1': _L0_gnn_in['b1'], 'L0_gnn_W2': _L0_gnn_in['W2'], 'L0_gnn_b2': _L0_gnn_in['b2'], 'L0_gnn_gamma': _L0_gnn_in['gamma'], 'L0_gnn_beta': _L0_gnn_in['beta'], 'L1_gnn_W1': _L1_gnn_in['W1'], 'L1_gnn_b1': _L1_gnn_in['b1'], 'L1_gnn_W2': _L1_gnn_in['W2'], 'L1_gnn_b2': _L1_gnn_in['b2'], 'L1_gnn_U1': _L1_gnn_in['U1'], 'L1_gnn_ub1': _L1_gnn_in['ub1'], 'L1_gnn_U2': _L1_gnn_in['U2'], 'L1_gnn_ub2': _L1_gnn_in['ub2'], 'L1_gnn_gamma': _L1_gnn_in['gamma'], 'L1_gnn_beta': _L1_gnn_in['beta'], 'L2_gnn_W': _L2_gnn_in['W'], 'L2_gnn_attn': _L2_gnn_in['attn'], 'L3_gnn_weight': _L3_gnn_in['weight'], 'L3_gnn_att': _L3_gnn_in['att']}

def reference(x, src, dst, edge_attr_128, L0_gnn_W1, L0_gnn_b1, L0_gnn_W2, L0_gnn_b2, L0_gnn_gamma, L0_gnn_beta, L1_gnn_W1, L1_gnn_b1, L1_gnn_W2, L1_gnn_b2, L1_gnn_U1, L1_gnn_ub1, L1_gnn_U2, L1_gnn_ub2, L1_gnn_gamma, L1_gnn_beta, L2_gnn_W, L2_gnn_attn, L3_gnn_weight, L3_gnn_att):
    import jax
    import jax.numpy as jnp

    def _L0_gnn_ref(x, edge_index, W1, b1, W2, b2, gamma, beta):
        import jax, jax.numpy as jnp
        import numpy as np
        ALPHA = 0.2
        LN_EPS = 1e-05
        N = x.shape[0]
        src, dst = (edge_index[0], edge_index[1])
        msg_sum = jax.ops.segment_sum(x[src], dst, num_segments=N)
        cnt = jax.ops.segment_sum(jnp.ones_like(dst, dtype=x.dtype), dst, num_segments=N)
        local_mean = msg_sum / jnp.maximum(cnt, 1.0)[:, None]
        feature_diff = jnp.tanh(jnp.linalg.norm(x - local_mean, axis=1, keepdims=True))
        enhanced = jax.nn.relu(x @ W1 + b1) @ W2 + b2
        h = x + ALPHA * enhanced * feature_diff
        mu = jnp.mean(h, axis=-1, keepdims=True)
        var = jnp.var(h, axis=-1, keepdims=True)
        return (h - mu) * jax.lax.rsqrt(var + LN_EPS) * gamma + beta

    def _L1_gnn_ref(node_features, edge_index, edge_attr, W1, b1, W2, b2, U1, ub1, U2, ub2, gamma, beta):
        import jax, jax.numpy as jnp
        import numpy as np
        N, E = (6250, 75000)
        ND, ED, HD = (128, 128, 128)
        EPS = 1e-05
        row, col = (edge_index[0], edge_index[1])
        edge_features = jnp.concatenate([node_features[row], node_features[col], edge_attr], axis=-1)
        messages = jax.nn.softplus(edge_features @ W1 + b1) @ W2 + b2
        aggregated = jax.ops.segment_sum(messages, row, num_segments=node_features.shape[0])
        combined = jnp.concatenate([node_features, aggregated], axis=-1)
        updated = jax.nn.softplus(combined @ U1 + ub1) @ U2 + ub2
        mu = jnp.mean(updated, axis=0)
        var = jnp.var(updated, axis=0)
        return (updated - mu) * jax.lax.rsqrt(var + EPS) * gamma + beta

    def _L2_gnn_ref(x, edge_index, W, attn):
        import jax, jax.numpy as jnp
        import numpy as np
        N_NODES = 12500
        N_EDGES = 200000
        IN_DIM = 128
        OUT_DIM = 128
        ALPHA = 0.2
        EPS = 9e-15
        N = x.shape[0]
        h = x @ W
        d = h.shape[1]
        a_src, a_dst = (attn[0, :d], attn[0, d:])
        src, dst = (edge_index[0], edge_index[1])
        values = (h @ a_src)[src] + (h @ a_dst)[dst]
        e_a = jnp.where(values > 0, values, ALPHA * values)
        edge_e = jnp.exp(e_a - jnp.max(e_a))
        rowsum = jax.ops.segment_sum(edge_e, src, num_segments=N)
        h_prime = jax.ops.segment_sum(edge_e[:, None] * h[dst], src, num_segments=N)
        h_prime = h_prime / (rowsum[:, None] + EPS)
        return jax.nn.elu(h_prime)

    def _L3_gnn_ref(x, weight, att, edge_index):
        import jax, jax.numpy as jnp
        import numpy as np
        N_NODES = 12500
        N_EDGES = 200000
        IN_CH = 128
        OUT_CH = 32
        HEADS = 4
        NEG_SLOPE = 0.2
        num_nodes = x.shape[0]
        h = jnp.matmul(x, weight).reshape(num_nodes, HEADS, OUT_CH)
        row, col = (edge_index[0], edge_index[1])
        x_i = h[row]
        x_j = h[col]
        a_i = att[0, :, :OUT_CH]
        a_j = att[0, :, OUT_CH:]
        alpha = jnp.einsum('ehc,hc->eh', x_i, a_i) + jnp.einsum('ehc,hc->eh', x_j, a_j)
        alpha = jnp.where(alpha >= 0, alpha, NEG_SLOPE * alpha)
        amax = jax.ops.segment_max(alpha, col, num_segments=num_nodes)
        amax = jnp.where(jnp.isfinite(amax), amax, 0.0)
        e = jnp.exp(alpha - amax[col])
        s = jax.ops.segment_sum(e, col, num_segments=num_nodes)
        alpha = e / (s[col] + 1e-16)
        msg = x_j * alpha[:, :, None]
        out = jax.ops.segment_sum(msg, col, num_segments=num_nodes)
        return out.reshape(num_nodes, HEADS * OUT_CH)
    edge_index = jnp.stack([src, dst])
    h = jnp.maximum(_layernorm(x, axis=-1), 0.0)
    x = x + _L0_gnn_ref(h, edge_index, L0_gnn_W1, L0_gnn_b1, L0_gnn_W2, L0_gnn_b2, L0_gnn_gamma, L0_gnn_beta)
    h = jnp.maximum(_layernorm(x, axis=-1), 0.0)
    x = x + _L1_gnn_ref(h, edge_index, edge_attr_128, L1_gnn_W1, L1_gnn_b1, L1_gnn_W2, L1_gnn_b2, L1_gnn_U1, L1_gnn_ub1, L1_gnn_U2, L1_gnn_ub2, L1_gnn_gamma, L1_gnn_beta)
    h = jnp.maximum(_layernorm(x, axis=-1), 0.0)
    x = x + _L2_gnn_ref(h, edge_index, L2_gnn_W, L2_gnn_attn)
    h = jnp.maximum(_layernorm(x, axis=-1), 0.0)
    x = x + _L3_gnn_ref(h, L3_gnn_weight, L3_gnn_att, edge_index)
    return x

_drawn_inputs = setup_inputs


def setup_inputs(seed=0):
    import zlib

    import numpy as np

    out = dict(_drawn_inputs(seed))
    spreads = {'L0_gnn_b1': (0.0, 0.755),
     'L0_gnn_b2': (0.0, 0.538),
     'L0_gnn_gamma': (1.0, 0.2),
     'L0_gnn_beta': (0.0, 0.1),
     'L1_gnn_b1': (0.0, 0.1),
     'L1_gnn_b2': (0.0, 0.1),
     'L1_gnn_ub1': (0.0, 0.8),
     'L1_gnn_ub2': (0.0, 0.8),
     'L1_gnn_gamma': (1.0, 0.2),
     'L1_gnn_beta': (0.0, 0.1)}
    factors = {'L3_gnn_att': 8.0}
    for name, (base, spread) in spreads.items():
        noise = np.random.default_rng([zlib.crc32(name.encode()), seed]).standard_normal(out[name].shape)
        drawn = base * np.exp(spread * noise) if base else spread * noise
        out[name] = jnp.asarray(drawn.astype(out[name].dtype))
    for name, factor in factors.items():
        out[name] = (out[name] * factor).astype(out[name].dtype)
    return out
```

```python
from contextlib import ExitStack

import concourse.bass as bass
from concourse import mybir

F32 = mybir.dt.float32
BF16 = mybir.dt.bfloat16
I32 = mybir.dt.int32
ALU = mybir.AluOpType
ACT = mybir.ActivationFunctionType
AX = mybir.AxisListType.X

P = 128
D = 128
N, E = 6250, 100000
BLOCKS = -(-N // P)
NB = 52
GROUPS = NB // 4
TAIL = N - (BLOCKS - 1) * P
TILES = -(-E // P)
LASTBASE = E - P
REST = E - (TILES - 1) * P
CH = -(-TILES // P)
PAIRS = TILES + BLOCKS - 1
HP = PAIRS // 2
R = 10
H = 5
ITERS = PAIRS // R
ROW = 132
NOKEY = 8191
NOWHERE = 200000
BIG = 1e30
POSB = 8
STEPS = -(-TILES // POSB)
SC = -(-E // P)
SREST = E - (P - 1) * SC
SG = -(-SC // R) * R
EPS = 1e-5


class Tally:

    def __init__(self, eng, sem):
        self.eng, self.sem, self.n, self.lead = eng, sem, 0, 0

    def __call__(self, ins):
        ins.then_inc(self.sem, 1)
        self.n += 1

    def wait(self):
        self.eng.wait_ge(self.sem, self.lead + self.n)


def repeat(eng, times, body, *tallies, peel=1):
    for k in range(peel):
        before = [t.n for t in tallies]
        body(k)
    start = [t.n for t in tallies]
    per = [n - b for n, b in zip(start, before)]
    with eng.Fori(peel, times) as i:
        for t, k in zip(tallies, per):
            t.lead = (i - peel) * k
        body(i)
    for t, n, k in zip(tallies, start, per):
        t.lead, t.n = 0, n + k * (times - peel)


def first(i):
    return isinstance(i, int) and i == 0


def landed(k, i):
    return 16 * (ITERS * k + i)


def gnn_kernel(nc, x, src, dst, edge_attr_128, L0_gnn_W1, L0_gnn_b1, L0_gnn_W2, L0_gnn_b2, L0_gnn_gamma,
               L0_gnn_beta, L1_gnn_W1, L1_gnn_b1, L1_gnn_W2, L1_gnn_b2, L1_gnn_U1, L1_gnn_ub1, L1_gnn_U2,
               L1_gnn_ub2, L1_gnn_gamma, L1_gnn_beta, L2_gnn_W, L2_gnn_attn, L3_gnn_weight, L3_gnn_att, out):
    with ExitStack() as ctx:
        def sb(name, shape, dt=F32):
            return ctx.enter_context(nc.sbuf_tensor(name, shape, dt))

        def sem(name):
            return ctx.enter_context(nc.semaphore(name))

        def ring(name, n):
            return [sem(f"{name}{k}") for k in range(n)]

        table0 = nc.dram_tensor("table0", [NB * P, D], F32, kind="Internal").ap()
        table1 = nc.dram_tensor("table1", [NB * P, D], F32, kind="Internal").ap()
        table2 = nc.dram_tensor("table2", [NB * P, 130], F32, kind="Internal").ap()
        table3 = nc.dram_tensor("table3", [NB * P, 4], F32, kind="Internal").ap()
        messages = nc.dram_tensor("messages", [E, ROW], F32, kind="Internal").ap()
        score2 = nc.dram_tensor("score2", [NB * P], F32, kind="Internal").ap()
        seg_max = nc.dram_tensor("seg_max", [P * SC, 4], F32, kind="Internal").ap()
        seg_sum = nc.dram_tensor("seg_sum", [P * SC, 4], F32, kind="Internal").ap()
        seg_fill = nc.dram_tensor("seg_fill", [P * SC, 8], F32, kind="Internal").ap()

        X = sb("X", [P, NB, D])
        Hn = sb("Hn", [P, NB, D])
        ACC = sb("ACC", [P, NB, 130])
        BT = sb("BT", [P, NB, D])
        CT = sb("CT", [P, NB, D])
        accw = ACC[:, :, :].rearrange("p b f -> p (b f)")
        btw = BT[:, :, :].rearrange("p b f -> p (b f)")
        ctw = CT[:, :, :].rearrange("p b f -> p (b f)")
        hnw = Hn[:, :, :].rearrange("p b f -> p (b f)")

        count_i = sb("count_i", [P, 1], I32)
        iota = sb("iota", [P, PAIRS])
        lane = sb("lane", [P, 1])
        lanes = sb("lanes", [P, CH])
        ident = sb("ident", [P, P])
        ones = sb("ones", [P, P])
        below = sb("below", [P, P], BF16)
        onesb = sb("onesb", [P, P], BF16)

        dst_rel = sb("dst_rel", [P, PAIRS])
        pay = sb("pay", [P, PAIRS, 2])
        src_idx = sb("src_idx", [P, PAIRS], I32)
        pos_idx = sb("pos_idx", [P, PAIRS], I32)
        regs = sb("regs", [P, PAIRS], I32)
        s_shift = sb("s_shift", [P, PAIRS])
        payS = sb("payS", [P, PAIRS, 2])
        dst_idx = pos_idx
        src_relS = dst_rel
        maskS = src_idx[:, :].bitcast(F32)

        rows = sb("rows", [P, R, ROW])
        mrow = sb("mrow", [P, R, ROW])
        edge = sb("edge", [P, R, D])
        onehot = sb("onehot", [P, R, P])
        turned = sb("turned", [P, H, 2, P])
        lnp = sb("lnp", [P, H, D])
        idxs = sb("idxs", [P, R], I32)
        pidx = sb("pidx", [P, R], I32)
        WA = sb("WA", [P, 14, D])
        small = sb("small", [P, 16, NB])
        st = mrow[:, :, :].rearrange("p r f -> p (r f)")[:, 0:NB * 6].rearrange("p (b s) -> p b s", s=6)
        tw = turned[:, :, :, :].rearrange("p a b f -> p (a b f)")
        hT, rT = tw[:, 0:512], tw[:, 512:1024]

        group = edge[:, 0:4, :].rearrange("p a f -> p (a f)")
        zgroup = edge[:, 4:8, :].rearrange("p a f -> p (a f)")

        PS = [ctx.enter_context(nc.psum_tensor(f"PS{k}", [P, 512], F32)) for k in range(8)]

        def seg_ps(s):
            return PS[s][:, 0:129]

        def turn_ps(s):
            return PS[s][:, 0:256]

        def pre_ps(s):
            return PS[2 + s][:, 0:D]

        srcL = accw[:, 0:896].bitcast(I32).rearrange("p (c e) -> p c e", e=P)
        dstL = accw[:, 896:1792].bitcast(I32).rearrange("p (c e) -> p c e", e=P)
        srcF = accw[:, 1792:2688].rearrange("p (c e) -> p c e", e=P)
        dstF = accw[:, 2688:3584].rearrange("p (c e) -> p c e", e=P)
        hiT = accw[:, 3584:4480]
        posT = accw[:, 4480:5376]
        posF = accw[:, 5376:6272].rearrange("p (c e) -> p c e", e=P)
        cnt_hi = accw[:, 6272:6321]
        cum_hi = accw[:, 6330:6379]
        base_hi = accw[:, 6380:6429]
        last_b = accw[:, 6430:6437]
        rise = accw[:, 6440:6447]
        xlast = accw[:, 6450:6457]
        junk_hi = accw[:, 6460:6509]
        last_i = accw[:, 6510:6517].bitcast(I32)
        hiF = posF
        sel = btw[:, 0:CH * PAIRS].rearrange("p (c n) -> p c n", n=PAIRS)
        gbf = ctw[:, 0:CH * PAIRS // 2].bitcast(BF16).rearrange("p (c n) -> p c n", n=PAIRS)
        kpair = ctw[:, 2910:2910 + PAIRS]
        bpair = ctw[:, 3750:3750 + PAIRS]
        tmpp = ctw[:, 4590:4590 + PAIRS]
        oh8 = [ctw[:, 5430 + 200 * q:5430 + 200 * q + 196].bitcast(BF16).rearrange("p (t h) -> p t h", h=BLOCKS)
               for q in range(2)]
        t8 = ctw[:, 5900:5900 + 392].rearrange("p (t h) -> p t h", h=BLOCKS)

        W0_1, W0_2 = WA[:, 0, 0:64], WA[0:65, 1, :]
        b0_1 = WA[0:64, 2, 0:1]
        g0, be0 = WA[:, 3, :], WA[:, 4, :]
        W1abu, W1c = WA[:, 0:3, :], WA[:, 3, :]
        b1bc, ub1bc, W1_2, U1b, U2w, ub2bc, g1, be1, W2U, b2Ubc = (WA[:, k, :] for k in range(4, 14))
        b1_2 = small[:, 15, 0:1]

        cnt_dst = small[:, 7, :]
        misc = small[:, 10, :]
        sv, lm, wgt, sc_mx = misc[:, 0:10], misc[:, 10:20], misc[:, 20:30], misc[:, 30:31]
        negm, m_all, fade, m_run, sc_top = misc[:, 31:33], misc[:, 33:35], misc[:, 35:37], misc[:, 37:39], misc[0:1, 39:40]
        m_block = small[:, 11, :]

        pay_flat = pay[:, :, :].rearrange("p n a -> p (n a)")
        payS_flat = payS[:, :, :].rearrange("p n a -> p (n a)")
        scan_idx = pay_flat[:, 0:SG].bitcast(I32)
        scan_dst = pay_flat[:, 800:800 + SC].bitcast(I32)
        scan_prev = payS_flat[:, 0:SC].bitcast(I32)
        contneg = payS_flat[:, 800:800 + SC]
        cont = s_shift[:, 0:SC]
        g4 = edge[:, :, :].rearrange("p r f -> p (r f)")[:, 0:4 * R].rearrange("p (r f) -> p r f", f=4)
        mrow_flat = mrow[:, :, :].rearrange("p r f -> p (r f)")
        SN = mrow_flat[:, 0:416].rearrange("p (b f) -> p b f", f=8)
        mx_node = mrow_flat[:, 416:624].rearrange("p (b f) -> p b f", f=4)
        sum_node = mrow_flat[:, 624:832].rearrange("p (b f) -> p b f", f=4)
        fill_node = mrow_flat[:, 832:1248].rearrange("p (b f) -> p b f", f=8)
        SI = ctw[:, 0:4 * SG].rearrange("p (i f) -> p i f", f=4)
        MX = ctw[:, 3200:3200 + 4 * SC].rearrange("p (i f) -> p i f", f=4)
        fill = accw[:, 0:8 * SC].rearrange("p (i f) -> p i f", f=8)
        FO = hnw[:, 0:8 * SC].rearrange("p (i f) -> p i f", f=8)
        upto = onehot[:, 0, :]
        start_idx, end_idx = small[:, 12, :].bitcast(I32), small[:, 13, :].bitcast(I32)
        last_v, last_c = small[:, 0, 0:8], small[:, 0, 8:16]
        all_cont, all_neg = small[:, 0, 16:17], small[:, 0, 17:18]
        carry_row = onehot[:, 1:4, :].rearrange("p a f -> p (a f)")

        s_const = sem("s_const")
        s_edges = sem("s_edges")
        s_x = sem("s_x")
        s_pad = sem("s_pad")
        s_w = ring("s_w", 4)
        s_wdone = ring("s_wdone", 3)
        s_dve = sem("s_dve")
        s_act = sem("s_act")
        s_pe0 = sem("s_pe0")
        s_ask0 = sem("s_ask0")
        s_idle = sem("s_idle")
        s_idleA = sem("s_idleA")
        s_tab = ring("s_tab", 4)
        s_h = ring("s_h", 4)
        s_st = sem("s_st")
        s_sd = sem("s_sd")
        s_nm = sem("s_nm")
        s_out = sem("s_out")

        s_ones0 = sem("s_ones0")
        s_tables = sem("s_tables")
        s_oh8 = sem("s_oh8")
        s_hist = sem("s_hist")
        s_ahead = sem("s_ahead")
        s_placed = sem("s_placed")
        s_bns = sem("s_bns")
        s_idx = sem("s_idx")
        s_row = ring("s_row", R)
        s_t, s_tc, s_p = sem("s_t"), sem("s_tc"), sem("s_p")
        s_m0, s_r0, s_e0, s_e0c = (sem(n) for n in ("s_m0", "s_r0", "s_e0", "s_e0c"))
        s_oh0, s_seg0, s_acc0 = sem("s_oh0"), sem("s_seg0"), sem("s_acc0")
        s_diff, s_diffa = sem("s_diff"), sem("s_diffa")
        s_xnew = ring("s_xnew", 4)
        s_put, s_put1 = sem("s_put"), sem("s_put1")
        s_fold, s_folded = sem("s_fold"), sem("s_folded")
        s_p1a, s_p1c = sem("s_p1a"), sem("s_p1c")
        s_edge = ring("s_edge", R)
        s_oh1 = sem("s_oh1")
        s_turn, s_turnedc = sem("s_turn"), sem("s_turnedc")
        s_pre = sem("s_pre")
        s_sum1 = sem("s_sum1")
        s_ln = sem("s_ln")
        s_msg = sem("s_msg")
        s_sent = ring("s_sent", R)
        s_oh1s, s_seg1, s_acc1, s_took = (sem(n) for n in ("s_oh1s", "s_seg1", "s_acc1", "s_took"))
        s_node1 = sem("s_node1")
        s_u1, s_u1c, s_u2, s_zin, s_zl, s_z1, s_u3, s_u3c, s_u4, s_u4c = (
            sem(n) for n in ("s_u1", "s_u1c", "s_u2", "s_zin", "s_zl", "s_z1", "s_u3", "s_u3c", "s_u4", "s_u4c"))
        s_bn, s_bnsum, s_bnsd = sem("s_bn"), sem("s_bnsum"), sem("s_bnsd")
        s_store2 = sem("s_store2")
        s_sc2 = sem("s_sc2")
        s_fold2, s_folded2 = sem("s_fold2"), sem("s_folded2")
        s_p2c = sem("s_p2c")
        s_mx, s_mxt, s_mnew, s_mbc, s_negm = (sem(n) for n in ("s_mx", "s_mxt", "s_mnew", "s_mbc", "s_negm"))
        s_wgt, s_oh2, s_seg2, s_acc2 = (sem(n) for n in ("s_wgt", "s_oh2", "s_seg2", "s_acc2"))
        s_fin2, s_fin2a = sem("s_fin2"), sem("s_fin2a")
        s_scanfree, s_scan, s_prev = (sem(n) for n in ("s_scanfree", "s_scan", "s_prev"))
        s_folded3, s_p3c = sem("s_folded3"), sem("s_p3c")
        s_cum, s_cump, s_got3, s_carry, s_carryp = (sem(n) for n in ("s_cum", "s_cump", "s_got3", "s_carry", "s_carryp"))
        s_scanned, s_segmax, s_mxnode, s_zero, s_fill, s_fillz, s_filled, s_fillback = (
            sem(n) for n in ("s_scanned", "s_segmax", "s_mxnode", "s_zero", "s_fill", "s_fillz", "s_filled",
                             "s_fillback"))
        s_alpha, s_alphae, s_segsum, s_sumnode = (sem(n) for n in ("s_alpha", "s_alphae", "s_segsum", "s_sumnode"))

        block = ctx.enter_context(nc.Block())

        def spread(col, n, w=D):
            return col.unsqueeze(2).to_broadcast([P, n, w])

        def over(row, n):
            return row.unsqueeze(1).to_broadcast([P, n, D])

        @block.sync
        def _(sp):
            sp.wait_ge(s_pad, 3)
            for a, s in ((srcL, src), (dstL, dst)):
                sp.dma_start(a[:, 0:CH - 1, :], s[0:(CH - 1) * P * P].rearrange("(c t e) -> t c e", t=P, e=P)
                             ).then_inc(s_edges, 16)
                sp.dma_start(a[0:TILES - 1 - (CH - 1) * P, CH - 1, :],
                             s[(CH - 1) * P * P:(TILES - 1) * P].rearrange("(t e) -> t e", e=P)).then_inc(s_edges, 16)
                sp.dma_start(a[TILES - 1 - (CH - 1) * P:TILES - (CH - 1) * P, CH - 1, P - REST:P],
                             s[(TILES - 1) * P:E].rearrange("(t e) -> t e", t=1)).then_inc(s_edges, 16)
            sp.dma_start(X[:, 0:BLOCKS - 1, :], x[0:(BLOCKS - 1) * P, :].rearrange("(b j) f -> j b f", j=P)
                         ).then_inc(s_x, 16)
            sp.dma_start(X[0:TAIL, BLOCKS - 1, :], x[(BLOCKS - 1) * P:N, :]).then_inc(s_x, 16)

            sp.wait_ge(s_h[0], NB)
            sp.dma_start(table0.rearrange("(b j) f -> j b f", j=P), Hn[:, :, :]).then_inc(s_tab[0], 16)
            sp.wait_ge(s_p1a, GROUPS)
            sp.dma_start(table1.rearrange("(b j) f -> j b f", j=P), Hn[:, :, :]).then_inc(s_tab[1], 16)
            sp.wait_ge(s_p1c, GROUPS)

            def edge_rows(i):
                for j in range(R):
                    at = sp.value_load(regs[32:33, bass.ds(R * i + j, 1)], min_val=0, max_val=LASTBASE)
                    if not first(i):
                        sp.wait_ge(s_turn, R * i - R + j + 1)
                    sp.dma_start(edge[:, j, :], edge_attr_128[bass.ds(at, P), :]).then_inc(s_edge[j], 16)
            repeat(sp, ITERS, edge_rows)

            for j in range(R):
                sp.wait_ge(s_sent[j], 16 * ITERS)
            sp.wait_ge(s_tables, 3)

            def message_rows(i):
                for j in range(R):
                    at = sp.value_load(regs[96:97, bass.ds(R * i + j, 1)], min_val=0, max_val=LASTBASE)
                    if not first(i):
                        sp.wait_ge(s_seg1, R * i - R + j + 1)
                        sp.wait_ge(s_took, 2 * i - 2 + j // H + 1)
                    sp.dma_start(rows[:, j, :], messages[bass.ds(at, P), :]).then_inc(s_edge[j], 16)
            repeat(sp, ITERS, message_rows)
            sp.wait_ge(s_store2, 1)
            sp.dma_start(table2.rearrange("(b j) f -> j b f", j=P), ACC[:, :, :]).then_inc(s_tab[2], 16)
            sp.dma_start(score2.rearrange("(b j) -> j b", j=P), small[:, 8, :],
                         allow_slow_non_contiguous=True).then_inc(s_sc2, 16)
            sp.wait_ge(s_sc2, 16)
            sp.dma_start(btw, score2.partition_broadcast(P)).then_inc(s_sc2, 16)
            sp.wait_ge(s_scanfree, 1)
            for a, s in ((scan_idx, src), (scan_dst, dst)):
                sp.dma_start(a[0:P - 1, 0:SC], s[0:(P - 1) * SC].rearrange("(p i) -> p i", i=SC)).then_inc(s_scan, 16)
                sp.dma_start(a[P - 1:P, 0:SREST], s[(P - 1) * SC:E].rearrange("(p i) -> p i", p=1)).then_inc(s_scan, 16)
            sp.dma_start(scan_prev[0:1, 1:SC], dst[0:SC - 1].rearrange("(p i) -> p i", p=1)).then_inc(s_prev, 16)
            sp.dma_start(scan_prev[1:P - 1, :], dst[SC - 1:(P - 1) * SC - 1].rearrange("(p i) -> p i", i=SC)
                         ).then_inc(s_prev, 16)
            sp.dma_start(scan_prev[P - 1:P, 0:SREST], dst[(P - 1) * SC - 1:E - 1].rearrange("(p i) -> p i", p=1)
                         ).then_inc(s_prev, 16)
            sp.wait_ge(s_p3c, GROUPS)
            sp.dma_start(table3.rearrange("(b j) f -> j b f", j=P), SN[:, :, 0:4]).then_inc(s_tab[3], 16)
            sp.wait_ge(s_zero, 1)
            sp.dma_start(seg_fill.rearrange("(p i) f -> p i f", i=SC), fill).then_inc(s_fillz, 16)
            sp.wait_ge(s_scanned, 1)
            sp.dma_start(seg_max.rearrange("(p i) f -> p i f", i=SC), MX[:, :, :]).then_inc(s_segmax, 16)
            sp.wait_ge(s_filled, 16 * BLOCKS)
            sp.dma_start(fill, seg_fill.rearrange("(p i) f -> p i f", i=SC)).then_inc(s_fillback, 16)
            sp.wait_ge(s_scanned, 2)
            sp.dma_start(seg_sum.rearrange("(p i) f -> p i f", i=SC), MX[:, :, :]).then_inc(s_segsum, 16)
            sp.wait_ge(s_xnew[3], 1)
            sp.dma_start(out[0:(BLOCKS - 1) * P, :].rearrange("(b j) f -> j b f", j=P), X[:, 0:BLOCKS - 1, :]
                         ).then_inc(s_out, 16)
            sp.dma_start(out[(BLOCKS - 1) * P:N, :], X[0:TAIL, BLOCKS - 1, :]).then_inc(s_out, 16)
            sp.wait_ge(s_out, 32)

        @block.gpsimd
        def _(pool):
            idx_steps = Tally(pool, s_idx)
            nc.gpsimd.iota(tmpp.bitcast(I32), pattern=[[1, PAIRS]], base=0, channel_multiplier=0).then_inc(s_const, 1)
            nc.gpsimd.iota(count_i[:, :], pattern=[[0, 1]], base=0, channel_multiplier=1).then_inc(s_const, 1)
            nc.gpsimd.memset(X[:, :, :], 0.0).then_inc(s_pad, 1)

            def stage(ring_idx, table, at):
                pool.sem_inc(s_idle, 1)
                idx_steps(nc.gpsimd.tensor_copy(ring_idx, table[:, bass.ds(at, H)]))
                idx_steps.wait()
                pool.sem_inc(s_idle, 1)

            def gather(table, i, h, idx_table, k, used, width, ring_to=rows, by_half=False):
                if not first(i):
                    for j in range(h * H, h * H + H):
                        pool.wait_ge(s_row[j], landed(k, i))
                    pool.wait_ge(used, 2 * i - 1 + h if by_half else R * i - R + h * H + H)
                stage(idxs[:, h * H:h * H + H], idx_table, R * i + h * H)
                for j in range(h * H, h * H + H):
                    nc.gpsimd.indirect_dma_start(ring_to[:, j, 0:width], None, table[:, :],
                                                 bass.IndirectOffsetOnAxis(idxs[:, j:j + 1], 0)
                                                 ).then_inc(s_row[j], 16)

            pool.wait_ge(s_tables, 1)
            pool.wait_ge(s_tab[0], 16)

            def sum0(i):
                for h in range(2):
                    gather(table0, i, h, src_idx, 0, s_seg0, D)
            repeat(pool, ITERS, sum0, idx_steps)

            pool.wait_ge(s_tables, 2)
            pool.wait_ge(s_tab[1], 16)

            def scatter(i, h):
                pool.wait_ge(s_msg, 2 * i + h + 1)
                if not first(i):
                    for j in range(h * H, h * H + H):
                        pool.wait_ge(s_sent[j], 16 * i)
                stage(pidx[:, h * H:h * H + H], pos_idx, R * i + h * H)
                for j in range(h * H, h * H + H):
                    nc.gpsimd.indirect_dma_start(messages[:, :], bass.IndirectOffsetOnAxis(pidx[:, j:j + 1], 0),
                                                 mrow[:, j, :], None, bounds_check=E - 1, oob_is_err=False
                                                 ).then_inc(s_sent[j], 16)

            def edges(i):
                gather(table1, i, 0, src_idx, 1, s_sum1, D)
                if not first(i):
                    scatter(i - 1, 1)
                gather(table1, i, 1, src_idx, 1, s_sum1, D)
                scatter(i, 0)
            repeat(pool, ITERS, edges, idx_steps, peel=2)
            scatter(ITERS - 1, 1)

            pool.wait_ge(s_tables, 4)
            pool.wait_ge(s_tab[2], 16)

            def attend(i):
                for h in range(2):
                    gather(table2, i, h, dst_idx, 2, s_seg2, 130)
            repeat(pool, ITERS, attend, idx_steps)

            pool.wait_ge(s_scan, 64)
            pool.wait_ge(s_tab[3], 16)

            def scores(i):
                for h in range(2):
                    gather(table3, i, h, scan_idx, 3, s_got3, 4, g4, by_half=True)
            repeat(pool, SG // R, scores, idx_steps)

            pool.wait_ge(s_segmax, 16)
            for b in range(BLOCKS):
                nc.gpsimd.indirect_dma_start(mx_node[:, b, :], None, seg_max[:, :],
                                             bass.IndirectOffsetOnAxis(end_idx[:, b:b + 1], 0)
                                             ).then_inc(s_mxnode, 16)
            pool.wait_ge(s_fill, 1)
            pool.wait_ge(s_fillz, 16)
            for b in range(BLOCKS):
                nc.gpsimd.indirect_dma_start(seg_fill[:, :], bass.IndirectOffsetOnAxis(start_idx[:, b:b + 1], 0),
                                             fill_node[:, b, :], None, bounds_check=E - 1, oob_is_err=False
                                             ).then_inc(s_filled, 16)
            pool.wait_ge(s_segsum, 16)
            for b in range(BLOCKS):
                nc.gpsimd.indirect_dma_start(sum_node[:, b, :], None, seg_sum[:, :],
                                             bass.IndirectOffsetOnAxis(end_idx[:, b:b + 1], 0)
                                             ).then_inc(s_sumnode, 16)

        @block.tensor
        def _(pe):
            def turn7(a, order):
                pe.wait_ge(s_ask0, order)
                for c in range(CH):
                    last = nc.tensor.transpose(PS[c // 4][:, c % 4 * P:c % 4 * P + P], a[:, c, :], ident[:, :])
                last.then_inc(s_pe0, 1)

            def count_below(order):
                pe.wait_ge(s_ask0, order)
                for half in range(2):
                    for c in range(CH):
                        last = nc.tensor.matmul(PS[2 + half][:, 0:HP], onesb[:, :], gbf[:, c, half * HP:half * HP + HP],
                                                start=(c == 0), stop=(c == CH - 1))
                last.then_inc(s_pe0, 1)

            def pick(a, order):
                pe.wait_ge(s_ask0, order)
                for half in range(2):
                    for c in range(CH):
                        last = nc.tensor.matmul(PS[2 + half][:, 0:HP], a[:, c, :], sel[:, c, half * HP:half * HP + HP],
                                                start=(c == 0), stop=(c == CH - 1))
                last.then_inc(s_pe0, 1)

            turn7(hiF, 1)
            count_below(2)
            pick(dstF, 3)
            pick(srcF, 4)

            def histogram(i):
                for q in range(2):
                    pe.wait_ge(s_oh8, 2 * i + q + 1)
                    nc.tensor.matmul(PS[4][:, 0:POSB * BLOCKS], onesb[:, :], oh8[q], start=first(i) and q == 0,
                                     stop=False, skip_group_check=True).then_inc(s_hist, 1)
            repeat(pe, STEPS // 2, histogram)

            def place(i):
                for q in range(2):
                    pe.wait_ge(s_oh8, STEPS + 2 * i + q + 1)
                    if not (first(i) and q == 0):
                        pe.wait_ge(s_placed, 2 * i + q)
                    ahead = PS[4][:, 0:POSB * BLOCKS].rearrange("p (t h) -> p t h", h=BLOCKS)
                    nc.tensor.matmul(ahead, below[:, :], oh8[q], start=True, stop=False, skip_group_check=True)
                    for t in range(POSB - 1):
                        nc.tensor.matmul(ahead[:, t + 1:POSB, :], onesb[:, :],
                                         oh8[q][:, t:t + 1, :].to_broadcast([P, POSB - 1 - t, BLOCKS]),
                                         start=False, stop=(t == POSB - 2), skip_group_check=True)
                    for t in range(POSB):
                        last = nc.tensor.matmul(PS[5][:, 0:BLOCKS], onesb[:, :], oh8[q][:, t, :], start=(t == 0),
                                                stop=(t == POSB - 1))
                    last.then_inc(s_ahead, 1)
            repeat(pe, STEPS // 2, place)
            turn7(posT.rearrange("p (c e) -> p c e", e=P), 5)
            pick(posF, 6)
            count_below(7)

            def turn_group(a, to):
                for q in range(4):
                    last = nc.tensor.transpose(to[:, q * P:q * P + P], a[:, q * P:q * P + P], ident[:, :])
                return last

            pe.wait_ge(s_w[0], 16 * 6)

            def mlp0(i):
                pe.wait_ge(s_put, i + 1)
                turn_group(group, PS[7]).then_inc(s_t, 1)
                pe.wait_ge(s_tc, i + 1)
                nc.tensor.matmul(PS[6][0:64, :], W0_1, hT, start=True, stop=True).then_inc(s_m0, 1)
                pe.wait_ge(s_r0, i + 1)
                if not first(i):
                    pe.wait_ge(s_e0c, i)
                for q in range(4):
                    last = nc.tensor.matmul(PS[5][:, q * P:q * P + P], rT[0:65, q * P:q * P + P], W0_2,
                                            start=True, stop=True)
                last.then_inc(s_e0, 1)
            repeat(pe, GROUPS, mlp0)

            def segment(i, j, oh_ready, row_ready, row_count, used, done, src_rows):
                pe.wait_ge(oh_ready, R * i + j + 1)
                pe.wait_ge(row_ready[j], row_count)
                if not (first(i) and j < H):
                    pe.wait_ge(used, R * i + j + 1 - H)
                nc.tensor.matmul(seg_ps(j % H), onehot[:, j, :], src_rows[:, j, 0:129], start=True, stop=True
                                 ).then_inc(done, 1)

            def sum0(i):
                for j in range(R):
                    segment(i, j, s_oh0, s_row, landed(0, i + 1), s_acc0, s_seg0, rows)
            repeat(pe, ITERS, sum0)

            pe.wait_ge(s_w[1], 16 * 13)
            nc.tensor.transpose(PS[7][:, 0:P], W1_2, ident[:, :]).then_inc(s_fold, 1)
            pe.wait_ge(s_folded, 1)
            nc.tensor.matmul(PS[6][:, 0:D], tw[:, 0:D], U1b, start=True, stop=True)
            nc.tensor.matmul(PS[6][:, D:2 * D], b1_2.to_broadcast([P, P]), U1b, start=True, stop=True
                             ).then_inc(s_fold, 1)
            pe.wait_ge(s_folded, 2)

            def project(k, i, weights, width, used):
                pe.wait_ge(s_put, GROUPS * k + i + 1)
                turn_group(group, PS[7]).then_inc(s_t, 1)
                pe.wait_ge(s_tc, GROUPS * k + i + 1)
                if not first(i):
                    pe.wait_ge(used, i)
                for q in range(4):
                    last = nc.tensor.matmul(PS[2 + q][:, 0:width], hT[:, q * P:q * P + P], weights,
                                            start=True, stop=True)
                last.then_inc(s_p, 1)
            repeat(pe, GROUPS, lambda i: project(1, i, W1abu.rearrange("p a f -> p (a f)"), 3 * D, s_p1c))

            def edges(i):
                blocks = {}

                def combine(j):
                    s = j % H
                    pe.wait_ge(s_turnedc, R * i + j + 1)
                    if not (first(i) and j < H):
                        pe.wait_ge(s_sum1, R * i + j + 1 - H)
                    nc.tensor.matmul(pre_ps(s), turned[:, s, 1, :], W1c, start=True, stop=False)
                    nc.tensor.matmul(pre_ps(s), turned[:, s, 0, :], BT[:, bass.ds(blocks[j], 1), :].rearrange("p a f -> p (a f)"),
                                     start=False, stop=True).then_inc(s_pre, 1)

                for h in range(2):
                    for j in range(h * H, h * H + H):
                        blocks[j] = pe.value_load(regs[0:1, bass.ds(R * i + j, 1)], min_val=0, max_val=BLOCKS - 1)
                        pe.wait_ge(s_oh1, R * i + j + 1)
                        pe.wait_ge(s_edge[j], 16 * i + 16)
                        if not (first(i) and j < 2):
                            pe.wait_ge(s_turnedc, R * i + j - 1)
                        nc.tensor.transpose(turn_ps(j % 2)[:, 0:P], onehot[:, j, :], ident[:, :])
                        nc.tensor.transpose(turn_ps(j % 2)[:, P:2 * P], edge[:, j, :], ident[:, :]
                                            ).then_inc(s_turn, 1)
                    for j in range(h * H, h * H + H):
                        combine(j)
            repeat(pe, ITERS, edges)

            def sum1(i):
                for j in range(R):
                    segment(i, j, s_oh1s, s_edge, landed(1, i + 1), s_acc1, s_seg1, rows)
            repeat(pe, ITERS, sum1)

            pe.wait_ge(s_node1, 1)

            def update(i):
                pe.wait_ge(s_put1, i + 1)
                turn_group(group, PS[7]).then_inc(s_u1, 1)
                pe.wait_ge(s_u1c, i + 1)
                for q in range(4):
                    last = nc.tensor.matmul(PS[6][:, q * P:q * P + P], hT[:, q * P:q * P + P], W2U, start=True, stop=True)
                last.then_inc(s_u2, 1)
                pe.wait_ge(s_z1, i + 1)
                turn_group(zgroup, PS[5]).then_inc(s_u3, 1)
                pe.wait_ge(s_u3c, i + 1)
                for q in range(4):
                    last = nc.tensor.matmul(PS[4][:, q * P:q * P + P], rT[:, q * P:q * P + P], U2w, start=True, stop=True)
                last.then_inc(s_u4, 1)
                pe.wait_ge(s_u4c, i + 1)
            repeat(pe, GROUPS, update)
            for k in range(2):
                pe.wait_ge(s_bn, k + 1)
                nc.tensor.matmul(PS[0][:, 0:D], ones[:, :], lnp[:, 0, :], start=True, stop=True).then_inc(s_bnsum, 1)

            pe.wait_ge(s_w[2], 48)
            nc.tensor.transpose(PS[7][:, 0:P], WA[:, 0, :], ident[:, :]).then_inc(s_fold2, 1)
            pe.wait_ge(s_folded2, 1)
            nc.tensor.matmul(PS[6][:, 0:2], tw[:, 0:D], WA[:, 3, 0:2], start=True, stop=True).then_inc(s_fold2, 1)
            pe.wait_ge(s_folded2, 2)
            waf = WA[:, :, :].rearrange("p a f -> p (a f)")
            repeat(pe, GROUPS, lambda i: project(2, i, waf[:, 0:130], 130, s_p2c))

            def attend(i):
                for h in range(2):
                    pe.wait_ge(s_mx, 2 * i + h + 1)
                    nc.tensor.transpose(PS[6][0:1, 0:P], sc_mx, ident[:, :]).then_inc(s_mxt, 1)
                    pe.wait_ge(s_mnew, 2 * i + h + 1)
                    nc.tensor.matmul(PS[6][:, 256:257], ones[0:1, :], m_run[0:1, h:h + 1], start=True, stop=True
                                     ).then_inc(s_mbc, 1)
                    for j in range(h * H, h * H + H):
                        segment(i, j, s_oh2, s_row, landed(2, i + 1), s_acc2, s_seg2, rows)
            repeat(pe, ITERS, attend)

            pe.wait_ge(s_folded3, 1)
            repeat(pe, GROUPS, lambda i: project(3, i, waf[:, 0:136], 136, s_p3c))
            pe.wait_ge(s_cum, 1)
            nc.tensor.matmul(PS[6][:, 0:BLOCKS], upto, cnt_dst[:, 0:BLOCKS], start=True, stop=True)
            nc.tensor.matmul(PS[6][:, 64:64 + BLOCKS], ones[:, :], cnt_dst[:, 0:BLOCKS], start=True, stop=True
                             ).then_inc(s_cump, 1)
            for k, w in enumerate((4, 8, 4)):
                pe.wait_ge(s_carry, 2 * k + 1)
                nc.tensor.transpose(PS[5][0:w, 0:P], last_v[:, 0:w], ident[:, :])
                nc.tensor.transpose(PS[5][0:w, P:2 * P], last_c[:, 0:w], ident[:, :]).then_inc(s_carryp, 1)
                pe.wait_ge(s_carry, 2 * k + 2)
                nc.tensor.transpose(PS[5][:, 256:256 + w], carry_row[0:w, 0:P], ident[0:w, 0:w]).then_inc(s_carryp, 1)

        @block.scalar
        def _(act):
            done = Tally(act, s_act)

            def step(ins):
                done(ins)
                done.wait()

            def norm_h(k, after):
                act.wait_ge(s_st, after)
                nc.scalar.activation(small[:, 2, :], small[:, 1, :], ACT.Sqrt).then_inc(s_sd, 1)
                act.wait_ge(s_nm, k + 1)
                if k:
                    act.wait_ge(s_tab[k - 1], 16)
                act.sem_inc(s_idleA, 1)
                with act.Fori(0, NB) as b:
                    nc.scalar.activation(Hn[:, bass.ds(b, 1), :].rearrange("p a f -> p (a f)"),
                                         X[:, bass.ds(b, 1), :].rearrange("p a f -> p (a f)"), ACT.Relu,
                                         bias=small[:, 4, bass.ds(b, 1)], scale=small[:, 3, bass.ds(b, 1)]
                                         ).then_inc(s_h[k], 1)

            def load(dest, source, k):
                act.dma_start(dest, source).then_inc(s_w[k], 16)

            def row(v):
                return v.partition_broadcast(P)

            load(W0_1, L0_gnn_W1, 0)
            load(WA[0:64, 1, :], L0_gnn_W2, 0)
            load(WA[64:65, 1, :], L0_gnn_b2.rearrange("(a f) -> a f", a=1), 0)
            load(b0_1, L0_gnn_b1.rearrange("(f a) -> f a", a=1), 0)
            load(g0, row(L0_gnn_gamma), 0)
            load(be0, row(L0_gnn_beta), 0)

            norm_h(0, 1)

            def mlp0(i):
                act.wait_ge(s_t, i + 1)
                nc.scalar.activation(hT, PS[7][:, :], ACT.Copy).then_inc(s_tc, 1)
                act.wait_ge(s_m0, i + 1)
                if not first(i):
                    act.wait_ge(s_e0, i)
                nc.scalar.activation(rT[0:64, :], PS[6][0:64, :], ACT.Relu, bias=b0_1).then_inc(s_r0, 1)
            act.wait_ge(s_w[0], 96)
            act.wait_ge(s_ones0, 1)
            repeat(act, GROUPS, mlp0)

            act.wait_ge(s_diff, 1)
            nc.scalar.activation(ACC[:, :, 0:D], ACC[:, :, 0:D], ACT.Square).then_inc(s_diffa, 1)
            act.wait_ge(s_diff, 2)
            step(nc.scalar.activation(small[:, 5, :], small[:, 5, :], ACT.Sqrt))
            nc.scalar.activation(small[:, 5, :], small[:, 5, :], ACT.Tanh).then_inc(s_diffa, 1)
            act.wait_ge(s_st, 2)
            nc.scalar.activation(small[:, 2, :], small[:, 1, :], ACT.Sqrt).then_inc(s_sd, 1)

            act.wait_ge(s_wdone[0], 1)
            for k in range(3):
                load(WA[:, k, :], (L1_gnn_W1[0:D, :], L1_gnn_W1[D:2 * D, :], L1_gnn_U1[0:D, :])[k], 1)
            load(W1c, L1_gnn_W1[2 * D:3 * D, :], 1)
            load(b1bc, row(L1_gnn_b1), 1)
            load(ub1bc, row(L1_gnn_ub1), 1)
            load(W1_2, L1_gnn_W2, 1)
            load(U1b, L1_gnn_U1[D:2 * D, :], 1)
            load(U2w, L1_gnn_U2, 1)
            load(ub2bc, row(L1_gnn_ub2), 1)
            load(g1, row(L1_gnn_gamma), 1)
            load(be1, row(L1_gnn_beta), 1)
            load(b1_2, L1_gnn_b2.rearrange("(f a) -> f a", a=1), 1)
            norm_h(1, 3)
            act.wait_ge(s_fold, 1)
            nc.scalar.activation(tw[:, 0:D], PS[7][:, 0:D], ACT.Copy).then_inc(s_folded, 1)
            act.wait_ge(s_fold, 2)
            nc.scalar.activation(WA[:, 12:14, :].rearrange("p a f -> p (a f)"), PS[6][:, 0:2 * D], ACT.Copy
                                 ).then_inc(s_folded, 1)

            def project1(i):
                act.wait_ge(s_t, GROUPS * 1 + i + 1)
                nc.scalar.activation(hT, PS[7][:, :], ACT.Copy).then_inc(s_tc, 1)
                act.wait_ge(s_p, i + 1)
                act.sem_inc(s_idleA, 1)
                for q in range(4):
                    last = nc.scalar.activation(Hn[:, bass.ds(4 * i + q, 1), :].rearrange("p a f -> p (a f)"),
                                                PS[2 + q][:, 0:D], ACT.Copy)
                last.then_inc(s_p1a, 1)
            repeat(act, GROUPS, project1)

            def softplus_tail(v):
                o = lnp[:, 0:v.shape[1], :]
                step(nc.scalar.activation(o, v, ACT.Abs))
                step(nc.scalar.activation(o, o, ACT.Exp, scale=-1.0))
                return nc.scalar.activation(o, o, ACT.Ln, bias=1.0)

            def edges(i):
                for h in range(2):
                    for j in range(h * H, h * H + H):
                        act.wait_ge(s_turn, R * i + j + 1)
                        if not (first(i) and j < H):
                            act.wait_ge(s_pre, R * i + j + 1 - H)
                        nc.scalar.activation(turned[:, j % H, :, :].rearrange("p a f -> p (a f)"), turn_ps(j % 2),
                                             ACT.Copy).then_inc(s_turnedc, 1)
                    act.wait_ge(s_sum1, R * i + h * H + H)
                    if not (first(i) and h == 0):
                        act.wait_ge(s_msg, 2 * i + h)
                    softplus_tail(rows[:, h * H:h * H + H, 0:D]).then_inc(s_ln, 1)
            repeat(act, ITERS, edges, done)

            def update(i):
                act.wait_ge(s_u1, i + 1)
                nc.scalar.activation(hT, PS[7][:, :], ACT.Copy).then_inc(s_u1c, 1)
                act.wait_ge(s_zin, i + 1)
                act.sem_inc(s_idleA, 1)
                softplus_tail(CT[:, bass.ds(4 * i, 4), :]).then_inc(s_zl, 1)
                act.wait_ge(s_u3, i + 1)
                nc.scalar.activation(rT, PS[5][:, :], ACT.Copy).then_inc(s_u3c, 1)
            repeat(act, GROUPS, update, done)
            act.wait_ge(s_bn, 3)
            nc.scalar.activation(lnp[:, 1, :], lnp[:, 1, :], ACT.Sqrt).then_inc(s_bnsd, 1)

            act.wait_ge(s_wdone[1], 1)
            load(WA[:, 0, :], L2_gnn_W, 2)
            for k in range(2):
                load(WA[:, 3, k:k + 1], L2_gnn_attn[0, k * D:(k + 1) * D].rearrange("(f a) -> f a", a=1), 2)
            norm_h(2, 4)
            act.wait_ge(s_fold2, 1)
            nc.scalar.activation(tw[:, 0:D], PS[7][:, 0:D], ACT.Copy).then_inc(s_folded2, 1)
            act.wait_ge(s_fold2, 2)
            nc.scalar.activation(WA[:, 1, 0:2], PS[6][:, 0:2], ACT.Copy).then_inc(s_folded2, 1)

            def project2(i):
                act.wait_ge(s_t, GROUPS * 2 + i + 1)
                nc.scalar.activation(hT, PS[7][:, :], ACT.Copy).then_inc(s_tc, 1)
                act.wait_ge(s_p, GROUPS * 1 + i + 1)
                act.sem_inc(s_idleA, 1)
                for q in range(4):
                    last = nc.scalar.activation(ACC[:, bass.ds(4 * i + q, 1), :].rearrange("p a f -> p (a f)"),
                                                PS[2 + q][:, 0:130], ACT.Copy)
                last.then_inc(s_p2c, 1)
            repeat(act, GROUPS, project2)

            def attend(i):
                for h in range(2):
                    act.wait_ge(s_negm, 2 * i + h + 1)
                    nc.scalar.activation(fade[:, h:h + 1], m_all[:, 1 - h:2 - h], ACT.Exp, bias=negm[:, h:h + 1])
                    nc.scalar.activation(wgt[:, h * H:h * H + H], lm[:, h * H:h * H + H], ACT.Exp,
                                         bias=negm[:, h:h + 1]).then_inc(s_wgt, 1)
            repeat(act, ITERS, attend)
            act.wait_ge(s_fin2, 1)
            nc.scalar.activation(small[:, 6, :], small[:, 6, :], ACT.Exp).then_inc(s_fin2a, 1)
            act.wait_ge(s_fin2, 2)
            nc.scalar.activation(BT[:, :, :], BT[:, :, :], ACT.Exp).then_inc(s_fin2a, 1)

            act.wait_ge(s_wdone[2], 1)
            load(WA[:, 0, :], L3_gnn_weight, 3)
            for k in range(2):
                load(WA[:, 2 + k, :].rearrange("p (h c) -> p h c", h=4),
                     L3_gnn_att[0, :, 32 * k:32 * k + 32].partition_broadcast(P), 3)
            norm_h(3, 5)

            def project3(i):
                act.wait_ge(s_t, GROUPS * 3 + i + 1)
                nc.scalar.activation(hT, PS[7][:, :], ACT.Copy).then_inc(s_tc, 1)
                act.wait_ge(s_p, GROUPS * 2 + i + 1)
                act.sem_inc(s_idleA, 1)
                for q in range(4):
                    nc.scalar.activation(BT[:, bass.ds(4 * i + q, 1), :].rearrange("p a f -> p (a f)"),
                                         PS[2 + q][:, 0:D], ACT.Copy)
                    last = nc.scalar.activation(SN[:, bass.ds(4 * i + q, 1), :].rearrange("p a f -> p (a f)"),
                                                PS[2 + q][:, D:D + 8], ACT.Copy)
                last.then_inc(s_p3c, 1)
            repeat(act, GROUPS, project3)
            act.wait_ge(s_alpha, 1)
            nc.scalar.activation(SI[:, 0:SC, :], SI[:, 0:SC, :], ACT.Exp).then_inc(s_alphae, 1)

        @block.vector
        def _(dve):
            done = Tally(dve, s_dve)

            def step(ins):
                done(ins)
                done.wait()

            v = nc.vector

            v.memset(accw[:, 0:1792].bitcast(I32), 0)
            step(v.memset(accw[:, 1792:6760], 0.0))
            v.memset(srcL[:, CH - 1, :], NOKEY).then_inc(s_pad, 1)
            v.memset(dstL[:, CH - 1, :], NOKEY).then_inc(s_pad, 1)
            v.memset(ones[:, :], 1.0)
            v.memset(onesb[:, :], 1.0)
            v.memset(rT[64:65, :], 1.0).then_inc(s_ones0, 1)
            dve.wait_ge(s_const, 2)
            v.tensor_copy(iota[:, :], tmpp.bitcast(I32))
            step(v.tensor_copy(lane[:, :], count_i[:, :]))
            v.tensor_scalar(ident[:, :], iota[:, 0:P], lane[:, 0:1], None, ALU.is_equal)
            v.tensor_scalar(below[:, :], iota[:, 0:P], lane[:, 0:1], None, ALU.is_gt)
            for c in range(CH):
                step(v.tensor_scalar(lanes[:, c:c + 1], lane[:, :], float(c * P), None, ALU.add))

            dve.wait_ge(s_edges, 96)
            v.tensor_copy(srcF[:, :, :], srcL[:, :, :])
            v.tensor_copy(dstF[:, :, :], dstL[:, :, :])
            v.tensor_scalar(last_i, dstL[:, :, P - 1], 7, None, ALU.logical_shift_right)
            step(v.tensor_scalar(srcL, srcL, 7, None, ALU.logical_shift_right))
            v.tensor_copy(last_b, last_i)
            step(v.tensor_copy(hiF, srcL))
            v.tensor_tensor(rise, last_b, lanes[:, :], ALU.add).then_inc(s_ask0, 1)
            dve.wait_ge(s_pe0, 1)
            v.tensor_copy(hiT[:, 0:512], PS[0][:, :])
            step(v.tensor_copy(hiT[:, 512:896], PS[1][:, 0:384]))

            def pairs(pe_count, order):
                for c in range(CH):
                    step(v.tensor_scalar(gbf[:, c, :], iota[:, :], rise[:, c:c + 1], None, ALU.is_gt))
                v.memset(junk_hi[:, 0:1], 0.0).then_inc(s_ask0, 1)
                dve.wait_ge(s_pe0, pe_count)
                for half in range(2):
                    step(v.tensor_scalar(kpair[:, half * HP:half * HP + HP], PS[2 + half][:, 0:HP],
                                         float(TILES - 1), None, ALU.min))
                step(v.tensor_tensor(bpair, iota[:, :], kpair, ALU.subtract))
                step(v.tensor_copy(regs[order:order + 1, :], bpair[order:order + 1, :]))
                step(v.tensor_scalar(tmpp, kpair, float(P), float(LASTBASE), ALU.mult, ALU.min))
                step(v.tensor_copy(regs[order + 32:order + 33, :], tmpp[order + 32:order + 33, :]))

            pairs(2, 0)
            for c in range(CH):
                last = v.tensor_scalar(sel[:, c, :], kpair, lanes[:, c:c + 1], None, ALU.is_equal)
            last.then_inc(s_ask0, 1)
            dve.wait_ge(s_pe0, 3)
            for half in range(2):
                v.tensor_copy(pay[:, half * HP:half * HP + HP, 0], PS[2 + half][:, 0:HP])
            step(v.tensor_scalar(tmpp, bpair, float(P), None, ALU.mult))
            step(v.tensor_tensor(dst_rel[:, :], pay[:, :, 0], tmpp, ALU.subtract))
            v.memset(junk_hi[:, 0:1], 0.0).then_inc(s_ask0, 1)
            dve.wait_ge(s_pe0, 4)
            for half in range(2):
                step(v.tensor_copy(pay[:, half * HP:half * HP + HP, 1], PS[2 + half][:, 0:HP]))
            v.tensor_scalar(src_idx[:, :], pay[:, :, 1], float(N - 1), None, ALU.min).then_inc(s_tables, 1)

            def one_hot8(i, q, slot):
                v.tensor_tensor(oh8[q], iota[:, 0:BLOCKS].unsqueeze(1).to_broadcast([P, POSB, BLOCKS]),
                                hiT[:, bass.ds(POSB * slot, POSB)].unsqueeze(2).to_broadcast([P, POSB, BLOCKS]),
                                ALU.is_equal).then_inc(s_oh8, 1)

            def histogram(i):
                for q in range(2):
                    if not first(i):
                        dve.wait_ge(s_hist, 2 * i + q - 1)
                    one_hot8(i, q, 2 * i + q)
            repeat(dve, STEPS // 2, histogram)
            dve.wait_ge(s_hist, STEPS)
            step(v.tensor_reduce(cnt_hi, PS[4][:, 0:POSB * BLOCKS].rearrange("p (t h) -> p h t", h=BLOCKS), AX, ALU.add))
            v.memset(junk_hi, 1.0)
            step(v.memset(t8, 0.0))
            step(v.tensor_tensor_scan(cum_hi, junk_hi, cnt_hi, 0.0, ALU.mult, ALU.add))
            step(v.tensor_tensor(base_hi, cum_hi, cnt_hi, ALU.subtract))

            def place(i):
                for q in range(2):
                    one_hot8(i, q, 2 * i + q)
                    dve.wait_ge(s_ahead, 2 * i + q + 1)
                    step(v.tensor_tensor(t8, PS[4][:, 0:POSB * BLOCKS].rearrange("p (t h) -> p t h", h=BLOCKS),
                                         base_hi.unsqueeze(1).to_broadcast([P, POSB, BLOCKS]), ALU.add))
                    step(v.tensor_tensor(t8, t8, oh8[q], ALU.mult))
                    v.tensor_reduce(posT[:, bass.ds(POSB * (2 * i + q), POSB)], t8, AX, ALU.add)
                    step(v.tensor_tensor(base_hi, base_hi, PS[5][:, 0:BLOCKS], ALU.add))
                    v.sem_inc(s_placed, 1)
            repeat(dve, STEPS // 2, place, done)
            step(v.memset(junk_hi[:, 0:1], 0.0))
            v.memset(junk_hi[:, 0:1], 0.0).then_inc(s_ask0, 1)
            dve.wait_ge(s_pe0, 5)
            v.tensor_copy(posF[:, 0:4, :].rearrange("p c e -> p (c e)"), PS[0][:, :])
            v.tensor_copy(posF[:, 4:7, :].rearrange("p c e -> p (c e)"), PS[1][:, 0:384]).then_inc(s_ask0, 1)
            dve.wait_ge(s_pe0, 6)
            step(v.tensor_scalar(tmpp, dst_rel[:, :], -1.0, None, ALU.is_gt))
            step(v.tensor_scalar(bpair, dst_rel[:, :], float(P), None, ALU.is_lt))
            step(v.tensor_tensor(tmpp, tmpp, bpair, ALU.mult))
            step(v.tensor_scalar(bpair, tmpp, float(-NOWHERE), float(NOWHERE), ALU.mult, ALU.add))
            for half in range(2):
                part = slice(half * HP, half * HP + HP)
                step(v.tensor_tensor(tmpp[:, part], tmpp[:, part], PS[2 + half][:, 0:HP], ALU.mult))
            step(v.tensor_tensor(tmpp, tmpp, bpair, ALU.add))
            step(v.tensor_copy(pos_idx[:, :], tmpp))
            v.memset(junk_hi[:, 0:1], 0.0).then_inc(s_tables, 1)

            for c in range(CH):
                step(v.tensor_scalar(xlast[:, c:c + 1], lanes[:, c:c + 1], float(P), float(P - 1), ALU.mult, ALU.add))
                step(v.tensor_scalar(junk_hi, cum_hi, xlast[:, c:c + 1], None, ALU.is_le))
                step(v.tensor_reduce(last_b[:, c:c + 1], junk_hi, AX, ALU.add))
            step(v.tensor_tensor(rise, last_b, lanes[:, :], ALU.add))
            pairs(7, 64)
            step(v.tensor_scalar(tmpp, kpair, float(TILES - 1), None, ALU.is_equal))
            step(v.tensor_scalar(junk_hi[:, 0:1], lane[:, 0:1], float(P - REST), -30000.0, ALU.is_lt, ALU.mult))
            step(v.tensor_scalar(tmpp, tmpp, junk_hi[:, 0:1], None, ALU.mult))
            step(v.scalar_tensor_tensor(s_shift[:, :], bpair, float(P), tmpp, ALU.mult, ALU.add))

            def stats(A, after):
                with dve.Fori(0, GROUPS) as g:
                    for q in range(4):
                        v.bn_stats(st[:, bass.ds(4 * g + q, 1), :].rearrange("p a f -> p (a f)"),
                                   A[:, bass.ds(4 * g + q, 1), :].rearrange("p a f -> p (a f)")).then_inc(s_bns, 1)
                dve.wait_ge(s_bns, NB * after)
                v.tensor_tensor(small[:, 0, :], st[:, :, 1], st[:, :, 4], ALU.add)
                v.tensor_tensor(small[:, 1, :], st[:, :, 2], st[:, :, 5], ALU.add)
                step(v.tensor_tensor(small[:, 2, :], st[:, :, 1], st[:, :, 4], ALU.subtract))
                step(v.tensor_tensor(small[:, 2, :], small[:, 2, :], small[:, 2, :], ALU.mult))
                v.tensor_scalar(small[:, 0, :], small[:, 0, :], 0.5, None, ALU.mult)
                step(v.tensor_scalar(small[:, 2, :], small[:, 2, :], 0.25, EPS, ALU.mult, ALU.add))
                v.scalar_tensor_tensor(small[:, 1, :], small[:, 1, :], 1.0 / D, small[:, 2, :], ALU.mult, ALU.add
                                       ).then_inc(s_st, 1)
                dve.wait_ge(s_sd, after)
                step(v.reciprocal(small[:, 3, :], small[:, 2, :]))
                step(v.scalar_tensor_tensor(small[:, 4, :], small[:, 0, :], -1.0, small[:, 3, :], ALU.mult, ALU.mult))

            def norm_ready():
                v.memset(small[:, 14, 0:1], 0.0).then_inc(s_nm, 1)

            dve.wait_ge(s_x, 32)
            stats(X, 1)
            norm_ready()

            def put(A, i, sem_put, turned_sem, k=0):
                if not first(i):
                    dve.wait_ge(turned_sem, GROUPS * k + i)
                v.tensor_scalar(group.rearrange("p (a f) -> p a f", a=4), A[:, bass.ds(4 * i, 4), 0:D], 1.0, None,
                                ALU.mult).then_inc(sem_put, 1)

            def mlp0(i):
                dve.wait_ge(s_h[0], 4 * i + 4)
                put(Hn, i, s_put, s_t)
                dve.wait_ge(s_e0, i + 1)
                v.tensor_scalar(BT[:, bass.ds(4 * i, 4), :].rearrange("p a f -> p (a f)"), PS[5][:, :], 0.2, None,
                                ALU.mult).then_inc(s_e0c, 1)
            repeat(dve, GROUPS, mlp0)

            v.memset(rows[:, :, D:ROW], 1.0)
            step(v.memset(ACC[:, :, :], 0.0))

            def sum_blocks(i, h, seg, acc, reg_row):
                for j in range(h * H, h * H + H):
                    b = dve.value_load(regs[reg_row:reg_row + 1, bass.ds(R * i + j, 1)], min_val=0, max_val=BLOCKS - 1)
                    to = ACC[:, bass.ds(b, 1), 0:129].rearrange("p a f -> p (a f)")
                    dve.wait_ge(seg, R * i + j + 1)
                    v.tensor_tensor(to, to, seg_ps(j % H), ALU.add).then_inc(acc, 1)
                    dve.wait_ge(acc, R * i + j + 1)

            def one_hots(i, h, used, ready):
                for j in range(h * H, h * H + H):
                    if not first(i):
                        dve.wait_ge(used, R * i - R + j + 1)
                    v.tensor_scalar(onehot[:, j, :], iota[:, 0:P], dst_rel[:, bass.ds(R * i + j, 1)], None,
                                    ALU.is_equal).then_inc(ready, 1)

            def sum0(i):
                for h in range(2):
                    one_hots(i, h, s_seg0, s_oh0)
                    sum_blocks(i, h, s_seg0, s_acc0, 0)
            repeat(dve, ITERS, sum0)

            step(v.tensor_copy(cnt_dst, ACC[:, :, D]))
            step(v.tensor_scalar(small[:, 5, :], cnt_dst, 1.0, None, ALU.max))
            step(v.reciprocal(small[:, 5, :], small[:, 5, :]))
            step(v.tensor_tensor(ACC[:, :, 0:D], ACC[:, :, 0:D], spread(small[:, 5, :], NB), ALU.mult))
            v.tensor_tensor(ACC[:, :, 0:D], ACC[:, :, 0:D], Hn[:, :, :], ALU.subtract).then_inc(s_diff, 1)
            dve.wait_ge(s_diffa, 1)
            v.tensor_reduce(small[:, 5, :], ACC[:, :, 0:D], AX, ALU.add).then_inc(s_diff, 1)
            dve.wait_ge(s_diffa, 2)
            step(v.tensor_tensor(BT[:, :, :], BT[:, :, :], spread(small[:, 5, :], NB), ALU.mult))
            step(v.tensor_tensor(BT[:, :, :], BT[:, :, :], Hn[:, :, :], ALU.add))
            stats(BT, 2)
            step(v.tensor_tensor(BT[:, :, :], BT[:, :, :], spread(small[:, 3, :], NB), ALU.mult))
            step(v.tensor_tensor(BT[:, :, :], BT[:, :, :], spread(small[:, 4, :], NB), ALU.add))
            step(v.tensor_tensor(BT[:, :, :], BT[:, :, :], over(g0, NB), ALU.mult))
            step(v.tensor_tensor(BT[:, :, :], BT[:, :, :], over(be0, NB), ALU.add))
            step(v.tensor_tensor(X[:, :, :], X[:, :, :], BT[:, :, :], ALU.add))
            v.memset(small[:, 14, 0:1], 0.0).then_inc(s_wdone[0], 1)
            v.memset(small[:, 14, 1:2], 0.0).then_inc(s_xnew[0], 1)

            stats(X, 3)
            norm_ready()
            step(v.memset(group[:, 0:1], 0.0))

            def project1(i):
                dve.wait_ge(s_h[1], 4 * i + 4)
                put(Hn, i, s_put, s_t, 1)
                dve.wait_ge(s_p1a, i + 1)
                for q in range(4):
                    at = bass.ds(4 * i + q, 1)
                    v.tensor_tensor(BT[:, at, :].rearrange("p a f -> p (a f)"), PS[2 + q][:, D:2 * D], b1bc, ALU.add)
                    last = v.tensor_tensor(CT[:, at, :].rearrange("p a f -> p (a f)"), PS[2 + q][:, 2 * D:3 * D], ub1bc,
                                           ALU.add)
                last.then_inc(s_p1c, 1)
            repeat(dve, GROUPS, project1)
            step(v.memset(mrow[:, :, D:ROW], 1.0))

            def edges(i):
                for h in range(2):
                    for j in range(h * H, h * H + H):
                        if not first(i):
                            dve.wait_ge(s_turn, R * i - R + j + 1)
                        v.tensor_scalar(onehot[:, j, :], iota[:, 0:P], dst_rel[:, bass.ds(R * i + j, 1)], None,
                                        ALU.is_equal).then_inc(s_oh1, 1)
                    for j in range(h * H, h * H + H):
                        dve.wait_ge(s_row[j], landed(1, i + 1))
                        dve.wait_ge(s_pre, R * i + j + 1)
                        v.tensor_tensor(rows[:, j, 0:D], rows[:, j, 0:D], pre_ps(j % H), ALU.add).then_inc(s_sum1, 1)
                    part = slice(h * H, h * H + H)
                    if not first(i):
                        for j in range(h * H, h * H + H):
                            dve.wait_ge(s_sent[j], 16 * i)
                    v.tensor_scalar(mrow[:, part, D + 1:D + 3], pay[:, bass.ds(R * i + h * H, H), :], 1.0, None, ALU.mult)
                    dve.wait_ge(s_sum1, R * i + h * H + H)
                    dve.wait_ge(s_ln, 2 * i + h + 1)
                    v.scalar_tensor_tensor(mrow[:, part, 0:D], rows[:, part, 0:D], 0.0, lnp[:, :, :], ALU.max, ALU.add
                                           ).then_inc(s_msg, 1)
            repeat(dve, ITERS, edges)

            for j in range(R):
                dve.wait_ge(s_row[j], landed(1, ITERS))
            dve.wait_ge(s_msg, 2 * ITERS)
            step(v.memset(ACC[:, :, :], 0.0))
            v.memset(small[:, 14, 0:1], 0.0).then_inc(s_tables, 1)

            def sum1(i):
                for h in range(2):
                    for j in range(h * H, h * H + H):
                        if not first(i):
                            dve.wait_ge(s_seg1, R * i - R + j + 1)
                        dve.wait_ge(s_edge[j], landed(1, i + 1))
                        v.tensor_scalar(onehot[:, j, :], iota[:, 0:P], s_shift[:, bass.ds(R * i + j, 1)],
                                        rows[:, j, D + 2:D + 3], ALU.add, ALU.is_equal).then_inc(s_oh1s, 1)
                    v.tensor_scalar(payS[:, bass.ds(R * i + h * H, H), :], rows[:, h * H:h * H + H, D + 1:D + 3], 1.0,
                                    None, ALU.mult).then_inc(s_took, 1)
                    sum_blocks(i, h, s_seg1, s_acc1, 64)
            repeat(dve, ITERS, sum1)

            cnt_src = small[:, 8, :]
            step(v.tensor_copy(cnt_src, ACC[:, :, D]))
            for b in range(NB):
                last = v.scalar_tensor_tensor(CT[:, b, :], b2Ubc, cnt_src[:, b:b + 1], CT[:, b, :], ALU.mult, ALU.add)
            last.then_inc(s_node1, 1)

            def update(i):
                put(ACC, i, s_put1, s_u1)
                at = CT[:, bass.ds(4 * i, 4), :].rearrange("p a f -> p (a f)")
                dve.wait_ge(s_u2, i + 1)
                v.tensor_tensor(at, at, PS[6][:, :], ALU.add).then_inc(s_zin, 1)
                dve.wait_ge(s_zin, i + 1)
                dve.wait_ge(s_zl, i + 1)
                if not first(i):
                    dve.wait_ge(s_u3, i)
                v.scalar_tensor_tensor(zgroup, at, 0.0, lnp[:, 0:4, :].rearrange("p a f -> p (a f)"), ALU.max, ALU.add
                                       ).then_inc(s_z1, 1)
                dve.wait_ge(s_u4, i + 1)
                v.tensor_tensor(BT[:, bass.ds(4 * i, 4), :], PS[4][:, :].rearrange("p (a f) -> p a f", a=4),
                                over(ub2bc, 4), ALU.add).then_inc(s_u4c, 1)
            repeat(dve, GROUPS, update)
            dve.wait_ge(s_u4c, GROUPS)

            real = small[:, 9, 0:1]
            step(v.tensor_scalar(real, lane[:, :], float(TAIL), None, ALU.is_lt))

            def node_mean(A, order):
                step(v.tensor_scalar(A[:, BLOCKS - 1, :], A[:, BLOCKS - 1, :], real, None, ALU.mult))
                v.tensor_reduce(lnp[:, 0, :], A[:, 0:BLOCKS, :].rearrange("p b f -> p f b"), AX, ALU.add).then_inc(s_bn, 1)
                dve.wait_ge(s_bnsum, order)

            node_mean(BT, 1)
            step(v.tensor_scalar(lnp[:, 2, :], PS[0][:, 0:D], 1.0 / N, None, ALU.mult))
            step(v.tensor_tensor(BT[:, :, :], BT[:, :, :], over(lnp[:, 2, :], NB), ALU.subtract))
            step(v.tensor_tensor(CT[:, :, :], BT[:, :, :], BT[:, :, :], ALU.mult))
            node_mean(CT, 2)
            v.tensor_scalar(lnp[:, 1, :], PS[0][:, 0:D], 1.0 / N, EPS, ALU.mult, ALU.add).then_inc(s_bn, 1)
            dve.wait_ge(s_bnsd, 1)
            step(v.reciprocal(lnp[:, 1, :], lnp[:, 1, :]))
            step(v.tensor_tensor(lnp[:, 1, :], lnp[:, 1, :], g1, ALU.mult))
            step(v.tensor_tensor(BT[:, :, :], BT[:, :, :], over(lnp[:, 1, :], NB), ALU.mult))
            step(v.tensor_tensor(BT[:, :, :], BT[:, :, :], over(be1, NB), ALU.add))
            step(v.tensor_tensor(X[:, :, :], X[:, :, :], BT[:, :, :], ALU.add))
            v.memset(small[:, 14, 0:1], 0.0).then_inc(s_wdone[1], 1)
            v.memset(small[:, 14, 1:2], 0.0).then_inc(s_xnew[1], 1)

            step(v.tensor_copy(dst_idx[:, :], payS[:, :, 0]))
            step(v.tensor_tensor(src_relS[:, :], payS[:, :, 1], s_shift[:, :], ALU.subtract))
            step(v.tensor_scalar(maskS, src_relS[:, :], -1.0, None, ALU.is_gt))
            step(v.tensor_scalar(payS[:, :, 0], src_relS[:, :], float(P), None, ALU.is_lt))
            step(v.tensor_tensor(maskS, maskS, payS[:, :, 0], ALU.mult))
            step(v.tensor_scalar(maskS, maskS, -1.0, BIG, ALU.add, ALU.mult))
            v.memset(small[:, 14, 0:1], 0.0).then_inc(s_tables, 1)
            v.memset(scan_idx, 0)
            v.memset(scan_dst, NOKEY)
            v.memset(scan_prev, -1).then_inc(s_scanfree, 1)
            stats(X, 4)
            norm_ready()

            def project2(i):
                dve.wait_ge(s_h[2], 4 * i + 4)
                put(Hn, i, s_put, s_t, 2)
            repeat(dve, GROUPS, project2)
            dve.wait_ge(s_p2c, GROUPS)
            step(v.tensor_copy(small[:, 8, :], ACC[:, :, D]))
            v.memset(ACC[:, :, D], 1.0).then_inc(s_store2, 1)
            step(v.memset(small[:, 10:12, :], 0.0))
            v.memset(m_run[0:1, 1:2], -BIG)
            step(v.memset(m_all[:, 1:2], -BIG))
            dve.wait_ge(s_tab[2], 16)
            step(v.memset(ACC[:, :, :], 0.0))
            dve.wait_ge(s_sc2, 32)

            def attend(i):
                for h in range(2):
                    part = slice(h * H, h * H + H)
                    blocks = {}
                    for j in range(h * H, h * H + H):
                        blocks[j] = dve.value_load(regs[64:65, bass.ds(R * i + j, 1)], min_val=0, max_val=BLOCKS - 1)
                        if not first(i):
                            dve.wait_ge(s_seg2, R * i - R + j + 1)
                        done(v.scalar_tensor_tensor(onehot[:, j, :], iota[:, 0:P], src_relS[:, bass.ds(R * i + j, 1)],
                                                    BT[:, bass.ds(blocks[j], 1), :].rearrange("p a f -> p (a f)"),
                                                    ALU.is_equal, ALU.mult, accum_out=sv[:, j:j + 1]))
                    done.wait()
                    for j in range(h * H, h * H + H):
                        dve.wait_ge(s_row[j], landed(2, i + 1))
                    step(v.tensor_tensor(sv[:, part], sv[:, part], rows[:, part, D + 1], ALU.add))
                    step(v.scalar_tensor_tensor(lm[:, part], sv[:, part], 0.2, sv[:, part], ALU.mult, ALU.max))
                    step(v.tensor_tensor(lm[:, part], lm[:, part], maskS[:, bass.ds(R * i + h * H, H)], ALU.add))
                    v.tensor_reduce(sc_mx, lm[:, part], AX, ALU.max).then_inc(s_mx, 1)
                    dve.wait_ge(s_mxt, 2 * i + h + 1)
                    step(v.tensor_reduce(sc_top, PS[6][0:1, 0:P], AX, ALU.max))
                    v.tensor_tensor(m_run[0:1, h:h + 1], m_run[0:1, 1 - h:2 - h], sc_top, ALU.max).then_inc(s_mnew, 1)
                    dve.wait_ge(s_mbc, 2 * i + h + 1)
                    step(v.tensor_copy(m_all[:, h:h + 1], PS[6][:, 256:257]))
                    v.tensor_scalar(negm[:, h:h + 1], m_all[:, h:h + 1], -1.0, None, ALU.mult).then_inc(s_negm, 1)
                    dve.wait_ge(s_negm, 2 * i + h + 1)
                    dve.wait_ge(s_wgt, 2 * i + h + 1)
                    for j in range(h * H, h * H + H):
                        v.tensor_scalar(onehot[:, j, :], iota[:, 0:P], src_relS[:, bass.ds(R * i + j, 1)],
                                        wgt[:, j:j + 1], ALU.is_equal, ALU.mult).then_inc(s_oh2, 1)
                    for j in range(h * H, h * H + H):
                        to = ACC[:, bass.ds(blocks[j], 1), 0:129].rearrange("p a f -> p (a f)")
                        dve.wait_ge(s_seg2, R * i + j + 1)
                        if j == h * H:
                            v.scalar_tensor_tensor(to, to, fade[:, h:h + 1], seg_ps(j % H), ALU.mult, ALU.add
                                                   ).then_inc(s_acc2, 1)
                        else:
                            v.tensor_tensor(to, to, seg_ps(j % H), ALU.add).then_inc(s_acc2, 1)
                        step(v.tensor_scalar(m_block[:, bass.ds(blocks[j], 1)], m_all[:, h:h + 1], 1.0, None, ALU.mult))
                        dve.wait_ge(s_acc2, R * i + j + 1)
            repeat(dve, ITERS, attend, done)

            step(v.tensor_scalar(small[:, 6, :], m_block, -1.0, m_all[:, 1:2], ALU.mult, ALU.add))
            v.tensor_scalar(small[:, 6, :], small[:, 6, :], 87.0, 0.0, ALU.min, ALU.max).then_inc(s_fin2, 1)
            dve.wait_ge(s_fin2a, 1)
            step(v.scalar_tensor_tensor(small[:, 6, :], small[:, 6, :], 9e-15, ACC[:, :, D], ALU.mult, ALU.add))
            step(v.reciprocal(small[:, 6, :], small[:, 6, :]))
            step(v.tensor_tensor(BT[:, :, :], ACC[:, :, 0:D], spread(small[:, 6, :], NB), ALU.mult))
            step(v.tensor_scalar(CT[:, :, :], BT[:, :, :], 0.0, None, ALU.max))
            v.tensor_scalar(BT[:, :, :], BT[:, :, :], 0.0, None, ALU.min).then_inc(s_fin2, 1)
            dve.wait_ge(s_fin2a, 2)
            step(v.scalar_tensor_tensor(CT[:, :, :], BT[:, :, :], -1.0, CT[:, :, :], ALU.add, ALU.add))
            step(v.tensor_tensor(X[:, :, :], X[:, :, :], CT[:, :, :], ALU.add))
            v.memset(small[:, 14, 0:1], 0.0).then_inc(s_wdone[2], 1)
            v.memset(small[:, 14, 1:2], 0.0).then_inc(s_xnew[2], 1)

            v.memset(fill, 0.0).then_inc(s_zero, 1)
            stats(X, 5)
            norm_ready()
            dve.wait_ge(s_w[3], 48)
            for k in range(2):
                step(v.tensor_tensor(WA[:, 4, :], WA[:, 0, :], WA[:, 2 + k, :], ALU.mult))
                step(v.tensor_reduce(WA[:, 1, 4 * k:4 * k + 4], WA[:, 4, :].rearrange("p (h c) -> p h c", h=4), AX,
                                     ALU.add))
            v.memset(small[:, 14, 0:1], 0.0).then_inc(s_folded3, 1)

            def project3(i):
                dve.wait_ge(s_h[3], 4 * i + 4)
                put(Hn, i, s_put, s_t, 3)
            repeat(dve, GROUPS, project3)

            v.tensor_scalar(upto, iota[:, 0:P], lane[:, 0:1], None, ALU.is_ge).then_inc(s_cum, 1)
            dve.wait_ge(s_cump, 1)
            nodes = slice(0, BLOCKS)
            total, cum, has = small[:, 10, nodes], small[:, 11, nodes], small[:, 5, nodes]
            start_f, end_f, one_row = small[:, 2, nodes], small[:, 3, nodes], small[:, 4, nodes]
            step(v.memset(one_row, 1.0))
            step(v.tensor_copy(total, PS[6][:, 64:64 + BLOCKS]))
            step(v.tensor_tensor_scan(cum, one_row, total, 0.0, ALU.mult, ALU.add))
            step(v.tensor_tensor(cum, cum, total, ALU.subtract))
            step(v.tensor_tensor(end_f, PS[6][:, 0:BLOCKS], cum, ALU.add))
            step(v.tensor_tensor(start_f, end_f, cnt_dst[:, nodes], ALU.subtract))
            step(v.tensor_scalar(end_f, end_f, -1.0, 0.0, ALU.add, ALU.max))
            step(v.tensor_copy(end_idx[:, nodes], end_f))
            step(v.tensor_scalar(has, cnt_dst[:, nodes], 1.0, None, ALU.min))
            step(v.tensor_tensor(start_f, start_f, has, ALU.mult))
            step(v.tensor_scalar(end_f, has, float(-NOWHERE), float(NOWHERE), ALU.mult, ALU.add))
            step(v.tensor_tensor(start_f, start_f, end_f, ALU.add))
            step(v.tensor_copy(start_idx[:, nodes], start_f))

            dve.wait_ge(s_scan, 64)
            dve.wait_ge(s_prev, 48)
            step(v.tensor_tensor(cont, scan_dst, scan_prev, ALU.is_equal))
            step(v.tensor_scalar(contneg, cont, -1.0, 1e38, ALU.add, ALU.mult))
            step(v.tensor_reduce(all_cont, cont, AX, ALU.min))
            dve.wait_ge(s_p3c, GROUPS)
            step(v.memset(mrow_flat[:, 416:1248], 0.0))

            def take(i):
                for h in range(2):
                    for j in range(h * H, h * H + H):
                        dve.wait_ge(s_row[j], landed(3, i + 1))
                    v.tensor_scalar(SI[:, bass.ds(R * i + h * H, H), :], g4[:, h * H:h * H + H, :], 1.0, None, ALU.mult
                                    ).then_inc(s_got3, 1)
            repeat(dve, SG // R, take)
            dve.wait_ge(s_got3, 2 * (SG // R))

            def segments(to, of, w, factor, whole, op0, op1, start, order):
                for c in range(w):
                    step(v.tensor_tensor_scan(to[:, :, c], factor, of[:, 0:SC, c], start, op0, op1))
                step(v.tensor_copy(last_v[:, 0:w], to[:, SC - 1, :]))
                v.tensor_copy(last_c[:, 0:w], whole.to_broadcast([P, w])).then_inc(s_carry, 1)
                dve.wait_ge(s_carryp, 2 * order + 1)
                step(v.tensor_copy(carry_row[0:w, P:3 * P], PS[5][0:w, 0:2 * P]))
                step(v.tensor_tensor_scan(carry_row[0:w, P:2 * P], carry_row[0:w, 2 * P:3 * P], carry_row[0:w, P:2 * P],
                                          start, op0, op1))
                step(v.memset(carry_row[0:w, 0:1], start))
                v.tensor_scalar(carry_row[0:w, 1:P], carry_row[0:w, P:2 * P - 1], 1.0, None, ALU.mult
                                ).then_inc(s_carry, 1)
                dve.wait_ge(s_carryp, 2 * order + 2)
                step(v.tensor_copy(last_v[:, 0:w], PS[5][:, 256:256 + w]))
                for c in range(w):
                    step(v.tensor_tensor_scan(to[:, :, c], factor, of[:, 0:SC, c], last_v[:, c:c + 1], op0, op1))

            step(v.tensor_scalar(all_neg, all_cont, -1.0, 1e38, ALU.add, ALU.mult))
            segments(MX, SI, 4, contneg, all_neg, ALU.add, ALU.max, -1e38, 0)
            v.memset(small[:, 14, 0:1], 0.0).then_inc(s_scanned, 1)
            dve.wait_ge(s_mxnode, 16 * BLOCKS)
            target = SN[:, :, 4:8]
            step(v.tensor_tensor(mx_node, mx_node, target, ALU.add))
            step(v.tensor_copy(fill_node[:, :, 0:4], target))
            v.scalar_tensor_tensor(fill_node[:, :, 4:8], mx_node, 0.2, mx_node, ALU.mult, ALU.max).then_inc(s_fill, 1)
            dve.wait_ge(s_fillback, 16)
            segments(FO, fill, 8, cont, all_cont, ALU.mult, ALU.add, 0.0, 1)
            edges_si = SI[:, 0:SC, :]
            step(v.tensor_tensor(edges_si, edges_si, FO[:, :, 0:4], ALU.add))
            step(v.scalar_tensor_tensor(edges_si, edges_si, 0.2, edges_si, ALU.mult, ALU.max))
            step(v.tensor_tensor(edges_si, edges_si, FO[:, :, 4:8], ALU.subtract))
            v.tensor_scalar(edges_si, edges_si, 0.0, None, ALU.min).then_inc(s_alpha, 1)
            dve.wait_ge(s_alphae, 1)
            dve.wait_ge(s_segmax, 16)
            segments(MX, SI, 4, cont, all_cont, ALU.mult, ALU.add, 0.0, 2)
            v.memset(small[:, 14, 0:1], 0.0).then_inc(s_scanned, 1)
            dve.wait_ge(s_sumnode, 16 * BLOCKS)
            step(v.tensor_scalar(mx_node, sum_node, 1e-16, None, ALU.add))
            step(v.reciprocal(mx_node, mx_node))
            step(v.tensor_tensor(sum_node, sum_node, mx_node, ALU.mult))
            step(v.tensor_tensor(sum_node[:, nodes, :], sum_node[:, nodes, :], has.unsqueeze(2).to_broadcast([P, BLOCKS, 4]),
                                 ALU.mult))
            heads = BT[:, :, :].rearrange("p b (h c) -> p (b h) c", h=4)
            step(v.tensor_tensor(heads, heads, sum_node.rearrange("p b h -> p (b h)").unsqueeze(2)
                                 .to_broadcast([P, NB * 4, 32]), ALU.mult))
            step(v.tensor_tensor(X[:, :, :], X[:, :, :], BT[:, :, :], ALU.add))
            v.memset(small[:, 14, 1:2], 0.0).then_inc(s_xnew[3], 1)


_INS = ['x', 'src', 'dst', 'edge_attr_128', 'L0_gnn_W1', 'L0_gnn_b1', 'L0_gnn_W2', 'L0_gnn_b2', 'L0_gnn_gamma', 'L0_gnn_beta', 'L1_gnn_W1', 'L1_gnn_b1', 'L1_gnn_W2', 'L1_gnn_b2', 'L1_gnn_U1', 'L1_gnn_ub1', 'L1_gnn_U2', 'L1_gnn_ub2', 'L1_gnn_gamma', 'L1_gnn_beta', 'L2_gnn_W', 'L2_gnn_attn', 'L3_gnn_weight', 'L3_gnn_att']
_OUTS = [((6250, 128), 'float32')]


def kernel(**inputs):
    import numpy as _np
    import concourse.bacc as _bacc
    from concourse import mybir as _mybir
    from concourse.bass_utils import run_bass_kernel_spmd as _run

    nc = _bacc.Bacc("TRN2", target_bir_lowering=False, num_devices=1)
    arrays, args = {}, {}
    for name in _INS:
        a = _np.ascontiguousarray(inputs[name])
        arrays[f"in_{name}_dram"] = a
        args[name] = nc.dram_tensor(f"in_{name}_dram", a.shape, _mybir.dt.from_np(a.dtype), kind="ExternalInput").ap()
    for i, (shape, dtype) in enumerate(_OUTS):
        dt = _mybir.dt.from_np(_np.dtype(dtype))
        args["out"] = nc.dram_tensor(f"out_{i}_dram", shape, dt, kind="ExternalOutput").ap()
    gnn_kernel(nc, **args)
    r = _run(nc, [arrays], core_ids=[0])
    return r.results[0]["out_0_dram"]
```

```python
from contextlib import ExitStack

import concourse.bass as bass
from concourse import mybir

F32 = mybir.dt.float32
BF16 = mybir.dt.bfloat16
I32 = mybir.dt.int32
ALU = mybir.AluOpType
ACT = mybir.ActivationFunctionType
AX = mybir.AxisListType.X

P = 128
D = 128
N, E = 6250, 100000
BLOCKS = -(-N // P)
NB = 52
GROUPS = NB // 4
TAIL = N - (BLOCKS - 1) * P
TILES = -(-E // P)
LASTBASE = E - P
REST = E - (TILES - 1) * P
CH = -(-TILES // P)
PAIRS = TILES + BLOCKS - 1
HP = PAIRS // 2
R = 10
H = 5
ITERS = PAIRS // R
U = 4
ITERS2 = -(-PAIRS // (U * H))
W2 = (ITERS2 * U + 1) * H
ROW = 132
NOKEY = 8191
NOWHERE = 200000
BIG = 1e30
HB = 8
STEPS = -(-TILES // HB)
SC = -(-E // P)
SREST = E - (P - 1) * SC
SG = -(-SC // R) * R
EPS = 1e-5
IN_RANGE = "a pair's tile is a count cut off at the last tile, and its block the rest of the pair's number"


class Tally:

    def __init__(self, eng, sem):
        self.eng, self.sem, self.n, self.lead = eng, sem, 0, 0

    def __call__(self, ins):
        ins.then_inc(self.sem, 1)
        self.n += 1

    def wait(self, but=0):
        self.eng.wait_ge(self.sem, self.lead + self.n - but)


def repeat(eng, times, body, *tallies, peel=1):
    for k in range(peel):
        before = [t.n for t in tallies]
        body(k)
    start = [t.n for t in tallies]
    per = [n - b for n, b in zip(start, before)]
    with eng.Fori(peel, times) as i:
        for t, k in zip(tallies, per):
            t.lead = (i - peel) * k
        body(i)
    for t, n, k in zip(tallies, start, per):
        t.lead, t.n = 0, n + k * (times - peel)


def first(i):
    return isinstance(i, int) and i == 0


def landed(k, i, u=0):
    before = (0, ITERS, 2 * ITERS if u < 2 else 0, 2 * ITERS + ITERS2)[k]
    return 16 * H * (before + i)


def halves(i):
    return (((i, 0), None if first(i) else (i - 1, 1)), ((i, 1), (i, 0)))


def gnn_kernel(nc, x, src, dst, edge_attr_128, L0_gnn_W1, L0_gnn_b1, L0_gnn_W2, L0_gnn_b2, L0_gnn_gamma,
               L0_gnn_beta, L1_gnn_W1, L1_gnn_b1, L1_gnn_W2, L1_gnn_b2, L1_gnn_U1, L1_gnn_ub1, L1_gnn_U2,
               L1_gnn_ub2, L1_gnn_gamma, L1_gnn_beta, L2_gnn_W, L2_gnn_attn, L3_gnn_weight, L3_gnn_att, out):
    with ExitStack() as ctx:
        def sb(name, shape, dt=F32):
            return ctx.enter_context(nc.sbuf_tensor(name, shape, dt))

        def sem(name):
            return ctx.enter_context(nc.semaphore(name))

        def ring(name, n):
            return [sem(f"{name}{k}") for k in range(n)]

        table0 = nc.dram_tensor("table0", [NB * P, D], F32, kind="Internal").ap()
        table1 = nc.dram_tensor("table1", [NB * P, D], F32, kind="Internal").ap()
        table2 = nc.dram_tensor("table2", [NB * P, 130], F32, kind="Internal").ap()
        table3 = nc.dram_tensor("table3", [NB * P, 4], F32, kind="Internal").ap()
        messages = nc.dram_tensor("messages", [E, ROW], F32, kind="Internal").ap()
        score2 = nc.dram_tensor("score2", [NB * P], F32, kind="Internal").ap()
        seg_max = nc.dram_tensor("seg_max", [P * SC, 4], F32, kind="Internal").ap()
        seg_sum = nc.dram_tensor("seg_sum", [P * SC, 4], F32, kind="Internal").ap()
        seg_fill = nc.dram_tensor("seg_fill", [P * SC, 8], F32, kind="Internal").ap()

        X = sb("X", [P, NB, D])
        Hn = sb("Hn", [P, NB, D])
        ACC = sb("ACC", [P, NB, 130])
        BT = sb("BT", [P, NB, D])
        CT = sb("CT", [P, NB, D])
        accw = ACC[:, :, :].rearrange("p b f -> p (b f)")
        btw = BT[:, :, :].rearrange("p b f -> p (b f)")
        ctw = CT[:, :, :].rearrange("p b f -> p (b f)")
        hnw = Hn[:, :, :].rearrange("p b f -> p (b f)")

        count_i = sb("count_i", [P, 1], I32)
        iota = sb("iota", [P, PAIRS])
        lane = sb("lane", [P, 1])
        lanes = sb("lanes", [P, CH])
        ident = sb("ident", [P, P])
        ones = sb("ones", [P, P])
        below = sb("below", [P, P], BF16)
        onesb = sb("onesb", [P, P], BF16)

        dst_rel = sb("dst_rel", [P, W2])
        pay = sb("pay", [P, PAIRS, 2])
        src_idx = sb("src_idx", [P, W2], I32)
        pos_idx = sb("pos_idx", [P, W2], I32)
        regs = sb("regs", [P, W2], I32)
        s_shift = sb("s_shift", [P, PAIRS])
        payS = sb("payS", [P, PAIRS, 2])
        dst_idx = pos_idx
        src_relS = dst_rel
        maskS = src_idx[:, :].bitcast(F32)

        rows = sb("rows", [P, R, ROW])
        mrow = sb("mrow", [P, R, ROW])
        edge = sb("edge", [P, R, D])
        onehot = sb("onehot", [P, R, P])
        turned = sb("turned", [P, H, 2, P])
        lnp = sb("lnp", [P, H, D])
        first_block = sb("first_block", [P, U * ITERS2])
        key = sb("key", [P, R])
        idxs = sb("idxs", [P, U * H], I32)
        pidx = sb("pidx", [P, R], I32)
        WA = sb("WA", [P, 14, D])
        small = sb("small", [P, 16, NB])
        st = mrow[:, :, :].rearrange("p r f -> p (r f)")[:, 0:NB * 6].rearrange("p (b s) -> p b s", s=6)
        mrow_flat = mrow[:, :, :].rearrange("p r f -> p (r f)")
        edge_flat = edge[:, :, :].rearrange("p r f -> p (r f)")
        tw = turned[:, :, :, :].rearrange("p a b f -> p (a b f)")
        hT, rT = tw[:, 0:512], tw[:, 512:1024]

        group = edge[:, 0:4, :].rearrange("p a f -> p (a f)")
        zgroup = edge[:, 4:8, :].rearrange("p a f -> p (a f)")

        PS = [ctx.enter_context(nc.psum_tensor(f"PS{k}", [P, 512], F32)) for k in range(8)]

        def seg_ps(h, q):
            return PS[2 * h + q // 3][:, 160 * (q % 3):160 * (q % 3) + 129]

        def turn_ps(q):
            return PS[q // 2][:, 256 * (q % 2):256 * (q % 2) + 256]

        def pre_ps(h, q):
            return PS[3 + 2 * h + q // 4][:, D * (q % 4):D * (q % 4) + D]

        srcL = accw[:, 0:896].bitcast(I32).rearrange("p (c e) -> p c e", e=P)
        dstL = accw[:, 896:1792].bitcast(I32).rearrange("p (c e) -> p c e", e=P)
        srcF = accw[:, 1792:2688].rearrange("p (c e) -> p c e", e=P)
        dstF = accw[:, 2688:3584].rearrange("p (c e) -> p c e", e=P)
        hiF = accw[:, 3584:4480].rearrange("p (c e) -> p c e", e=P)
        hiT = mrow_flat[:, 320:1216]
        posT = edge_flat[:, 0:896]
        posF = tw[:, 0:896].rearrange("p (c e) -> p c e", e=P)
        sel = btw[:, 0:CH * PAIRS].rearrange("p (c n) -> p c n", n=PAIRS)
        gbf = ctw[:, 0:CH * PAIRS // 2].bitcast(BF16).rearrange("p (c n) -> p c n", n=PAIRS)
        kpair = ctw[:, 2910:2910 + PAIRS]
        bpair = ctw[:, 3750:3750 + PAIRS]
        tmpp = ctw[:, 4590:4590 + PAIRS]
        oh8 = [ctw[:, 5430 + 200 * q:5430 + 200 * q + 196].bitcast(BF16).rearrange("p (t h) -> p t h", h=BLOCKS)
               for q in range(2)]
        ohp = ctw[:, 5430:5430 + 245].bitcast(BF16).rearrange("p (t h) -> p t h", h=BLOCKS)
        tpos = ctw[:, 5930:5930 + 490].rearrange("p (t h) -> p t h", h=BLOCKS)
        cnt_hi, cum_hi, base_hi, junk_hi = (ctw[:, 6420 + 49 * k:6469 + 49 * k] for k in range(4))
        last_b, rise, xlast = (ctw[:, 6616 + 8 * k:6616 + 8 * k + CH] for k in range(3))
        last_i = ctw[:, 6640:6640 + CH].bitcast(I32)

        W0_1, W0_2 = WA[:, 0, 0:64], WA[0:65, 1, :]
        b0_1 = WA[0:64, 2, 0:1]
        g0, be0 = WA[:, 3, :], WA[:, 4, :]
        W1abu, W1c = WA[:, 0:3, :], WA[:, 3, :]
        b1bc, ub1bc, W1_2, U1b, U2w, ub2bc, g1, be1, W2U, b2Ubc = (WA[:, k, :] for k in range(4, 14))
        b1_2 = small[:, 15, 0:1]

        cnt_dst = small[:, 7, :]
        misc = small[:, 10, :]
        lm = misc[:, 0:12].rearrange("p (h q) -> p h q", h=2)
        sv, wgt = misc[:, 12:22], misc[:, 22:32]
        negm, m_all, fade, m_run = misc[:, 32:34], misc[:, 34:36], misc[:, 36:38], misc[:, 38:40]
        m_block = small[:, 11, :]
        history = s_shift[:, 0:U * ITERS2]

        pay_flat = pay[:, :, :].rearrange("p n a -> p (n a)")
        payS_flat = payS[:, :, :].rearrange("p n a -> p (n a)")
        scan_idx = pay_flat[:, 0:SG].bitcast(I32)
        scan_dst = pay_flat[:, 800:800 + SC].bitcast(I32)
        scan_prev = payS_flat[:, 0:SC].bitcast(I32)
        contneg = payS_flat[:, 800:800 + SC]
        cont = s_shift[:, 0:SC]
        g4 = edge[:, :, :].rearrange("p r f -> p (r f)")[:, 0:4 * R].rearrange("p (r f) -> p r f", f=4)
        SN = mrow_flat[:, 0:416].rearrange("p (b f) -> p b f", f=8)
        mx_node = mrow_flat[:, 416:624].rearrange("p (b f) -> p b f", f=4)
        sum_node = mrow_flat[:, 624:832].rearrange("p (b f) -> p b f", f=4)
        fill_node = mrow_flat[:, 832:1248].rearrange("p (b f) -> p b f", f=8)
        SI = ctw[:, 0:4 * SG].rearrange("p (i f) -> p i f", f=4)
        MX = ctw[:, 3200:3200 + 4 * SC].rearrange("p (i f) -> p i f", f=4)
        fill = accw[:, 0:8 * SC].rearrange("p (i f) -> p i f", f=8)
        FO = hnw[:, 0:8 * SC].rearrange("p (i f) -> p i f", f=8)
        upto = onehot[:, 0, :]
        start_idx, end_idx = small[:, 12, :].bitcast(I32), small[:, 13, :].bitcast(I32)
        last_v, last_c = small[:, 0, 0:8], small[:, 0, 8:16]
        all_cont, all_neg = small[:, 0, 16:17], small[:, 0, 17:18]
        carry_row = onehot[:, 1:4, :].rearrange("p a f -> p (a f)")

        s_const = sem("s_const")
        s_edges = sem("s_edges")
        s_x = sem("s_x")
        s_pad = sem("s_pad")
        s_w = ring("s_w", 4)
        s_wdone = ring("s_wdone", 3)
        s_dve = sem("s_dve")
        s_act = sem("s_act")
        s_pe0 = sem("s_pe0")
        s_ask0 = sem("s_ask0")
        s_idle = sem("s_idle")
        s_idleA = sem("s_idleA")
        s_tab = ring("s_tab", 4)
        s_h = ring("s_h", 4)
        s_st = sem("s_st")
        s_sd = sem("s_sd")
        s_nm = sem("s_nm")
        s_out = sem("s_out")

        s_ones0 = sem("s_ones0")
        s_tables = sem("s_tables")
        s_oh8 = sem("s_oh8")
        s_hist = sem("s_hist")
        s_ahead = sem("s_ahead")
        s_placed = sem("s_placed")
        s_bns = sem("s_bns")
        s_idx = sem("s_idx")
        s_row = ring("s_row", U)
        s_t, s_tc, s_p = sem("s_t"), sem("s_tc"), sem("s_p")
        s_m0, s_r0, s_e0, s_e0c = (sem(n) for n in ("s_m0", "s_r0", "s_e0", "s_e0c"))
        s_oh0, s_seg0, s_acc0 = sem("s_oh0"), sem("s_seg0"), sem("s_acc0")
        s_diff, s_diffa = sem("s_diff"), sem("s_diffa")
        s_xnew = ring("s_xnew", 4)
        s_put, s_put1 = sem("s_put"), sem("s_put1")
        s_fold, s_folded = sem("s_fold"), sem("s_folded")
        s_p1a, s_p1c = sem("s_p1a"), sem("s_p1c")
        s_edge = ring("s_edge", 2)
        s_oh1 = sem("s_oh1")
        s_turn, s_turnedc = sem("s_turn"), sem("s_turnedc")
        s_pre = sem("s_pre")
        s_sum1 = sem("s_sum1")
        s_ln = sem("s_ln")
        s_msg = sem("s_msg")
        s_sent = ring("s_sent", 2)
        s_oh1s, s_seg1, s_acc1, s_took = (sem(n) for n in ("s_oh1s", "s_seg1", "s_acc1", "s_took"))
        s_node1 = sem("s_node1")
        s_u1, s_u1c, s_u2, s_zin, s_zl, s_z1, s_u3, s_u3c, s_u4, s_u4c = (
            sem(n) for n in ("s_u1", "s_u1c", "s_u2", "s_zin", "s_zl", "s_z1", "s_u3", "s_u3c", "s_u4", "s_u4c"))
        s_bn, s_bnsum, s_bnsd = sem("s_bn"), sem("s_bnsum"), sem("s_bnsd")
        s_store2 = sem("s_store2")
        s_sc2 = sem("s_sc2")
        s_fold2, s_folded2 = sem("s_fold2"), sem("s_folded2")
        s_p2c = sem("s_p2c")
        s_mx, s_mxt, s_mnew, s_mbc, s_negm = (sem(n) for n in ("s_mx", "s_mxt", "s_mnew", "s_mbc", "s_negm"))
        s_wgt, s_oh2, s_seg2, s_acc2 = (sem(n) for n in ("s_wgt", "s_oh2", "s_seg2", "s_acc2"))
        s_scaled, s_hmax = sem("s_scaled"), sem("s_hmax")
        s_fin2, s_fin2a = sem("s_fin2"), sem("s_fin2a")
        s_scanfree, s_scan, s_prev = (sem(n) for n in ("s_scanfree", "s_scan", "s_prev"))
        s_folded3, s_p3c = sem("s_folded3"), sem("s_p3c")
        s_cum, s_cump, s_got3, s_carry, s_carryp = (sem(n) for n in ("s_cum", "s_cump", "s_got3", "s_carry", "s_carryp"))
        s_scanned, s_segmax, s_mxnode, s_zero, s_fill, s_fillz, s_filled, s_fillback = (
            sem(n) for n in ("s_scanned", "s_segmax", "s_mxnode", "s_zero", "s_fill", "s_fillz", "s_filled",
                             "s_fillback"))
        s_alpha, s_alphae, s_segsum, s_sumnode = (sem(n) for n in ("s_alpha", "s_alphae", "s_segsum", "s_sumnode"))

        block = ctx.enter_context(nc.Block())

        def spread(col, n, w=D):
            return col.unsqueeze(2).to_broadcast([P, n, w])

        def over(row, n):
            return row.unsqueeze(1).to_broadcast([P, n, D])

        def message_rows(eng, kind, i, h):
            _, places = nc.values_load_multi_w_load_instructions(
                regs[96:97, bass.ds(R * i + h * H, H)], engines=[kind], min_val=0, max_val=LASTBASE,
                skip_runtime_bounds_check_because=IN_RANGE)
            if not first(i):
                eng.wait_ge(s_seg1, 2 * i - 1 + h)
                eng.wait_ge(s_took, 2 * i - 1 + h)
            for q in range(H):
                eng.dma_start(rows[:, h * H + q, :], messages[bass.ds(places[q], P), :]).then_inc(s_edge[h], 16)

        @block.sync
        def _(sp):
            sp.wait_ge(s_pad, 3)
            for a, s in ((srcL, src), (dstL, dst)):
                sp.dma_start(a[:, 0:CH - 1, :], s[0:(CH - 1) * P * P].rearrange("(c t e) -> t c e", t=P, e=P)
                             ).then_inc(s_edges, 16)
                sp.dma_start(a[0:TILES - 1 - (CH - 1) * P, CH - 1, :],
                             s[(CH - 1) * P * P:(TILES - 1) * P].rearrange("(t e) -> t e", e=P)).then_inc(s_edges, 16)
                sp.dma_start(a[TILES - 1 - (CH - 1) * P:TILES - (CH - 1) * P, CH - 1, P - REST:P],
                             s[(TILES - 1) * P:E].rearrange("(t e) -> t e", t=1)).then_inc(s_edges, 16)
            sp.dma_start(X[:, 0:BLOCKS - 1, :], x[0:(BLOCKS - 1) * P, :].rearrange("(b j) f -> j b f", j=P)
                         ).then_inc(s_x, 16)
            sp.dma_start(X[0:TAIL, BLOCKS - 1, :], x[(BLOCKS - 1) * P:N, :]).then_inc(s_x, 16)

            sp.wait_ge(s_h[0], NB)
            sp.dma_start(table0.rearrange("(b j) f -> j b f", j=P), Hn[:, :, :]).then_inc(s_tab[0], 16)
            sp.wait_ge(s_p1a, GROUPS)
            sp.dma_start(table1.rearrange("(b j) f -> j b f", j=P), Hn[:, :, :]).then_inc(s_tab[1], 16)
            sp.wait_ge(s_p1c, GROUPS)

            def edge_rows(i):
                for h in range(2):
                    if not first(i):
                        sp.wait_ge(s_turn, 2 * i - 1 + h)
                    for j in range(h * H, h * H + H):
                        at = sp.value_load(regs[32:33, bass.ds(R * i + j, 1)], min_val=0, max_val=LASTBASE)
                        sp.dma_start(edge[:, j, :], edge_attr_128[bass.ds(at, P), :]).then_inc(s_edge[h], 16)
            repeat(sp, ITERS, edge_rows)

            for h in range(2):
                sp.wait_ge(s_sent[h], landed(0, ITERS))
            sp.wait_ge(s_tables, 3)

            repeat(sp, ITERS, lambda i: message_rows(sp, mybir.EngineType.SP, i, 0))
            sp.wait_ge(s_store2, 1)
            sp.dma_start(table2.rearrange("(b j) f -> j b f", j=P), ACC[:, :, :]).then_inc(s_tab[2], 16)
            sp.dma_start(score2.rearrange("(b j) -> j b", j=P), small[:, 8, :],
                         allow_slow_non_contiguous=True).then_inc(s_sc2, 16)
            sp.wait_ge(s_sc2, 16)
            sp.dma_start(btw, score2.partition_broadcast(P)).then_inc(s_sc2, 16)
            sp.wait_ge(s_scanfree, 1)
            for a, s in ((scan_idx, src), (scan_dst, dst)):
                sp.dma_start(a[0:P - 1, 0:SC], s[0:(P - 1) * SC].rearrange("(p i) -> p i", i=SC)).then_inc(s_scan, 16)
                sp.dma_start(a[P - 1:P, 0:SREST], s[(P - 1) * SC:E].rearrange("(p i) -> p i", p=1)).then_inc(s_scan, 16)
            sp.dma_start(scan_prev[0:1, 1:SC], dst[0:SC - 1].rearrange("(p i) -> p i", p=1)).then_inc(s_prev, 16)
            sp.dma_start(scan_prev[1:P - 1, :], dst[SC - 1:(P - 1) * SC - 1].rearrange("(p i) -> p i", i=SC)
                         ).then_inc(s_prev, 16)
            sp.dma_start(scan_prev[P - 1:P, 0:SREST], dst[(P - 1) * SC - 1:E - 1].rearrange("(p i) -> p i", p=1)
                         ).then_inc(s_prev, 16)
            sp.wait_ge(s_p3c, GROUPS)
            sp.dma_start(table3.rearrange("(b j) f -> j b f", j=P), SN[:, :, 0:4]).then_inc(s_tab[3], 16)
            sp.wait_ge(s_zero, 1)
            sp.dma_start(seg_fill.rearrange("(p i) f -> p i f", i=SC), fill).then_inc(s_fillz, 16)
            sp.wait_ge(s_scanned, 1)
            sp.dma_start(seg_max.rearrange("(p i) f -> p i f", i=SC), MX[:, :, :]).then_inc(s_segmax, 16)
            sp.wait_ge(s_filled, 16 * BLOCKS)
            sp.dma_start(fill, seg_fill.rearrange("(p i) f -> p i f", i=SC)).then_inc(s_fillback, 16)
            sp.wait_ge(s_scanned, 2)
            sp.dma_start(seg_sum.rearrange("(p i) f -> p i f", i=SC), MX[:, :, :]).then_inc(s_segsum, 16)
            sp.wait_ge(s_xnew[3], 1)
            sp.dma_start(out[0:(BLOCKS - 1) * P, :].rearrange("(b j) f -> j b f", j=P), X[:, 0:BLOCKS - 1, :]
                         ).then_inc(s_out, 16)
            sp.dma_start(out[(BLOCKS - 1) * P:N, :], X[0:TAIL, BLOCKS - 1, :]).then_inc(s_out, 16)
            sp.wait_ge(s_out, 32)

        @block.gpsimd
        def _(pool):
            idx_steps = Tally(pool, s_idx)
            nc.gpsimd.iota(tmpp.bitcast(I32), pattern=[[1, PAIRS]], base=0, channel_multiplier=0).then_inc(s_const, 1)
            nc.gpsimd.iota(count_i[:, :], pattern=[[0, 1]], base=0, channel_multiplier=1).then_inc(s_const, 1)
            nc.gpsimd.memset(X[:, :, :], 0.0).then_inc(s_pad, 1)

            def stage(ring_idx, table, at):
                pool.sem_inc(s_idle, 1)
                idx_steps(nc.gpsimd.tensor_copy(ring_idx, table[:, bass.ds(at, H)]))
                idx_steps.wait()
                pool.sem_inc(s_idle, 1)

            def gather(table, i, h, idx_table, k, used, width, rings=(rows,)):
                n = 2 * len(rings)
                if not first(i):
                    pool.wait_ge(s_row[h], landed(k, i, h))
                    pool.wait_ge(used, n * i - n + 1 + h)
                stage(idxs[:, h * H:h * H + H], idx_table, n * H * i + h * H)
                for j in range(h * H, h * H + H):
                    nc.gpsimd.indirect_dma_start(rings[h // 2][:, j % R, 0:width], None, table[:, :],
                                                 bass.IndirectOffsetOnAxis(idxs[:, j:j + 1], 0)
                                                 ).then_inc(s_row[h], 16)

            pool.wait_ge(s_tables, 1)
            pool.wait_ge(s_tab[0], 16)

            def sum0(i):
                for h in range(2):
                    gather(table0, i, h, src_idx, 0, s_seg0, D)
            repeat(pool, ITERS, sum0, idx_steps)

            pool.wait_ge(s_tables, 2)
            pool.wait_ge(s_tab[1], 16)

            def scatter(i, h):
                pool.wait_ge(s_msg, 2 * i + h + 1)
                if not first(i):
                    pool.wait_ge(s_sent[h], landed(0, i))
                stage(pidx[:, h * H:h * H + H], pos_idx, R * i + h * H)
                for j in range(h * H, h * H + H):
                    nc.gpsimd.indirect_dma_start(messages[:, :], bass.IndirectOffsetOnAxis(pidx[:, j:j + 1], 0),
                                                 mrow[:, j, :], None, bounds_check=E - 1, oob_is_err=False
                                                 ).then_inc(s_sent[h], 16)

            def edges(i):
                gather(table1, i, 0, src_idx, 1, s_msg, D)
                if not first(i):
                    scatter(i - 1, 1)
                gather(table1, i, 1, src_idx, 1, s_msg, D)
                scatter(i, 0)
            repeat(pool, ITERS, edges, idx_steps, peel=2)
            scatter(ITERS - 1, 1)

            pool.wait_ge(s_tables, 4)
            pool.wait_ge(s_tab[2], 16)

            def attend(i):
                for u in range(U):
                    gather(table2, i, u, dst_idx, 2, s_seg2, 130, (rows, mrow))
            repeat(pool, ITERS2, attend, idx_steps)

            pool.wait_ge(s_scan, 64)
            pool.wait_ge(s_tab[3], 16)

            def scores(i):
                for h in range(2):
                    gather(table3, i, h, scan_idx, 3, s_got3, 4, (g4,))
            repeat(pool, SG // R, scores, idx_steps)

            pool.wait_ge(s_segmax, 16)
            for b in range(BLOCKS):
                nc.gpsimd.indirect_dma_start(mx_node[:, b, :], None, seg_max[:, :],
                                             bass.IndirectOffsetOnAxis(end_idx[:, b:b + 1], 0)
                                             ).then_inc(s_mxnode, 16)
            pool.wait_ge(s_fill, 1)
            pool.wait_ge(s_fillz, 16)
            for b in range(BLOCKS):
                nc.gpsimd.indirect_dma_start(seg_fill[:, :], bass.IndirectOffsetOnAxis(start_idx[:, b:b + 1], 0),
                                             fill_node[:, b, :], None, bounds_check=E - 1, oob_is_err=False
                                             ).then_inc(s_filled, 16)
            pool.wait_ge(s_segsum, 16)
            for b in range(BLOCKS):
                nc.gpsimd.indirect_dma_start(sum_node[:, b, :], None, seg_sum[:, :],
                                             bass.IndirectOffsetOnAxis(end_idx[:, b:b + 1], 0)
                                             ).then_inc(s_sumnode, 16)

        @block.tensor
        def _(pe):
            def turn7(a, order):
                pe.wait_ge(s_ask0, order)
                for c in range(CH):
                    last = nc.tensor.transpose(PS[c // 4][:, c % 4 * P:c % 4 * P + P], a[:, c, :], ident[:, :])
                last.then_inc(s_pe0, 1)

            def count_below(order):
                pe.wait_ge(s_ask0, order)
                for half in range(2):
                    for c in range(CH):
                        last = nc.tensor.matmul(PS[2 + half][:, 0:HP], onesb[:, :], gbf[:, c, half * HP:half * HP + HP],
                                                start=(c == 0), stop=(c == CH - 1))
                last.then_inc(s_pe0, 1)

            def pick(a, order):
                pe.wait_ge(s_ask0, order)
                for half in range(2):
                    for c in range(CH):
                        last = nc.tensor.matmul(PS[2 + half][:, 0:HP], a[:, c, :], sel[:, c, half * HP:half * HP + HP],
                                                start=(c == 0), stop=(c == CH - 1))
                last.then_inc(s_pe0, 1)

            turn7(hiF, 1)
            count_below(2)
            pick(dstF, 3)
            pick(srcF, 4)

            def histogram(i):
                for q in range(2):
                    pe.wait_ge(s_oh8, 2 * i + q + 1)
                    nc.tensor.matmul(PS[4][:, 0:HB * BLOCKS], onesb[:, :], oh8[q], start=first(i) and q == 0,
                                     stop=False, skip_group_check=True).then_inc(s_hist, 1)
            repeat(pe, STEPS // 2, histogram)

            def turn_group(a, to):
                for q in range(4):
                    last = nc.tensor.transpose(to[:, q * P:q * P + P], a[:, q * P:q * P + P], ident[:, :])
                return last

            pe.wait_ge(s_w[0], 16 * 6)

            def mlp0(i):
                pe.wait_ge(s_put, i + 1)
                turn_group(group, PS[7]).then_inc(s_t, 1)
                pe.wait_ge(s_tc, i + 1)
                nc.tensor.matmul(PS[6][0:64, :], W0_1, hT, start=True, stop=True).then_inc(s_m0, 1)
                pe.wait_ge(s_r0, i + 1)
                if not first(i):
                    pe.wait_ge(s_e0c, i)
                for q in range(4):
                    last = nc.tensor.matmul(PS[5][:, q * P:q * P + P], rT[0:65, q * P:q * P + P], W0_2,
                                            start=True, stop=True)
                last.then_inc(s_e0, 1)
            repeat(pe, GROUPS, mlp0)

            def segment(i, h, oh_ready, row_ready, row_count, used, done):
                pe.wait_ge(oh_ready, 2 * i + h + 1)
                pe.wait_ge(row_ready[h], row_count)
                if not first(i):
                    pe.wait_ge(used, 2 * i - 1 + h)
                for q in range(H):
                    last = nc.tensor.matmul(seg_ps(h, q), onehot[:, h * H + q, :], rows[:, h * H + q, 0:129],
                                            start=True, stop=True)
                last.then_inc(done, 1)

            def place(i):
                pe.wait_ge(s_oh8, STEPS + i + 1)
                if not first(i):
                    pe.wait_ge(s_placed, i)
                ahead = PS[4][:, 0:R * BLOCKS].rearrange("p (t h) -> p t h", h=BLOCKS)
                nc.tensor.matmul(ahead, below[:, :], ohp, start=True, stop=False, skip_group_check=True)
                for t in range(R - 1):
                    nc.tensor.matmul(ahead[:, t + 1:R, :], onesb[:, :],
                                     ohp[:, t:t + 1, :].to_broadcast([P, R - 1 - t, BLOCKS]),
                                     start=False, stop=(t == R - 2), skip_group_check=True)
                for t in range(R):
                    last = nc.tensor.matmul(PS[5][:, 0:BLOCKS], onesb[:, :], ohp[:, t, :], start=(t == 0),
                                            stop=(t == R - 1))
                last.then_inc(s_ahead, 1)

            def sum0(i):
                segment(i, 0, s_oh0, s_row, landed(0, i + 1), s_acc0, s_seg0)
                place(i)
                segment(i, 1, s_oh0, s_row, landed(0, i + 1), s_acc0, s_seg0)
            repeat(pe, ITERS, sum0)

            turn7(posT.rearrange("p (c e) -> p c e", e=P), 5)
            pick(posF, 6)
            count_below(7)

            pe.wait_ge(s_w[1], 16 * 13)
            nc.tensor.transpose(PS[7][:, 0:P], W1_2, ident[:, :]).then_inc(s_fold, 1)
            pe.wait_ge(s_folded, 1)
            nc.tensor.matmul(PS[6][:, 0:D], tw[:, 0:D], U1b, start=True, stop=True)
            nc.tensor.matmul(PS[6][:, D:2 * D], b1_2.to_broadcast([P, P]), U1b, start=True, stop=True
                             ).then_inc(s_fold, 1)
            pe.wait_ge(s_folded, 2)

            def project(k, i, weights, width, used):
                pe.wait_ge(s_put, GROUPS * k + i + 1)
                turn_group(group, PS[7]).then_inc(s_t, 1)
                pe.wait_ge(s_tc, GROUPS * k + i + 1)
                if not first(i):
                    pe.wait_ge(used, i)
                for q in range(4):
                    last = nc.tensor.matmul(PS[2 + q][:, 0:width], hT[:, q * P:q * P + P], weights,
                                            start=True, stop=True)
                last.then_inc(s_p, 1)
            repeat(pe, GROUPS, lambda i: project(1, i, W1abu.rearrange("p a f -> p (a f)"), 3 * D, s_p1c))

            def edges(i):
                for (_, h), before in halves(i):
                    _, blocks = nc.values_load_multi_w_load_instructions(
                        regs[0:1, bass.ds(R * i + h * H, H)], engines=[mybir.EngineType.PE], min_val=0,
                        max_val=BLOCKS - 1, skip_runtime_bounds_check_because=IN_RANGE)
                    pe.wait_ge(s_oh1, 2 * i + h + 1)
                    pe.wait_ge(s_edge[h], landed(0, i + 1))
                    if before:
                        pe.wait_ge(s_turnedc, 2 * i + h)
                    for q in range(H):
                        nc.tensor.transpose(turn_ps(q)[:, 0:P], onehot[:, h * H + q, :], ident[:, :])
                        last = nc.tensor.transpose(turn_ps(q)[:, P:2 * P], edge[:, h * H + q, :], ident[:, :])
                    last.then_inc(s_turn, 1)
                    pe.wait_ge(s_turnedc, 2 * i + h + 1)
                    if not first(i):
                        pe.wait_ge(s_sum1, 2 * i - 1 + h)
                    for q in range(H):
                        nc.tensor.matmul(pre_ps(h, q), turned[:, q, 1, :], W1c, start=True, stop=False)
                        last = nc.tensor.matmul(pre_ps(h, q), turned[:, q, 0, :],
                                                BT[:, bass.ds(blocks[q], 1), :].rearrange("p a f -> p (a f)"),
                                                start=False, stop=True)
                    last.then_inc(s_pre, 1)
            repeat(pe, ITERS, edges)

            def sum1(i):
                for h in range(2):
                    segment(i, h, s_oh1s, s_edge, landed(1, i + 1), s_acc1, s_seg1)
            repeat(pe, ITERS, sum1)

            pe.wait_ge(s_node1, 1)

            def update(i):
                pe.wait_ge(s_put1, i + 1)
                turn_group(group, PS[7]).then_inc(s_u1, 1)
                pe.wait_ge(s_u1c, i + 1)
                for q in range(4):
                    last = nc.tensor.matmul(PS[6][:, q * P:q * P + P], hT[:, q * P:q * P + P], W2U, start=True, stop=True)
                last.then_inc(s_u2, 1)
                pe.wait_ge(s_z1, i + 1)
                turn_group(zgroup, PS[5]).then_inc(s_u3, 1)
                pe.wait_ge(s_u3c, i + 1)
                for q in range(4):
                    last = nc.tensor.matmul(PS[4][:, q * P:q * P + P], rT[:, q * P:q * P + P], U2w, start=True, stop=True)
                last.then_inc(s_u4, 1)
                pe.wait_ge(s_u4c, i + 1)
            repeat(pe, GROUPS, update)
            for k in range(2):
                pe.wait_ge(s_bn, k + 1)
                nc.tensor.matmul(PS[0][:, 0:D], ones[:, :], lnp[:, 0, :], start=True, stop=True).then_inc(s_bnsum, 1)

            pe.wait_ge(s_w[2], 48)
            nc.tensor.transpose(PS[7][:, 0:P], WA[:, 0, :], ident[:, :]).then_inc(s_fold2, 1)
            pe.wait_ge(s_folded2, 1)
            nc.tensor.matmul(PS[6][:, 0:2], tw[:, 0:D], WA[:, 3, 0:2], start=True, stop=True).then_inc(s_fold2, 1)
            pe.wait_ge(s_folded2, 2)
            waf = WA[:, :, :].rearrange("p a f -> p (a f)")
            repeat(pe, GROUPS, lambda i: project(2, i, waf[:, 0:130], 130, s_p2c))

            def weigh(i, u):
                n, h, ring_of = U * i + u, u % 2, (rows, mrow)[u // 2]
                pe.wait_ge(s_oh2, n + 1)
                pe.wait_ge(s_scaled, n + 1)
                if not (first(i) and u < 2):
                    pe.wait_ge(s_acc2, n - 1)
                for q in range(H):
                    last = nc.tensor.matmul(seg_ps(h, q), onehot[:, h * H + q, :], ring_of[:, h * H + q, 0:129],
                                            start=True, stop=True)
                last.then_inc(s_seg2, 1)

            def attend(i):
                for u in range(U):
                    n, h = U * i + u, u % 2
                    pe.wait_ge(s_mx, n + 1)
                    if not (first(i) and u == 0):
                        pe.wait_ge(s_negm, n)
                    nc.tensor.transpose(PS[6][0:1, 0:P], lm[:, 1 - h, H:H + 1], ident[:, :]).then_inc(s_mxt, 1)
                    if u:
                        weigh(i, u - 1)
                    elif not first(i):
                        weigh(i - 1, U - 1)
                    pe.wait_ge(s_mnew, n + 1)
                    nc.tensor.matmul(PS[6][:, 256:257], ones[0:1, :], m_run[0:1, h:h + 1], start=True, stop=True
                                     ).then_inc(s_mbc, 1)
            repeat(pe, ITERS2, attend)
            weigh(ITERS2 - 1, U - 1)

            pe.wait_ge(s_folded3, 1)
            repeat(pe, GROUPS, lambda i: project(3, i, waf[:, 0:136], 136, s_p3c))
            pe.wait_ge(s_cum, 1)
            nc.tensor.matmul(PS[6][:, 0:BLOCKS], upto, cnt_dst[:, 0:BLOCKS], start=True, stop=True)
            nc.tensor.matmul(PS[6][:, 64:64 + BLOCKS], ones[:, :], cnt_dst[:, 0:BLOCKS], start=True, stop=True
                             ).then_inc(s_cump, 1)
            for k, w in enumerate((4, 8, 4)):
                pe.wait_ge(s_carry, 2 * k + 1)
                nc.tensor.transpose(PS[5][0:w, 0:P], last_v[:, 0:w], ident[:, :])
                nc.tensor.transpose(PS[5][0:w, P:2 * P], last_c[:, 0:w], ident[:, :]).then_inc(s_carryp, 1)
                pe.wait_ge(s_carry, 2 * k + 2)
                nc.tensor.transpose(PS[5][:, 256:256 + w], carry_row[0:w, 0:P], ident[0:w, 0:w]).then_inc(s_carryp, 1)

        @block.scalar
        def _(act):
            done = Tally(act, s_act)

            def step(ins):
                done(ins)
                done.wait()

            def norm_h(k, after):
                act.wait_ge(s_st, after)
                nc.scalar.activation(small[:, 2, :], small[:, 1, :], ACT.Sqrt).then_inc(s_sd, 1)
                act.wait_ge(s_nm, k + 1)
                if k:
                    act.wait_ge(s_tab[k - 1], 16)
                act.sem_inc(s_idleA, 1)
                with act.Fori(0, NB) as b:
                    nc.scalar.activation(Hn[:, bass.ds(b, 1), :].rearrange("p a f -> p (a f)"),
                                         X[:, bass.ds(b, 1), :].rearrange("p a f -> p (a f)"), ACT.Relu,
                                         bias=small[:, 4, bass.ds(b, 1)], scale=small[:, 3, bass.ds(b, 1)]
                                         ).then_inc(s_h[k], 1)

            def load(dest, source, k):
                act.dma_start(dest, source).then_inc(s_w[k], 16)

            def row(v):
                return v.partition_broadcast(P)

            load(W0_1, L0_gnn_W1, 0)
            load(WA[0:64, 1, :], L0_gnn_W2, 0)
            load(WA[64:65, 1, :], L0_gnn_b2.rearrange("(a f) -> a f", a=1), 0)
            load(b0_1, L0_gnn_b1.rearrange("(f a) -> f a", a=1), 0)
            load(g0, row(L0_gnn_gamma), 0)
            load(be0, row(L0_gnn_beta), 0)

            norm_h(0, 1)

            def mlp0(i):
                act.wait_ge(s_t, i + 1)
                nc.scalar.activation(hT, PS[7][:, :], ACT.Copy).then_inc(s_tc, 1)
                act.wait_ge(s_m0, i + 1)
                if not first(i):
                    act.wait_ge(s_e0, i)
                nc.scalar.activation(rT[0:64, :], PS[6][0:64, :], ACT.Relu, bias=b0_1).then_inc(s_r0, 1)
            act.wait_ge(s_w[0], 96)
            act.wait_ge(s_ones0, 1)
            repeat(act, GROUPS, mlp0)

            act.wait_ge(s_diff, 1)
            nc.scalar.activation(ACC[:, :, 0:D], ACC[:, :, 0:D], ACT.Square).then_inc(s_diffa, 1)
            act.wait_ge(s_diff, 2)
            step(nc.scalar.activation(small[:, 5, :], small[:, 5, :], ACT.Sqrt))
            nc.scalar.activation(small[:, 5, :], small[:, 5, :], ACT.Tanh).then_inc(s_diffa, 1)
            act.wait_ge(s_st, 2)
            nc.scalar.activation(small[:, 2, :], small[:, 1, :], ACT.Sqrt).then_inc(s_sd, 1)

            act.wait_ge(s_wdone[0], 1)
            for k in range(3):
                load(WA[:, k, :], (L1_gnn_W1[0:D, :], L1_gnn_W1[D:2 * D, :], L1_gnn_U1[0:D, :])[k], 1)
            load(W1c, L1_gnn_W1[2 * D:3 * D, :], 1)
            load(b1bc, row(L1_gnn_b1), 1)
            load(ub1bc, row(L1_gnn_ub1), 1)
            load(W1_2, L1_gnn_W2, 1)
            load(U1b, L1_gnn_U1[D:2 * D, :], 1)
            load(U2w, L1_gnn_U2, 1)
            load(ub2bc, row(L1_gnn_ub2), 1)
            load(g1, row(L1_gnn_gamma), 1)
            load(be1, row(L1_gnn_beta), 1)
            load(b1_2, L1_gnn_b2.rearrange("(f a) -> f a", a=1), 1)
            norm_h(1, 3)
            act.wait_ge(s_fold, 1)
            nc.scalar.activation(tw[:, 0:D], PS[7][:, 0:D], ACT.Copy).then_inc(s_folded, 1)
            act.wait_ge(s_fold, 2)
            nc.scalar.activation(WA[:, 12:14, :].rearrange("p a f -> p (a f)"), PS[6][:, 0:2 * D], ACT.Copy
                                 ).then_inc(s_folded, 1)

            def project1(i):
                act.wait_ge(s_t, GROUPS * 1 + i + 1)
                nc.scalar.activation(hT, PS[7][:, :], ACT.Copy).then_inc(s_tc, 1)
                act.wait_ge(s_p, i + 1)
                act.sem_inc(s_idleA, 1)
                for q in range(4):
                    last = nc.scalar.activation(Hn[:, bass.ds(4 * i + q, 1), :].rearrange("p a f -> p (a f)"),
                                                PS[2 + q][:, 0:D], ACT.Copy)
                last.then_inc(s_p1a, 1)
            repeat(act, GROUPS, project1)

            def softplus_tail(v):
                o = lnp[:, 0:v.shape[1], :]
                step(nc.scalar.activation(o, v, ACT.Abs))
                step(nc.scalar.activation(o, o, ACT.Exp, scale=-1.0))
                return nc.scalar.activation(o, o, ACT.Ln, bias=1.0)

            nc.scalar.preload_act_table_set("natural_log_exp_and_others")

            def edges(i):
                for h in range(2):
                    act.wait_ge(s_turn, 2 * i + h + 1)
                    if not (first(i) and h == 0):
                        act.wait_ge(s_pre, 2 * i + h)
                    for bank, n in enumerate((512, 512, 256)):
                        last = nc.scalar.activation(tw[:, 512 * bank:512 * bank + n], PS[bank][:, 0:n], ACT.Copy)
                    last.then_inc(s_turnedc, 1)
                    act.wait_ge(s_sum1, 2 * i + h + 1)
                    if not (first(i) and h == 0):
                        act.wait_ge(s_msg, 2 * i + h)
                    softplus_tail(rows[:, h * H:h * H + H, 0:D]).then_inc(s_ln, 1)
            repeat(act, ITERS, edges, done)

            for h in range(2):
                act.wait_ge(s_sent[h], landed(0, ITERS))
            act.wait_ge(s_tables, 3)
            repeat(act, ITERS, lambda i: message_rows(act, mybir.EngineType.Activation, i, 1))
            nc.scalar.preload_act_table_set("natural_log_exp_and_others")

            def update(i):
                act.wait_ge(s_u1, i + 1)
                nc.scalar.activation(hT, PS[7][:, :], ACT.Copy).then_inc(s_u1c, 1)
                act.wait_ge(s_zin, i + 1)
                act.sem_inc(s_idleA, 1)
                softplus_tail(CT[:, bass.ds(4 * i, 4), :]).then_inc(s_zl, 1)
                act.wait_ge(s_u3, i + 1)
                nc.scalar.activation(rT, PS[5][:, :], ACT.Copy).then_inc(s_u3c, 1)
            repeat(act, GROUPS, update, done)
            act.wait_ge(s_bn, 3)
            nc.scalar.activation(lnp[:, 1, :], lnp[:, 1, :], ACT.Sqrt).then_inc(s_bnsd, 1)

            act.wait_ge(s_wdone[1], 1)
            load(WA[:, 0, :], L2_gnn_W, 2)
            for k in range(2):
                load(WA[:, 3, k:k + 1], L2_gnn_attn[0, k * D:(k + 1) * D].rearrange("(f a) -> f a", a=1), 2)
            norm_h(2, 4)
            act.wait_ge(s_fold2, 1)
            nc.scalar.activation(tw[:, 0:D], PS[7][:, 0:D], ACT.Copy).then_inc(s_folded2, 1)
            act.wait_ge(s_fold2, 2)
            nc.scalar.activation(WA[:, 1, 0:2], PS[6][:, 0:2], ACT.Copy).then_inc(s_folded2, 1)

            def project2(i):
                act.wait_ge(s_t, GROUPS * 2 + i + 1)
                nc.scalar.activation(hT, PS[7][:, :], ACT.Copy).then_inc(s_tc, 1)
                act.wait_ge(s_p, GROUPS * 1 + i + 1)
                act.sem_inc(s_idleA, 1)
                for q in range(4):
                    last = nc.scalar.activation(ACC[:, bass.ds(4 * i + q, 1), :].rearrange("p a f -> p (a f)"),
                                                PS[2 + q][:, 0:130], ACT.Copy)
                last.then_inc(s_p2c, 1)
            repeat(act, GROUPS, project2)

            nc.scalar.preload_act_table_set("natural_log_exp_and_others")

            def attend(i):
                for u in range(U):
                    n, h, ring_of = U * i + u, u % 2, (rows, mrow)[u // 2]
                    act.wait_ge(s_mbc, n + 1)
                    nc.scalar.activation(m_all[:, h:h + 1], PS[6][:, 256:257], ACT.Copy)
                    nc.scalar.activation(negm[:, h:h + 1], PS[6][:, 256:257], ACT.Copy, scale=-1.0).then_inc(s_negm, 1)
                    act.wait_ge(s_negm, n + 1)
                    nc.scalar.activation(fade[:, h:h + 1], m_all[:, 1 - h:2 - h], ACT.Exp, bias=negm[:, h:h + 1])
                    nc.scalar.activation(wgt[:, h * H:h * H + H], lm[:, h, 0:H], ACT.Exp,
                                         bias=negm[:, h:h + 1]).then_inc(s_wgt, 1)
                    act.wait_ge(s_wgt, n + 1)
                    for j in range(h * H, h * H + H):
                        last = nc.scalar.activation(ring_of[:, j, 0:129], ring_of[:, j, 0:129], ACT.Copy,
                                                    scale=wgt[:, j:j + 1])
                    last.then_inc(s_scaled, 1)
                    nc.scalar.activation(history[:, bass.ds(n, 1)], m_all[:, h:h + 1], ACT.Copy).then_inc(s_hmax, 1)
            repeat(act, ITERS2, attend)
            act.wait_ge(s_fin2, 1)
            nc.scalar.activation(small[:, 6, :], small[:, 6, :], ACT.Exp).then_inc(s_fin2a, 1)
            act.wait_ge(s_fin2, 2)
            nc.scalar.activation(BT[:, :, :], BT[:, :, :], ACT.Exp).then_inc(s_fin2a, 1)

            act.wait_ge(s_wdone[2], 1)
            load(WA[:, 0, :], L3_gnn_weight, 3)
            for k in range(2):
                load(WA[:, 2 + k, :].rearrange("p (h c) -> p h c", h=4),
                     L3_gnn_att[0, :, 32 * k:32 * k + 32].partition_broadcast(P), 3)
            norm_h(3, 5)

            def project3(i):
                act.wait_ge(s_t, GROUPS * 3 + i + 1)
                nc.scalar.activation(hT, PS[7][:, :], ACT.Copy).then_inc(s_tc, 1)
                act.wait_ge(s_p, GROUPS * 2 + i + 1)
                act.sem_inc(s_idleA, 1)
                for q in range(4):
                    nc.scalar.activation(BT[:, bass.ds(4 * i + q, 1), :].rearrange("p a f -> p (a f)"),
                                         PS[2 + q][:, 0:D], ACT.Copy)
                    last = nc.scalar.activation(SN[:, bass.ds(4 * i + q, 1), :].rearrange("p a f -> p (a f)"),
                                                PS[2 + q][:, D:D + 8], ACT.Copy)
                last.then_inc(s_p3c, 1)
            repeat(act, GROUPS, project3)
            act.wait_ge(s_alpha, 1)
            nc.scalar.activation(SI[:, 0:SC, :], SI[:, 0:SC, :], ACT.Exp).then_inc(s_alphae, 1)

        @block.vector
        def _(dve):
            done = Tally(dve, s_dve)

            def step(ins):
                done(ins)
                done.wait()

            v = nc.vector

            v.memset(accw[:, 0:1792].bitcast(I32), 0)
            v.memset(edge_flat[:, 0:896], 0.0)
            step(v.memset(accw[:, 1792:6760], 0.0))
            v.memset(srcL[:, CH - 1, :], NOKEY).then_inc(s_pad, 1)
            v.memset(dstL[:, CH - 1, :], NOKEY).then_inc(s_pad, 1)
            v.memset(ones[:, :], 1.0)
            v.memset(onesb[:, :], 1.0)
            v.memset(rT[64:65, :], 1.0).then_inc(s_ones0, 1)
            dve.wait_ge(s_const, 2)
            v.tensor_copy(iota[:, :], tmpp.bitcast(I32))
            step(v.tensor_copy(lane[:, :], count_i[:, :]))
            v.tensor_scalar(ident[:, :], iota[:, 0:P], lane[:, 0:1], None, ALU.is_equal)
            v.tensor_scalar(below[:, :], iota[:, 0:P], lane[:, 0:1], None, ALU.is_gt)
            for c in range(CH):
                step(v.tensor_scalar(lanes[:, c:c + 1], lane[:, :], float(c * P), None, ALU.add))

            dve.wait_ge(s_edges, 96)
            v.tensor_copy(srcF[:, :, :], srcL[:, :, :])
            v.tensor_copy(dstF[:, :, :], dstL[:, :, :])
            v.tensor_scalar(last_i, dstL[:, :, P - 1], 7, None, ALU.logical_shift_right)
            step(v.tensor_scalar(srcL, srcL, 7, None, ALU.logical_shift_right))
            v.tensor_copy(last_b, last_i)
            step(v.tensor_copy(hiF, srcL))
            v.tensor_tensor(rise, last_b, lanes[:, :], ALU.add).then_inc(s_ask0, 1)
            dve.wait_ge(s_pe0, 1)
            v.tensor_copy(hiT[:, 0:512], PS[0][:, :])
            step(v.tensor_copy(hiT[:, 512:896], PS[1][:, 0:384]))

            def pairs(pe_count, order):
                for c in range(CH):
                    step(v.tensor_scalar(gbf[:, c, :], iota[:, :], rise[:, c:c + 1], None, ALU.is_gt))
                v.memset(junk_hi[:, 0:1], 0.0).then_inc(s_ask0, 1)
                dve.wait_ge(s_pe0, pe_count)
                for half in range(2):
                    step(v.tensor_scalar(kpair[:, half * HP:half * HP + HP], PS[2 + half][:, 0:HP],
                                         float(TILES - 1), None, ALU.min))
                step(v.tensor_tensor(bpair, iota[:, :], kpair, ALU.subtract))
                step(v.tensor_copy(regs[order:order + 1, 0:PAIRS], bpair[order:order + 1, :]))
                step(v.tensor_scalar(tmpp, kpair, float(P), float(LASTBASE), ALU.mult, ALU.min))
                step(v.tensor_copy(regs[order + 32:order + 33, 0:PAIRS], tmpp[order + 32:order + 33, :]))

            pairs(2, 0)
            for c in range(CH):
                last = v.tensor_scalar(sel[:, c, :], kpair, lanes[:, c:c + 1], None, ALU.is_equal)
            last.then_inc(s_ask0, 1)
            dve.wait_ge(s_pe0, 3)
            for half in range(2):
                v.tensor_copy(pay[:, half * HP:half * HP + HP, 0], PS[2 + half][:, 0:HP])
            step(v.tensor_scalar(tmpp, bpair, float(P), None, ALU.mult))
            step(v.tensor_tensor(dst_rel[:, 0:PAIRS], pay[:, :, 0], tmpp, ALU.subtract))
            v.memset(junk_hi[:, 0:1], 0.0).then_inc(s_ask0, 1)
            dve.wait_ge(s_pe0, 4)
            for half in range(2):
                step(v.tensor_copy(pay[:, half * HP:half * HP + HP, 1], PS[2 + half][:, 0:HP]))
            v.tensor_scalar(src_idx[:, 0:PAIRS], pay[:, :, 1], float(N - 1), None, ALU.min).then_inc(s_tables, 1)

            def block_rows(to, at, n):
                v.tensor_tensor(to, iota[:, 0:BLOCKS].unsqueeze(1).to_broadcast([P, n, BLOCKS]),
                                hiT[:, bass.ds(at, n)].unsqueeze(2).to_broadcast([P, n, BLOCKS]),
                                ALU.is_equal).then_inc(s_oh8, 1)

            def histogram(i):
                for q in range(2):
                    if not first(i):
                        dve.wait_ge(s_hist, 2 * i + q - 1)
                    block_rows(oh8[q], HB * (2 * i + q), HB)
            repeat(dve, STEPS // 2, histogram)
            dve.wait_ge(s_hist, STEPS)
            step(v.tensor_reduce(cnt_hi, PS[4][:, 0:HB * BLOCKS].rearrange("p (t h) -> p h t", h=BLOCKS), AX, ALU.add))
            step(v.memset(junk_hi, 1.0))
            step(v.tensor_tensor_scan(cum_hi, junk_hi, cnt_hi, 0.0, ALU.mult, ALU.add))
            step(v.tensor_tensor(base_hi, cum_hi, cnt_hi, ALU.subtract))

            def stats(A, after):
                with dve.Fori(0, GROUPS) as g:
                    for q in range(4):
                        v.bn_stats(st[:, bass.ds(4 * g + q, 1), :].rearrange("p a f -> p (a f)"),
                                   A[:, bass.ds(4 * g + q, 1), :].rearrange("p a f -> p (a f)")).then_inc(s_bns, 1)
                dve.wait_ge(s_bns, NB * after)
                v.tensor_tensor(small[:, 0, :], st[:, :, 1], st[:, :, 4], ALU.add)
                v.tensor_tensor(small[:, 1, :], st[:, :, 2], st[:, :, 5], ALU.add)
                step(v.tensor_tensor(small[:, 2, :], st[:, :, 1], st[:, :, 4], ALU.subtract))
                step(v.tensor_tensor(small[:, 2, :], small[:, 2, :], small[:, 2, :], ALU.mult))
                v.tensor_scalar(small[:, 0, :], small[:, 0, :], 0.5, None, ALU.mult)
                step(v.tensor_scalar(small[:, 2, :], small[:, 2, :], 0.25, EPS, ALU.mult, ALU.add))
                v.scalar_tensor_tensor(small[:, 1, :], small[:, 1, :], 1.0 / D, small[:, 2, :], ALU.mult, ALU.add
                                       ).then_inc(s_st, 1)
                dve.wait_ge(s_sd, after)
                step(v.reciprocal(small[:, 3, :], small[:, 2, :]))
                step(v.scalar_tensor_tensor(small[:, 4, :], small[:, 0, :], -1.0, small[:, 3, :], ALU.mult, ALU.mult))

            def norm_ready():
                v.memset(small[:, 14, 0:1], 0.0).then_inc(s_nm, 1)

            dve.wait_ge(s_x, 32)
            stats(X, 1)
            norm_ready()

            def put(A, i, sem_put, turned_sem, k=0):
                if not first(i):
                    dve.wait_ge(turned_sem, GROUPS * k + i)
                v.tensor_scalar(group.rearrange("p (a f) -> p a f", a=4), A[:, bass.ds(4 * i, 4), 0:D], 1.0, None,
                                ALU.mult).then_inc(sem_put, 1)

            def mlp0(i):
                dve.wait_ge(s_h[0], 4 * i + 4)
                put(Hn, i, s_put, s_t)
                dve.wait_ge(s_e0, i + 1)
                v.tensor_scalar(BT[:, bass.ds(4 * i, 4), :].rearrange("p a f -> p (a f)"), PS[5][:, :], 0.2, None,
                                ALU.mult).then_inc(s_e0c, 1)
            repeat(dve, GROUPS, mlp0)

            v.memset(rows[:, :, D:ROW], 1.0)
            step(v.memset(ACC[:, :, :], 0.0))

            def block_numbers_at(at, reg_row=64):
                return nc.values_load_multi_w_load_instructions(
                    regs[reg_row:reg_row + 1, bass.ds(at, H)], engines=[mybir.EngineType.DVE],
                    min_val=0, max_val=BLOCKS - 1, skip_runtime_bounds_check_because=IN_RANGE)[1]

            def sum_blocks(i, h, seg, acc, reg_row):
                blocks = block_numbers_at(R * i + h * H, reg_row)
                dve.wait_ge(seg, 2 * i + h + 1)
                for q in range(H):
                    to = ACC[:, bass.ds(blocks[q], 1), 0:129].rearrange("p a f -> p (a f)")
                    last = v.tensor_tensor(to, to, seg_ps(h, q), ALU.add)
                    if q < H - 1:
                        step(last)
                last.then_inc(acc, 1)
                dve.wait_ge(acc, 2 * i + h + 1)

            def one_hots(h, keys, ready):
                v.tensor_tensor(onehot[:, h * H:h * H + H, :], iota[:, 0:P].unsqueeze(1).to_broadcast([P, H, P]),
                                keys.unsqueeze(2).to_broadcast([P, H, P]), ALU.is_equal).then_inc(ready, 1)

            def place(i):
                dve.wait_ge(s_ahead, i + 1)
                step(v.tensor_tensor(tpos, PS[4][:, 0:R * BLOCKS].rearrange("p (t h) -> p t h", h=BLOCKS),
                                     base_hi.unsqueeze(1).to_broadcast([P, R, BLOCKS]), ALU.add))
                done(v.tensor_tensor(base_hi, base_hi, PS[5][:, 0:BLOCKS], ALU.add))
                step(v.tensor_tensor(tpos, tpos, ohp, ALU.mult))
                v.tensor_reduce(posT[:, bass.ds(R * i, R)], tpos, AX, ALU.add).then_inc(s_placed, 1)
                dve.wait_ge(s_placed, i + 1)

            def sum0(i):
                block_rows(ohp, R * i, R)
                for (_, h), before in halves(i):
                    one_hots(h, dst_rel[:, bass.ds(R * i + h * H, H)], s_oh0)
                    if before:
                        sum_blocks(*before, s_seg0, s_acc0, 0)
                place(i)
            repeat(dve, ITERS, sum0, done, peel=2)
            sum_blocks(ITERS - 1, 1, s_seg0, s_acc0, 0)

            step(v.tensor_copy(cnt_dst, ACC[:, :, D]))
            step(v.tensor_scalar(small[:, 5, :], cnt_dst, 1.0, None, ALU.max))
            step(v.reciprocal(small[:, 5, :], small[:, 5, :]))
            step(v.tensor_tensor(ACC[:, :, 0:D], ACC[:, :, 0:D], spread(small[:, 5, :], NB), ALU.mult))
            v.tensor_tensor(ACC[:, :, 0:D], ACC[:, :, 0:D], Hn[:, :, :], ALU.subtract).then_inc(s_diff, 1)
            dve.wait_ge(s_diffa, 1)
            v.tensor_reduce(small[:, 5, :], ACC[:, :, 0:D], AX, ALU.add).then_inc(s_diff, 1)
            dve.wait_ge(s_diffa, 2)
            step(v.tensor_tensor(BT[:, :, :], BT[:, :, :], spread(small[:, 5, :], NB), ALU.mult))
            step(v.tensor_tensor(BT[:, :, :], BT[:, :, :], Hn[:, :, :], ALU.add))
            stats(BT, 2)
            step(v.tensor_tensor(BT[:, :, :], BT[:, :, :], spread(small[:, 3, :], NB), ALU.mult))
            step(v.tensor_tensor(BT[:, :, :], BT[:, :, :], spread(small[:, 4, :], NB), ALU.add))
            step(v.tensor_tensor(BT[:, :, :], BT[:, :, :], over(g0, NB), ALU.mult))
            step(v.tensor_tensor(BT[:, :, :], BT[:, :, :], over(be0, NB), ALU.add))
            step(v.tensor_tensor(X[:, :, :], X[:, :, :], BT[:, :, :], ALU.add))
            v.memset(small[:, 14, 0:1], 0.0).then_inc(s_wdone[0], 1)
            v.memset(small[:, 14, 1:2], 0.0).then_inc(s_xnew[0], 1)

            stats(X, 3)
            norm_ready()

            for c in range(CH):
                step(v.tensor_scalar(sel[:, c, :], kpair, lanes[:, c:c + 1], None, ALU.is_equal))
            v.memset(junk_hi[:, 0:1], 0.0).then_inc(s_ask0, 1)
            dve.wait_ge(s_pe0, 5)
            v.tensor_copy(posF[:, 0:4, :].rearrange("p c e -> p (c e)"), PS[0][:, :])
            v.tensor_copy(posF[:, 4:7, :].rearrange("p c e -> p (c e)"), PS[1][:, 0:384]).then_inc(s_ask0, 1)
            dve.wait_ge(s_pe0, 6)
            step(v.tensor_scalar(tmpp, dst_rel[:, 0:PAIRS], -1.0, None, ALU.is_gt))
            step(v.tensor_scalar(bpair, dst_rel[:, 0:PAIRS], float(P), None, ALU.is_lt))
            step(v.tensor_tensor(tmpp, tmpp, bpair, ALU.mult))
            step(v.tensor_scalar(bpair, tmpp, float(-NOWHERE), float(NOWHERE), ALU.mult, ALU.add))
            for half in range(2):
                part = slice(half * HP, half * HP + HP)
                step(v.tensor_tensor(tmpp[:, part], tmpp[:, part], PS[2 + half][:, 0:HP], ALU.mult))
            step(v.tensor_tensor(tmpp, tmpp, bpair, ALU.add))
            step(v.tensor_copy(pos_idx[:, 0:PAIRS], tmpp))
            v.memset(junk_hi[:, 0:1], 0.0).then_inc(s_tables, 1)

            for c in range(CH):
                step(v.tensor_scalar(xlast[:, c:c + 1], lanes[:, c:c + 1], float(P), float(P - 1), ALU.mult, ALU.add))
                step(v.tensor_scalar(junk_hi, cum_hi, xlast[:, c:c + 1], None, ALU.is_le))
                step(v.tensor_reduce(last_b[:, c:c + 1], junk_hi, AX, ALU.add))
            step(v.tensor_tensor(rise, last_b, lanes[:, :], ALU.add))
            pairs(7, 64)
            v.memset(first_block[:, 2 * ITERS:], BLOCKS - 1)
            v.tensor_copy(first_block[:, 0:2 * ITERS], bpair.rearrange("p (n q) -> p n q", q=H)[:, :, 0])
            step(v.tensor_scalar(tmpp, kpair, float(TILES - 1), None, ALU.is_equal))
            step(v.tensor_scalar(junk_hi[:, 0:1], lane[:, 0:1], float(P - REST), -30000.0, ALU.is_lt, ALU.mult))
            step(v.tensor_scalar(tmpp, tmpp, junk_hi[:, 0:1], None, ALU.mult))
            step(v.scalar_tensor_tensor(s_shift[:, :], bpair, float(P), tmpp, ALU.mult, ALU.add))

            step(v.memset(group[:, 0:1], 0.0))

            def project1(i):
                dve.wait_ge(s_h[1], 4 * i + 4)
                put(Hn, i, s_put, s_t, 1)
                dve.wait_ge(s_p1a, i + 1)
                for q in range(4):
                    at = bass.ds(4 * i + q, 1)
                    v.tensor_tensor(BT[:, at, :].rearrange("p a f -> p (a f)"), PS[2 + q][:, D:2 * D], b1bc, ALU.add)
                    last = v.tensor_tensor(CT[:, at, :].rearrange("p a f -> p (a f)"), PS[2 + q][:, 2 * D:3 * D], ub1bc,
                                           ALU.add)
                last.then_inc(s_p1c, 1)
            repeat(dve, GROUPS, project1)
            step(v.memset(mrow[:, :, D:ROW], 1.0))

            def edges(i):
                for (_, h), before in halves(i):
                    part = slice(h * H, h * H + H)
                    if before:
                        one_hots(h, dst_rel[:, bass.ds(R * i + h * H, H)], s_oh1)
                        messages_of(*before)
                    dve.wait_ge(s_row[h], landed(1, i + 1))
                    dve.wait_ge(s_pre, 2 * i + h + 1)
                    v.tensor_tensor(rows[:, h * H:h * H + 4, 0:D], rows[:, h * H:h * H + 4, 0:D],
                                    PS[3 + 2 * h][:, :].rearrange("p (q f) -> p q f", f=D), ALU.add)
                    v.tensor_tensor(rows[:, h * H + 4, 0:D], rows[:, h * H + 4, 0:D], pre_ps(h, 4), ALU.add
                                    ).then_inc(s_sum1, 1)

            def messages_of(i, h):
                part = slice(h * H, h * H + H)
                if not first(i):
                    dve.wait_ge(s_sent[h], landed(0, i))
                v.tensor_scalar(mrow[:, part, D + 1:D + 3], pay[:, bass.ds(R * i + h * H, H), :], 1.0, None, ALU.mult)
                dve.wait_ge(s_sum1, 2 * i + h + 1)
                dve.wait_ge(s_ln, 2 * i + h + 1)
                v.scalar_tensor_tensor(mrow[:, part, 0:D], rows[:, part, 0:D], 0.0, lnp[:, :, :], ALU.max, ALU.add
                                       ).then_inc(s_msg, 1)
            one_hots(0, dst_rel[:, 0:H], s_oh1)
            repeat(dve, ITERS, edges)
            messages_of(ITERS - 1, 1)

            dve.wait_ge(s_msg, 2 * ITERS)
            step(v.memset(ACC[:, :, :], 0.0))
            v.memset(small[:, 14, 0:1], 0.0).then_inc(s_tables, 1)

            def sum1(i):
                for (_, h), before in halves(i):
                    part = slice(h * H, h * H + H)
                    dve.wait_ge(s_edge[h], landed(1, i + 1))
                    v.tensor_tensor(key[:, part], rows[:, part, D + 2], s_shift[:, bass.ds(R * i + h * H, H)],
                                    ALU.subtract)
                    v.tensor_scalar(payS[:, bass.ds(R * i + h * H, H), :], rows[:, part, D + 1:D + 3], 1.0,
                                    None, ALU.mult).then_inc(s_took, 1)
                    dve.wait_ge(s_took, 2 * i + h + 1)
                    one_hots(h, key[:, part], s_oh1s)
                    if before:
                        sum_blocks(*before, s_seg1, s_acc1, 64)
            repeat(dve, ITERS, sum1, done, peel=2)
            sum_blocks(ITERS - 1, 1, s_seg1, s_acc1, 64)

            cnt_src = small[:, 8, :]
            step(v.tensor_copy(cnt_src, ACC[:, :, D]))
            for b in range(NB):
                last = v.scalar_tensor_tensor(CT[:, b, :], b2Ubc, cnt_src[:, b:b + 1], CT[:, b, :], ALU.mult, ALU.add)
            last.then_inc(s_node1, 1)

            def update(i):
                put(ACC, i, s_put1, s_u1)
                at = CT[:, bass.ds(4 * i, 4), :].rearrange("p a f -> p (a f)")
                dve.wait_ge(s_u2, i + 1)
                v.tensor_tensor(at, at, PS[6][:, :], ALU.add).then_inc(s_zin, 1)
                dve.wait_ge(s_zin, i + 1)
                dve.wait_ge(s_zl, i + 1)
                if not first(i):
                    dve.wait_ge(s_u3, i)
                v.scalar_tensor_tensor(zgroup, at, 0.0, lnp[:, 0:4, :].rearrange("p a f -> p (a f)"), ALU.max, ALU.add
                                       ).then_inc(s_z1, 1)
                dve.wait_ge(s_u4, i + 1)
                v.tensor_tensor(BT[:, bass.ds(4 * i, 4), :], PS[4][:, :].rearrange("p (a f) -> p a f", a=4),
                                over(ub2bc, 4), ALU.add).then_inc(s_u4c, 1)
            repeat(dve, GROUPS, update)
            dve.wait_ge(s_u4c, GROUPS)

            real = small[:, 9, 0:1]
            step(v.tensor_scalar(real, lane[:, :], float(TAIL), None, ALU.is_lt))

            def node_mean(A, order):
                step(v.tensor_scalar(A[:, BLOCKS - 1, :], A[:, BLOCKS - 1, :], real, None, ALU.mult))
                v.tensor_reduce(lnp[:, 0, :], A[:, 0:BLOCKS, :].rearrange("p b f -> p f b"), AX, ALU.add).then_inc(s_bn, 1)
                dve.wait_ge(s_bnsum, order)

            node_mean(BT, 1)
            step(v.tensor_scalar(lnp[:, 2, :], PS[0][:, 0:D], 1.0 / N, None, ALU.mult))
            step(v.tensor_tensor(BT[:, :, :], BT[:, :, :], over(lnp[:, 2, :], NB), ALU.subtract))
            step(v.tensor_tensor(CT[:, :, :], BT[:, :, :], BT[:, :, :], ALU.mult))
            node_mean(CT, 2)
            v.tensor_scalar(lnp[:, 1, :], PS[0][:, 0:D], 1.0 / N, EPS, ALU.mult, ALU.add).then_inc(s_bn, 1)
            dve.wait_ge(s_bnsd, 1)
            step(v.reciprocal(lnp[:, 1, :], lnp[:, 1, :]))
            step(v.tensor_tensor(lnp[:, 1, :], lnp[:, 1, :], g1, ALU.mult))
            step(v.tensor_tensor(BT[:, :, :], BT[:, :, :], over(lnp[:, 1, :], NB), ALU.mult))
            step(v.tensor_tensor(BT[:, :, :], BT[:, :, :], over(be1, NB), ALU.add))
            step(v.tensor_tensor(X[:, :, :], X[:, :, :], BT[:, :, :], ALU.add))
            v.memset(small[:, 14, 0:1], 0.0).then_inc(s_wdone[1], 1)
            v.memset(small[:, 14, 1:2], 0.0).then_inc(s_xnew[1], 1)

            step(v.tensor_copy(dst_idx[:, 0:PAIRS], payS[:, :, 0]))
            step(v.tensor_tensor(src_relS[:, 0:PAIRS], payS[:, :, 1], s_shift[:, :], ALU.subtract))
            step(v.tensor_scalar(maskS[:, 0:PAIRS], src_relS[:, 0:PAIRS], -1.0, None, ALU.is_gt))
            step(v.tensor_scalar(payS[:, :, 0], src_relS[:, 0:PAIRS], float(P), None, ALU.is_lt))
            step(v.tensor_tensor(maskS[:, 0:PAIRS], maskS[:, 0:PAIRS], payS[:, :, 0], ALU.mult))
            step(v.tensor_scalar(maskS[:, 0:PAIRS], maskS[:, 0:PAIRS], -1.0, BIG, ALU.add, ALU.mult))
            v.memset(dst_idx[:, PAIRS:W2], 0)
            v.memset(src_relS[:, PAIRS:W2], -1.0)
            v.memset(maskS[:, PAIRS:W2], -BIG)
            step(v.memset(regs[64:65, PAIRS:W2], BLOCKS - 1))
            v.memset(small[:, 14, 0:1], 0.0).then_inc(s_tables, 1)
            v.memset(scan_idx, 0)
            v.memset(scan_dst, NOKEY)
            v.memset(scan_prev, -1).then_inc(s_scanfree, 1)
            stats(X, 4)
            norm_ready()

            def project2(i):
                dve.wait_ge(s_h[2], 4 * i + 4)
                put(Hn, i, s_put, s_t, 2)
            repeat(dve, GROUPS, project2)
            dve.wait_ge(s_p2c, GROUPS)
            step(v.tensor_copy(small[:, 8, :], ACC[:, :, D]))
            v.memset(ACC[:, :, D], 1.0).then_inc(s_store2, 1)
            step(v.memset(small[:, 10:12, :], 0.0))
            v.memset(lm[:, 0, H:H + 1], -BIG)
            step(v.memset(m_all[:, 1:2], -BIG))
            dve.wait_ge(s_tab[2], 16)
            step(v.memset(ACC[:, :, :], 0.0))
            dve.wait_ge(s_sc2, 32)

            def block_scores(i, u):
                n, h = U * i + u, u % 2
                blocks = block_numbers_at(H * n)

                def score(q):
                    done(v.scalar_tensor_tensor(lnp[:, q, :], iota[:, 0:P], src_relS[:, bass.ds(H * n + q, 1)],
                                                BT[:, bass.ds(blocks[q], 1), :].rearrange("p a f -> p (a f)"),
                                                ALU.is_equal, ALU.mult, accum_out=sv[:, h * H + q:h * H + q + 1]))
                return score

            def add_up(i, u):
                n, h = U * i + u, u % 2
                blocks = block_numbers_at(H * n)

                def add(q):
                    to = ACC[:, bass.ds(blocks[q], 1), 0:129].rearrange("p a f -> p (a f)")
                    if q == 0:
                        done(v.scalar_tensor_tensor(to, to, fade[:, h:h + 1], seg_ps(h, 0), ALU.mult, ALU.add))
                    elif q < H - 1:
                        done(v.tensor_tensor(to, to, seg_ps(h, q), ALU.add))
                    else:
                        v.tensor_tensor(to, to, seg_ps(h, q), ALU.add).then_inc(s_acc2, 1)
                return add

            def attend(i):
                for u in range(U):
                    n, h = U * i + u, u % 2
                    part = slice(h * H, h * H + H)
                    before = (i, u - 2) if u >= 2 else None if first(i) else (i - 1, u + 2)
                    done.wait()
                    dve.wait_ge(s_row[u], landed(2, i + 1, u))
                    done(v.tensor_tensor(sv[:, part], sv[:, part], (rows, mrow)[u // 2][:, part, D + 1], ALU.add))
                    if before:
                        dve.wait_ge(s_seg2, n - 1)
                    one_hots(h, src_relS[:, bass.ds(H * n, H)], s_oh2)
                    done.wait()
                    step(v.scalar_tensor_tensor(lm[:, h, 0:H], sv[:, part], 0.2, sv[:, part], ALU.mult, ALU.max))
                    step(v.tensor_tensor(lm[:, h, 0:H], lm[:, h, 0:H], maskS[:, bass.ds(H * n, H)], ALU.add))
                    v.tensor_reduce(lm[:, 1 - h, H:H + 1], lm[:, h, :], AX, ALU.max).then_inc(s_mx, 1)
                    score = block_scores(i, u + 1)
                    if before:
                        add = add_up(*before)
                    for q in range(H):
                        if before:
                            if q:
                                done.wait(but=1)
                            add(q)
                        score(q)
                    if before:
                        dve.wait_ge(s_acc2, n - 1)
                    dve.wait_ge(s_mxt, n + 1)
                    v.tensor_reduce(m_run[0:1, h:h + 1], PS[6][0:1, 0:P], AX, ALU.max).then_inc(s_mnew, 1)
            score = block_scores(0, 0)
            for q in range(H):
                score(q)
            repeat(dve, ITERS2, attend, done, peel=2)
            for u in (U - 2, U - 1):
                add = add_up(ITERS2 - 1, u)
                dve.wait_ge(s_seg2, U * ITERS2 - U + u + 1)
                for q in range(H):
                    add(q)
                    if q < H - 1:
                        done.wait()
                dve.wait_ge(s_acc2, U * ITERS2 - U + u + 1)
            dve.wait_ge(s_hmax, U * ITERS2)
            for A, b0 in ((BT, 0), (CT, NB // 2)):
                by_half = A[:, :, :].rearrange("p b f -> p (b f)")[:, 0:NB // 2 * U * ITERS2].rearrange(
                    "p (b n) -> p b n", n=U * ITERS2)
                shape = [P, NB // 2, U * ITERS2]
                step(v.tensor_tensor(by_half, first_block[:, :].unsqueeze(1).to_broadcast(shape),
                                     iota[:, b0:b0 + NB // 2].unsqueeze(2).to_broadcast(shape), ALU.is_le))
                step(v.tensor_scalar(by_half, by_half, -1.0, BIG, ALU.add, ALU.mult))
                step(v.tensor_tensor(by_half, by_half, history.unsqueeze(1).to_broadcast(shape), ALU.add))
                step(v.tensor_reduce(m_block[:, b0:b0 + NB // 2], by_half, AX, ALU.max))

            step(v.tensor_scalar(small[:, 6, :], m_block, -1.0, m_all[:, 1:2], ALU.mult, ALU.add))
            v.tensor_scalar(small[:, 6, :], small[:, 6, :], 87.0, 0.0, ALU.min, ALU.max).then_inc(s_fin2, 1)
            dve.wait_ge(s_fin2a, 1)
            step(v.scalar_tensor_tensor(small[:, 6, :], small[:, 6, :], 9e-15, ACC[:, :, D], ALU.mult, ALU.add))
            step(v.reciprocal(small[:, 6, :], small[:, 6, :]))
            step(v.tensor_tensor(BT[:, :, :], ACC[:, :, 0:D], spread(small[:, 6, :], NB), ALU.mult))
            step(v.tensor_scalar(CT[:, :, :], BT[:, :, :], 0.0, None, ALU.max))
            v.tensor_scalar(BT[:, :, :], BT[:, :, :], 0.0, None, ALU.min).then_inc(s_fin2, 1)
            dve.wait_ge(s_fin2a, 2)
            step(v.scalar_tensor_tensor(CT[:, :, :], BT[:, :, :], -1.0, CT[:, :, :], ALU.add, ALU.add))
            step(v.tensor_tensor(X[:, :, :], X[:, :, :], CT[:, :, :], ALU.add))
            v.memset(small[:, 14, 0:1], 0.0).then_inc(s_wdone[2], 1)
            v.memset(small[:, 14, 1:2], 0.0).then_inc(s_xnew[2], 1)

            v.memset(fill, 0.0).then_inc(s_zero, 1)
            stats(X, 5)
            norm_ready()
            dve.wait_ge(s_w[3], 48)
            for k in range(2):
                step(v.tensor_tensor(WA[:, 4, :], WA[:, 0, :], WA[:, 2 + k, :], ALU.mult))
                step(v.tensor_reduce(WA[:, 1, 4 * k:4 * k + 4], WA[:, 4, :].rearrange("p (h c) -> p h c", h=4), AX,
                                     ALU.add))
            v.memset(small[:, 14, 0:1], 0.0).then_inc(s_folded3, 1)

            def project3(i):
                dve.wait_ge(s_h[3], 4 * i + 4)
                put(Hn, i, s_put, s_t, 3)
            repeat(dve, GROUPS, project3)

            v.tensor_scalar(upto, iota[:, 0:P], lane[:, 0:1], None, ALU.is_ge).then_inc(s_cum, 1)
            dve.wait_ge(s_cump, 1)
            nodes = slice(0, BLOCKS)
            total, cum, has = small[:, 10, nodes], small[:, 11, nodes], small[:, 5, nodes]
            start_f, end_f, one_row = small[:, 2, nodes], small[:, 3, nodes], small[:, 4, nodes]
            step(v.memset(one_row, 1.0))
            step(v.tensor_copy(total, PS[6][:, 64:64 + BLOCKS]))
            step(v.tensor_tensor_scan(cum, one_row, total, 0.0, ALU.mult, ALU.add))
            step(v.tensor_tensor(cum, cum, total, ALU.subtract))
            step(v.tensor_tensor(end_f, PS[6][:, 0:BLOCKS], cum, ALU.add))
            step(v.tensor_tensor(start_f, end_f, cnt_dst[:, nodes], ALU.subtract))
            step(v.tensor_scalar(end_f, end_f, -1.0, 0.0, ALU.add, ALU.max))
            step(v.tensor_copy(end_idx[:, nodes], end_f))
            step(v.tensor_scalar(has, cnt_dst[:, nodes], 1.0, None, ALU.min))
            step(v.tensor_tensor(start_f, start_f, has, ALU.mult))
            step(v.tensor_scalar(end_f, has, float(-NOWHERE), float(NOWHERE), ALU.mult, ALU.add))
            step(v.tensor_tensor(start_f, start_f, end_f, ALU.add))
            step(v.tensor_copy(start_idx[:, nodes], start_f))

            dve.wait_ge(s_scan, 64)
            dve.wait_ge(s_prev, 48)
            step(v.tensor_tensor(cont, scan_dst, scan_prev, ALU.is_equal))
            step(v.tensor_scalar(contneg, cont, -1.0, 1e38, ALU.add, ALU.mult))
            step(v.tensor_reduce(all_cont, cont, AX, ALU.min))
            dve.wait_ge(s_p3c, GROUPS)
            step(v.memset(mrow_flat[:, 416:1248], 0.0))

            def take(i):
                for h in range(2):
                    dve.wait_ge(s_row[h], landed(3, i + 1))
                    v.tensor_scalar(SI[:, bass.ds(R * i + h * H, H), :], g4[:, h * H:h * H + H, :], 1.0, None, ALU.mult
                                    ).then_inc(s_got3, 1)
            repeat(dve, SG // R, take)
            dve.wait_ge(s_got3, 2 * (SG // R))

            def segments(to, of, w, factor, whole, op0, op1, start, order):
                for c in range(w):
                    step(v.tensor_tensor_scan(to[:, :, c], factor, of[:, 0:SC, c], start, op0, op1))
                step(v.tensor_copy(last_v[:, 0:w], to[:, SC - 1, :]))
                v.tensor_copy(last_c[:, 0:w], whole.to_broadcast([P, w])).then_inc(s_carry, 1)
                dve.wait_ge(s_carryp, 2 * order + 1)
                step(v.tensor_copy(carry_row[0:w, P:3 * P], PS[5][0:w, 0:2 * P]))
                step(v.tensor_tensor_scan(carry_row[0:w, P:2 * P], carry_row[0:w, 2 * P:3 * P], carry_row[0:w, P:2 * P],
                                          start, op0, op1))
                step(v.memset(carry_row[0:w, 0:1], start))
                v.tensor_scalar(carry_row[0:w, 1:P], carry_row[0:w, P:2 * P - 1], 1.0, None, ALU.mult
                                ).then_inc(s_carry, 1)
                dve.wait_ge(s_carryp, 2 * order + 2)
                step(v.tensor_copy(last_v[:, 0:w], PS[5][:, 256:256 + w]))
                for c in range(w):
                    step(v.tensor_tensor_scan(to[:, :, c], factor, of[:, 0:SC, c], last_v[:, c:c + 1], op0, op1))

            step(v.tensor_scalar(all_neg, all_cont, -1.0, 1e38, ALU.add, ALU.mult))
            segments(MX, SI, 4, contneg, all_neg, ALU.add, ALU.max, -1e38, 0)
            v.memset(small[:, 14, 0:1], 0.0).then_inc(s_scanned, 1)
            dve.wait_ge(s_mxnode, 16 * BLOCKS)
            target = SN[:, :, 4:8]
            step(v.tensor_tensor(mx_node, mx_node, target, ALU.add))
            step(v.tensor_copy(fill_node[:, :, 0:4], target))
            v.scalar_tensor_tensor(fill_node[:, :, 4:8], mx_node, 0.2, mx_node, ALU.mult, ALU.max).then_inc(s_fill, 1)
            dve.wait_ge(s_fillback, 16)
            segments(FO, fill, 8, cont, all_cont, ALU.mult, ALU.add, 0.0, 1)
            edges_si = SI[:, 0:SC, :]
            step(v.tensor_tensor(edges_si, edges_si, FO[:, :, 0:4], ALU.add))
            step(v.scalar_tensor_tensor(edges_si, edges_si, 0.2, edges_si, ALU.mult, ALU.max))
            step(v.tensor_tensor(edges_si, edges_si, FO[:, :, 4:8], ALU.subtract))
            v.tensor_scalar(edges_si, edges_si, 0.0, None, ALU.min).then_inc(s_alpha, 1)
            dve.wait_ge(s_alphae, 1)
            dve.wait_ge(s_segmax, 16)
            segments(MX, SI, 4, cont, all_cont, ALU.mult, ALU.add, 0.0, 2)
            v.memset(small[:, 14, 0:1], 0.0).then_inc(s_scanned, 1)
            dve.wait_ge(s_sumnode, 16 * BLOCKS)
            step(v.tensor_scalar(mx_node, sum_node, 1e-16, None, ALU.add))
            step(v.reciprocal(mx_node, mx_node))
            step(v.tensor_tensor(sum_node, sum_node, mx_node, ALU.mult))
            step(v.tensor_tensor(sum_node[:, nodes, :], sum_node[:, nodes, :], has.unsqueeze(2).to_broadcast([P, BLOCKS, 4]),
                                 ALU.mult))
            heads = BT[:, :, :].rearrange("p b (h c) -> p (b h) c", h=4)
            step(v.tensor_tensor(heads, heads, sum_node.rearrange("p b h -> p (b h)").unsqueeze(2)
                                 .to_broadcast([P, NB * 4, 32]), ALU.mult))
            step(v.tensor_tensor(X[:, :, :], X[:, :, :], BT[:, :, :], ALU.add))
            v.memset(small[:, 14, 1:2], 0.0).then_inc(s_xnew[3], 1)


_INS = ['x', 'src', 'dst', 'edge_attr_128', 'L0_gnn_W1', 'L0_gnn_b1', 'L0_gnn_W2', 'L0_gnn_b2', 'L0_gnn_gamma', 'L0_gnn_beta', 'L1_gnn_W1', 'L1_gnn_b1', 'L1_gnn_W2', 'L1_gnn_b2', 'L1_gnn_U1', 'L1_gnn_ub1', 'L1_gnn_U2', 'L1_gnn_ub2', 'L1_gnn_gamma', 'L1_gnn_beta', 'L2_gnn_W', 'L2_gnn_attn', 'L3_gnn_weight', 'L3_gnn_att']
_OUTS = [((6250, 128), 'float32')]


def kernel(**inputs):
    import numpy as _np
    import concourse.bacc as _bacc
    from concourse import mybir as _mybir
    from concourse.bass_utils import run_bass_kernel_spmd as _run

    nc = _bacc.Bacc("TRN2", target_bir_lowering=False, num_devices=1)
    arrays, args = {}, {}
    for name in _INS:
        a = _np.ascontiguousarray(inputs[name])
        arrays[f"in_{name}_dram"] = a
        args[name] = nc.dram_tensor(f"in_{name}_dram", a.shape, _mybir.dt.from_np(a.dtype), kind="ExternalInput").ap()
    for i, (shape, dtype) in enumerate(_OUTS):
        dt = _mybir.dt.from_np(_np.dtype(dtype))
        args["out"] = nc.dram_tensor(f"out_{i}_dram", shape, dt, kind="ExternalOutput").ap()
    gnn_kernel(nc, **args)
    r = _run(nc, [arrays], core_ids=[0])
    return r.results[0]["out_0_dram"]
```

```python
from contextlib import ExitStack

import concourse.bass as bass
from concourse import mybir

F32 = mybir.dt.float32
BF16 = mybir.dt.bfloat16
I32 = mybir.dt.int32
ALU = mybir.AluOpType
ACT = mybir.ActivationFunctionType
AX = mybir.AxisListType.X

P = 128
D = 128
N, E = 6250, 100000
BLOCKS = -(-N // P)
NB = 52
GROUPS = NB // 4
TAIL = N - (BLOCKS - 1) * P
TILES = -(-E // P)
LASTBASE = E - P
REST = E - (TILES - 1) * P
CH = -(-TILES // P)
PAIRS = TILES + BLOCKS - 1
HP = PAIRS // 2
R = 10
H = 5
ITERS = PAIRS // R
U = 4
OH_DVE = 2
ITERS2 = -(-PAIRS // (U * H))
W2 = (ITERS2 * U + 1) * H
ROW = 132
NOKEY = 8191
NOWHERE = 200000
BIG = 1e30
HB = 8
STEPS = -(-TILES // HB)
SC = -(-E // P)
SREST = E - (P - 1) * SC
SG = -(-SC // (2 * R)) * 2 * R
ITERS3 = SG // (2 * R)
EPS = 1e-5
IN_RANGE = "a pair's tile is a count cut off at the last tile, and its block the rest of the pair's number"


class Tally:

    def __init__(self, eng, sem):
        self.eng, self.sem, self.n, self.lead = eng, sem, 0, 0

    def __call__(self, ins):
        ins.then_inc(self.sem, 1)
        self.n += 1

    def wait(self, but=0):
        self.eng.wait_ge(self.sem, self.lead + self.n - but)


def repeat(eng, times, body, *tallies, peel=1, begin=0):
    peel += begin
    for k in range(begin, peel):
        before = [t.n for t in tallies]
        body(k)
    start = [t.n for t in tallies]
    per = [n - b for n, b in zip(start, before)]
    with eng.Fori(peel, times) as i:
        for t, k in zip(tallies, per):
            t.lead = (i - peel) * k
        body(i)
    for t, n, k in zip(tallies, start, per):
        t.lead, t.n = 0, n + k * (times - peel)


def first(i):
    return isinstance(i, int) and i == 0


def landed(k, i, u=0):
    before = (0, ITERS, 2 * ITERS if u < 2 else 0, 2 * ITERS + ITERS2)[k]
    return 16 * H * (before + i)


def loaded(i, u):
    return 16 * H * ((ITERS if u < 2 else 0) + i)


def halves(i):
    return (((i, 0), None if first(i) else (i - 1, 1)), ((i, 1), (i, 0)))


def gnn_kernel(nc, x, src, dst, edge_attr_128, L0_gnn_W1, L0_gnn_b1, L0_gnn_W2, L0_gnn_b2, L0_gnn_gamma,
               L0_gnn_beta, L1_gnn_W1, L1_gnn_b1, L1_gnn_W2, L1_gnn_b2, L1_gnn_U1, L1_gnn_ub1, L1_gnn_U2,
               L1_gnn_ub2, L1_gnn_gamma, L1_gnn_beta, L2_gnn_W, L2_gnn_attn, L3_gnn_weight, L3_gnn_att, out):
    with ExitStack() as ctx:
        def sb(name, shape, dt=F32):
            return ctx.enter_context(nc.sbuf_tensor(name, shape, dt))

        def sem(name):
            return ctx.enter_context(nc.semaphore(name))

        def ring(name, n):
            return [sem(f"{name}{k}") for k in range(n)]

        table0 = nc.dram_tensor("table0", [NB * P, D], F32, kind="Internal").ap()
        table1 = nc.dram_tensor("table1", [NB * P, D], F32, kind="Internal").ap()
        table2 = nc.dram_tensor("table2", [NB * P, 130], F32, kind="Internal").ap()
        table3 = nc.dram_tensor("table3", [NB * P, 4], F32, kind="Internal").ap()
        messages = nc.dram_tensor("messages", [E, ROW], F32, kind="Internal").ap()
        score2 = nc.dram_tensor("score2", [NB * P], F32, kind="Internal").ap()
        seg_max = nc.dram_tensor("seg_max", [P * SC, 4], F32, kind="Internal").ap()
        seg_sum = nc.dram_tensor("seg_sum", [P * SC, 4], F32, kind="Internal").ap()
        seg_fill = nc.dram_tensor("seg_fill", [P * SC, 8], F32, kind="Internal").ap()

        X = sb("X", [P, NB, D])
        Hn = sb("Hn", [P, NB, D])
        ACC = sb("ACC", [P, NB, 130])
        BT = sb("BT", [P, NB, D])
        CT = sb("CT", [P, NB, D])
        accw = ACC[:, :, :].rearrange("p b f -> p (b f)")
        btw = BT[:, :, :].rearrange("p b f -> p (b f)")
        ctw = CT[:, :, :].rearrange("p b f -> p (b f)")
        hnw = Hn[:, :, :].rearrange("p b f -> p (b f)")

        ACC2 = hnw[:, 0:BLOCKS * 129].rearrange("p (b f) -> p b f", f=129)

        count_i = sb("count_i", [P, 1], I32)
        iota = sb("iota", [P, PAIRS])
        lane = sb("lane", [P, 1])
        lanes = sb("lanes", [P, CH])
        ident = sb("ident", [P, P])
        ones = sb("ones", [P, P])
        below = sb("below", [P, P], BF16)
        onesb = sb("onesb", [P, P], BF16)

        dst_rel = sb("dst_rel", [P, W2])
        pay = sb("pay", [P, PAIRS, 2])
        src_idx = sb("src_idx", [P, W2], I32)
        pos_idx = sb("pos_idx", [P, W2], I32)
        regs = sb("regs", [P, W2], I32)
        s_shift = sb("s_shift", [P, W2])
        payS = sb("payS", [P, W2, 2])
        dst_idx = pos_idx
        src_relS = dst_rel
        maskS = src_idx[:, :].bitcast(F32)

        rows = sb("rows", [P, R, ROW])
        mrow = sb("mrow", [P, R, ROW])
        edge = sb("edge", [P, R, D])
        onehot = sb("onehot", [P, R, P])
        turned = sb("turned", [P, H, 2, P])
        lnp = sb("lnp", [P, H, D])
        first_block = sb("first_block", [P, U * ITERS2])
        key = sb("key", [P, R])
        idxs = sb("idxs", [P, U * H], I32)
        pidx = sb("pidx", [P, R], I32)
        WA = sb("WA", [P, 14, D])
        small = sb("small", [P, 16, NB])
        st = mrow[:, :, :].rearrange("p r f -> p (r f)")[:, 0:NB * 6].rearrange("p (b s) -> p b s", s=6)
        mrow_flat = mrow[:, :, :].rearrange("p r f -> p (r f)")
        tw = turned[:, :, :, :].rearrange("p a b f -> p (a b f)")
        hT, rT = tw[:, 0:512], tw[:, 512:1024]

        group = edge[:, 0:4, :].rearrange("p a f -> p (a f)")
        zgroup = edge[:, 4:8, :].rearrange("p a f -> p (a f)")

        PS = [ctx.enter_context(nc.psum_tensor(f"PS{k}", [P, 512], F32)) for k in range(8)]

        def seg_ps(h, q):
            return PS[2 * h + q // 3][:, 160 * (q % 3):160 * (q % 3) + 129]

        def spread_ps(h, q, n=1):
            at = NB * 4 * (q % 2)
            return PS[3 * h + q // 2][:, at:at + n * NB * 4].rearrange("p (q b f) -> p q b f", q=n, f=4)

        def turn_ps(q):
            return PS[q // 2][:, 256 * (q % 2):256 * (q % 2) + 256]

        def pre_ps(h, q):
            return PS[3 + 2 * h + q // 4][:, D * (q % 4):D * (q % 4) + D]

        pay_flat = pay[:, :, :].rearrange("p n a -> p (n a)")
        payS_flat = payS[:, :, :].rearrange("p n a -> p (n a)")

        srcL = accw[:, 0:896].bitcast(I32).rearrange("p (c e) -> p c e", e=P)
        dstL = accw[:, 896:1792].bitcast(I32).rearrange("p (c e) -> p c e", e=P)
        srcF = accw[:, 1792:2688].rearrange("p (c e) -> p c e", e=P)
        dstF = accw[:, 2688:3584].rearrange("p (c e) -> p c e", e=P)
        hiF = accw[:, 3584:4480].rearrange("p (c e) -> p c e", e=P)
        hiT = mrow_flat[:, 320:1216]
        posT = payS_flat[:, 0:896]
        posF = tw[:, 0:896].rearrange("p (c e) -> p c e", e=P)
        sel = btw[:, 0:CH * PAIRS].rearrange("p (c n) -> p c n", n=PAIRS)
        gbf = ctw[:, 0:CH * PAIRS // 2].bitcast(BF16).rearrange("p (c n) -> p c n", n=PAIRS)
        kpair = ctw[:, 2910:2910 + PAIRS]
        bpair = ctw[:, 3750:3750 + PAIRS]
        tmpp = ctw[:, 4590:4590 + PAIRS]
        oh8 = [ctw[:, 5430 + 200 * q:5430 + 200 * q + 196].bitcast(BF16).rearrange("p (t h) -> p t h", h=BLOCKS)
               for q in range(2)]
        ohp = ctw[:, 5430:5430 + 245].bitcast(BF16).rearrange("p (t h) -> p t h", h=BLOCKS)
        tpos = ctw[:, 5930:5930 + 490].rearrange("p (t h) -> p t h", h=BLOCKS)
        cnt_hi, cum_hi, base_hi, junk_hi = (ctw[:, 6420 + 49 * k:6469 + 49 * k] for k in range(4))
        last_b, rise, xlast = (ctw[:, 6616 + 8 * k:6616 + 8 * k + CH] for k in range(3))
        last_i = ctw[:, 6640:6640 + CH].bitcast(I32)

        W0_1, W0_2 = WA[:, 0, 0:64], WA[0:65, 1, :]
        b0_1 = WA[0:64, 2, 0:1]
        g0, be0 = WA[:, 3, :], WA[:, 4, :]
        W1abu, W1c = WA[:, 0:3, :], WA[:, 3, :]
        b1bc, ub1bc, W1_2, U1b, U2w, ub2bc, g1, be1, W2U, b2Ubc = (WA[:, k, :] for k in range(4, 14))
        b1_2 = small[:, 15, 0:1]

        cnt_dst = small[:, 7, :]
        misc = small[:, 10, :]
        lm = misc[:, 0:12].rearrange("p (h q) -> p h q", h=2)
        sv, wgt = misc[:, 12:22], misc[:, 22:32]
        negm, m_all, fade, m_run = misc[:, 32:34], misc[:, 34:36], misc[:, 36:38], misc[:, 38:40]
        m_block = small[:, 11, :]
        m_col = misc[:, 40:41]
        history = s_shift[:, 0:U * ITERS2]

        scan_idx = pay_flat[:, 0:SG].bitcast(I32)
        scan_dst = pay_flat[:, 800:800 + SC].bitcast(I32)
        scan_prev = payS_flat[:, 0:SC].bitcast(I32)
        contneg = payS_flat[:, 800:800 + SC]
        cont = s_shift[:, 0:SC]
        g4 = edge[:, :, :].rearrange("p r f -> p (r f)")[:, 0:4 * R].rearrange("p (r f) -> p r f", f=4)
        SN = mrow_flat[:, 0:416].rearrange("p (b f) -> p b f", f=8)
        mx_node = mrow_flat[:, 416:624].rearrange("p (b f) -> p b f", f=4)
        sum_node = mrow_flat[:, 624:832].rearrange("p (b f) -> p b f", f=4)
        fill_node = mrow_flat[:, 832:1248].rearrange("p (b f) -> p b f", f=8)
        SI = ctw[:, 0:4 * SG].rearrange("p (i f) -> p i f", f=4)
        MX = ctw[:, 3200:3200 + 4 * SC].rearrange("p (i f) -> p i f", f=4)
        lo3, hi3 = ctw[:, 3200:3200 + SG // 2], ctw[:, 3600:3600 + SG // 2]
        hi_oh = ctw[:, 4000:4000 + R * NB].rearrange("p (r b) -> p r b", b=NB)
        picked = ctw[:, 4520:4520 + H * NB * 4].rearrange("p (q b f) -> p q b f", b=NB, f=4)
        part_i = ctw[:, 5560:5560 + SG // 2].bitcast(I32)
        fill = accw[:, 0:8 * SC].rearrange("p (i f) -> p i f", f=8)
        FO = hnw[:, 0:8 * SC].rearrange("p (i f) -> p i f", f=8)
        upto = onehot[:, 0, :]
        start_idx, end_idx = small[:, 12, :].bitcast(I32), small[:, 13, :].bitcast(I32)
        last_v, last_c = small[:, 0, 0:8], small[:, 0, 8:16]
        all_cont, all_neg = small[:, 0, 16:17], small[:, 0, 17:18]
        carry_row = onehot[:, 1:4, :].rearrange("p a f -> p (a f)")

        s_const = sem("s_const")
        s_edges = sem("s_edges")
        s_x = sem("s_x")
        s_pad = sem("s_pad")
        s_w = ring("s_w", 4)
        s_wdone = ring("s_wdone", 3)
        s_dve = sem("s_dve")
        s_act = sem("s_act")
        s_pe0 = sem("s_pe0")
        s_ask0 = sem("s_ask0")
        s_idle = sem("s_idle")
        s_idleA = sem("s_idleA")
        s_tab = ring("s_tab", 4)
        s_h = ring("s_h", 4)
        s_st = sem("s_st")
        s_sd = sem("s_sd")
        s_nm = sem("s_nm")
        s_out = sem("s_out")

        s_ones0 = sem("s_ones0")
        s_tables = sem("s_tables")
        s_oh8 = sem("s_oh8")
        s_hist = sem("s_hist")
        s_ahead = sem("s_ahead")
        s_placed = sem("s_placed")
        s_bns = sem("s_bns")
        s_idx = sem("s_idx")
        s_row = ring("s_row", U)
        s_t, s_tc, s_p = sem("s_t"), sem("s_tc"), sem("s_p")
        s_m0, s_r0, s_e0, s_e0c = (sem(n) for n in ("s_m0", "s_r0", "s_e0", "s_e0c"))
        s_oh0, s_seg0, s_acc0 = sem("s_oh0"), sem("s_seg0"), sem("s_acc0")
        s_diff, s_diffa = sem("s_diff"), sem("s_diffa")
        s_xnew = ring("s_xnew", 4)
        s_put, s_put1 = sem("s_put"), sem("s_put1")
        s_fold, s_folded = sem("s_fold"), sem("s_folded")
        s_p1a, s_p1c = sem("s_p1a"), sem("s_p1c")
        s_edge = ring("s_edge", U)
        s_oh1 = sem("s_oh1")
        s_turn, s_turnedc = sem("s_turn"), sem("s_turnedc")
        s_pre = sem("s_pre")
        s_sum1 = sem("s_sum1")
        s_ln = sem("s_ln")
        s_msg = sem("s_msg")
        s_sent = ring("s_sent", 2)
        s_oh1s, s_oh1d, s_seg1, s_acc1, s_took = (sem(n) for n in ("s_oh1s", "s_oh1d", "s_seg1", "s_acc1", "s_took"))
        s_u1, s_u1c, s_u2, s_zin, s_zl, s_z1, s_u3, s_u3c, s_u4, s_u4c = (
            sem(n) for n in ("s_u1", "s_u1c", "s_u2", "s_zin", "s_zl", "s_z1", "s_u3", "s_u3c", "s_u4", "s_u4c"))
        s_bn, s_bnsum, s_bnsd = sem("s_bn"), sem("s_bnsum"), sem("s_bnsd")
        s_store2 = sem("s_store2")
        s_sc2 = sem("s_sc2")
        s_fold2, s_folded2 = sem("s_fold2"), sem("s_folded2")
        s_p2c = sem("s_p2c")
        s_mx, s_mxt, s_mnew, s_mbc, s_negm = (sem(n) for n in ("s_mx", "s_mxt", "s_mnew", "s_mbc", "s_negm"))
        s_wgt, s_oh2, s_seg2, s_acc2 = (sem(n) for n in ("s_wgt", "s_oh2", "s_seg2", "s_acc2"))
        s_scaled, s_hmax = sem("s_scaled"), sem("s_hmax")
        s_mcol, s_mrow = sem("s_mcol"), sem("s_mrow")
        s_fin2, s_fin2a = sem("s_fin2"), sem("s_fin2a")
        s_scanfree, s_scan, s_prev = (sem(n) for n in ("s_scanfree", "s_scan", "s_prev"))
        s_folded3, s_p3c = sem("s_folded3"), sem("s_p3c")
        s_cum, s_cump, s_got3, s_carry, s_carryp = (sem(n) for n in ("s_cum", "s_cump", "s_got3", "s_carry", "s_carryp"))
        s_oh3, s_turn3, s_turned3, s_sel3, s_took3 = (
            sem(n) for n in ("s_oh3", "s_turn3", "s_turned3", "s_sel3", "s_took3"))
        s_scanned, s_segmax, s_mxnode, s_zero, s_fill, s_fillz, s_filled, s_fillback = (
            sem(n) for n in ("s_scanned", "s_segmax", "s_mxnode", "s_zero", "s_fill", "s_fillz", "s_filled",
                             "s_fillback"))
        s_alpha, s_alphae, s_segsum, s_sumnode = (sem(n) for n in ("s_alpha", "s_alphae", "s_segsum", "s_sumnode"))

        block = ctx.enter_context(nc.Block())

        def spread(col, n, w=D):
            return col.unsqueeze(2).to_broadcast([P, n, w])

        def over(row, n):
            return row.unsqueeze(1).to_broadcast([P, n, D])

        def message_rows(eng, kind, i, mine):
            for u in (mine, mine + 2):
                n = U * i + u
                _, places = nc.values_load_multi_w_load_instructions(
                    regs[96:97, bass.ds(H * n, H)], engines=[kind], min_val=0, max_val=LASTBASE,
                    skip_runtime_bounds_check_because=IN_RANGE)
                if not first(i):
                    eng.wait_ge(s_seg1, n - U + 1)
                    eng.wait_ge(s_took, n - U + 1)
                for q in range(H):
                    eng.dma_start((rows, mrow)[u // 2][:, mine * H + q, :], messages[bass.ds(places[q], P), :]
                                  ).then_inc(s_edge[u], 16)

        @block.sync
        def _(sp):
            sp.wait_ge(s_pad, 3)
            for a, s in ((srcL, src), (dstL, dst)):
                sp.dma_start(a[:, 0:CH - 1, :], s[0:(CH - 1) * P * P].rearrange("(c t e) -> t c e", t=P, e=P)
                             ).then_inc(s_edges, 16)
                sp.dma_start(a[0:TILES - 1 - (CH - 1) * P, CH - 1, :],
                             s[(CH - 1) * P * P:(TILES - 1) * P].rearrange("(t e) -> t e", e=P)).then_inc(s_edges, 16)
                sp.dma_start(a[TILES - 1 - (CH - 1) * P:TILES - (CH - 1) * P, CH - 1, P - REST:P],
                             s[(TILES - 1) * P:E].rearrange("(t e) -> t e", t=1)).then_inc(s_edges, 16)
            sp.dma_start(X[:, 0:BLOCKS - 1, :], x[0:(BLOCKS - 1) * P, :].rearrange("(b j) f -> j b f", j=P)
                         ).then_inc(s_x, 16)
            sp.dma_start(X[0:TAIL, BLOCKS - 1, :], x[(BLOCKS - 1) * P:N, :]).then_inc(s_x, 16)

            sp.wait_ge(s_h[0], GROUPS)
            sp.dma_start(table0.rearrange("(b j) f -> j b f", j=P), Hn[:, :, :]).then_inc(s_tab[0], 16)
            sp.wait_ge(s_p1a, 2 * GROUPS)
            sp.dma_start(table1.rearrange("(b j) f -> j b f", j=P), Hn[:, :, :]).then_inc(s_tab[1], 16)
            sp.wait_ge(s_p1c, 2 * GROUPS)

            def edge_rows(i):
                for h in range(2):
                    if not first(i):
                        sp.wait_ge(s_turn, 2 * i - 1 + h)
                    for j in range(h * H, h * H + H):
                        at = sp.value_load(regs[32:33, bass.ds(R * i + j, 1)], min_val=0, max_val=LASTBASE)
                        sp.dma_start(edge[:, j, :], edge_attr_128[bass.ds(at, P), :]).then_inc(s_edge[h], 16)
            repeat(sp, ITERS, edge_rows)

            for h in range(2):
                sp.wait_ge(s_sent[h], landed(0, ITERS))
            sp.wait_ge(s_tables, 3)

            repeat(sp, ITERS2, lambda i: message_rows(sp, mybir.EngineType.SP, i, 0))
            sp.wait_ge(s_store2, 1)
            sp.dma_start(table2.rearrange("(b j) f -> j b f", j=P), ACC[:, :, :]).then_inc(s_tab[2], 16)
            sp.dma_start(score2.rearrange("(b j) -> j b", j=P), small[:, 8, :],
                         allow_slow_non_contiguous=True).then_inc(s_sc2, 16)
            sp.wait_ge(s_sc2, 16)
            sp.dma_start(btw, score2.partition_broadcast(P)).then_inc(s_sc2, 16)
            sp.wait_ge(s_scanfree, 1)
            for a, s in ((scan_idx, src), (scan_dst, dst)):
                sp.dma_start(a[0:P - 1, 0:SC], s[0:(P - 1) * SC].rearrange("(p i) -> p i", i=SC)).then_inc(s_scan, 16)
                sp.dma_start(a[P - 1:P, 0:SREST], s[(P - 1) * SC:E].rearrange("(p i) -> p i", p=1)).then_inc(s_scan, 16)
            sp.dma_start(scan_prev[0:1, 1:SC], dst[0:SC - 1].rearrange("(p i) -> p i", p=1)).then_inc(s_prev, 16)
            sp.dma_start(scan_prev[1:P - 1, :], dst[SC - 1:(P - 1) * SC - 1].rearrange("(p i) -> p i", i=SC)
                         ).then_inc(s_prev, 16)
            sp.dma_start(scan_prev[P - 1:P, 0:SREST], dst[(P - 1) * SC - 1:E - 1].rearrange("(p i) -> p i", p=1)
                         ).then_inc(s_prev, 16)
            sp.wait_ge(s_p3c, 2 * GROUPS)
            sp.dma_start(table3.rearrange("(b j) f -> j b f", j=P), SN[:, :, 0:4]).then_inc(s_tab[3], 16)
            sp.wait_ge(s_zero, 1)
            sp.dma_start(seg_fill.rearrange("(p i) f -> p i f", i=SC), fill).then_inc(s_fillz, 16)
            sp.wait_ge(s_scanned, 1)
            sp.dma_start(seg_max.rearrange("(p i) f -> p i f", i=SC), MX[:, :, :]).then_inc(s_segmax, 16)
            sp.wait_ge(s_filled, 16 * BLOCKS)
            sp.dma_start(fill, seg_fill.rearrange("(p i) f -> p i f", i=SC)).then_inc(s_fillback, 16)
            sp.wait_ge(s_scanned, 2)
            sp.dma_start(seg_sum.rearrange("(p i) f -> p i f", i=SC), MX[:, :, :]).then_inc(s_segsum, 16)
            sp.wait_ge(s_xnew[3], 1)
            sp.dma_start(out[0:(BLOCKS - 1) * P, :].rearrange("(b j) f -> j b f", j=P), X[:, 0:BLOCKS - 1, :]
                         ).then_inc(s_out, 16)
            sp.dma_start(out[(BLOCKS - 1) * P:N, :], X[0:TAIL, BLOCKS - 1, :]).then_inc(s_out, 16)
            sp.wait_ge(s_out, 32)

        @block.gpsimd
        def _(pool):
            idx_steps = Tally(pool, s_idx)
            nc.gpsimd.iota(tmpp.bitcast(I32), pattern=[[1, PAIRS]], base=0, channel_multiplier=0).then_inc(s_const, 1)
            nc.gpsimd.iota(count_i[:, :], pattern=[[0, 1]], base=0, channel_multiplier=1).then_inc(s_const, 1)
            nc.gpsimd.memset(X[:, :, :], 0.0).then_inc(s_pad, 1)

            def stage(ring_idx, table, at):
                pool.sem_inc(s_idle, 1)
                idx_steps(nc.gpsimd.tensor_copy(ring_idx, table[:, bass.ds(at, H)]))
                idx_steps.wait()
                pool.sem_inc(s_idle, 1)

            def gather(table, i, h, idx_table, k, used, width, rings=(rows,)):
                n = 2 * len(rings)
                if not first(i):
                    pool.wait_ge(s_row[h], landed(k, i, h))
                    pool.wait_ge(used, n * i - n + 1 + h)
                stage(idxs[:, h * H:h * H + H], idx_table, n * H * i + h * H)
                for j in range(h * H, h * H + H):
                    nc.gpsimd.indirect_dma_start(rings[h // 2][:, j % R, 0:width], None, table[:, :],
                                                 bass.IndirectOffsetOnAxis(idxs[:, j:j + 1], 0)
                                                 ).then_inc(s_row[h], 16)

            pool.wait_ge(s_tables, 1)
            pool.wait_ge(s_tab[0], 16)

            def sum0(i):
                for h in range(2):
                    gather(table0, i, h, src_idx, 0, s_seg0, D)
            repeat(pool, ITERS, sum0, idx_steps)

            pool.wait_ge(s_tables, 2)
            pool.wait_ge(s_tab[1], 16)

            def scatter(i, h):
                pool.wait_ge(s_msg, 2 * i + h + 1)
                if not first(i):
                    pool.wait_ge(s_sent[h], landed(0, i))
                stage(pidx[:, h * H:h * H + H], pos_idx, R * i + h * H)
                for j in range(h * H, h * H + H):
                    nc.gpsimd.indirect_dma_start(messages[:, :], bass.IndirectOffsetOnAxis(pidx[:, j:j + 1], 0),
                                                 mrow[:, j, :], None, bounds_check=E - 1, oob_is_err=False
                                                 ).then_inc(s_sent[h], 16)

            def edges(i):
                gather(table1, i, 0, src_idx, 1, s_msg, D)
                if not first(i):
                    scatter(i - 1, 1)
                gather(table1, i, 1, src_idx, 1, s_msg, D)
                scatter(i, 0)
            repeat(pool, ITERS, edges, idx_steps, peel=2)
            scatter(ITERS - 1, 1)

            def one_hots1(i):
                for u in range(U):
                    n, h = U * i + u, u % 2
                    pool.wait_ge(s_took, n + 1)
                    if not (first(i) and u < 2):
                        pool.wait_ge(s_seg1, n - 1)
                    pool.sem_inc(s_idle, 1)
                    for j in range(h * H + OH_DVE, h * H + H):
                        last = nc.gpsimd.tensor_scalar(onehot[:, j, :], iota[:, 0:P], key[:, j:j + 1], None, ALU.is_equal)
                    last.then_inc(s_oh1s, 1)
            repeat(pool, ITERS2, one_hots1)

            pool.wait_ge(s_tables, 4)
            pool.wait_ge(s_tab[2], 16)

            def attend(i):
                for u in range(U):
                    gather(table2, i, u, dst_idx, 2, s_seg2, 130, (rows, mrow))
            repeat(pool, ITERS2, attend, idx_steps)

            pool.wait_ge(s_scan, 64)
            pool.wait_ge(s_tab[3], 16)

            def scores(i):
                for h in range(2):
                    gather(table3, i, h, scan_idx, 3, s_got3, 4, (g4,))
            repeat(pool, ITERS3, scores, idx_steps)

            pool.wait_ge(s_segmax, 16)
            for b in range(BLOCKS):
                nc.gpsimd.indirect_dma_start(mx_node[:, b, :], None, seg_max[:, :],
                                             bass.IndirectOffsetOnAxis(end_idx[:, b:b + 1], 0)
                                             ).then_inc(s_mxnode, 16)
            pool.wait_ge(s_fill, 1)
            pool.wait_ge(s_fillz, 16)
            for b in range(BLOCKS):
                nc.gpsimd.indirect_dma_start(seg_fill[:, :], bass.IndirectOffsetOnAxis(start_idx[:, b:b + 1], 0),
                                             fill_node[:, b, :], None, bounds_check=E - 1, oob_is_err=False
                                             ).then_inc(s_filled, 16)
            pool.wait_ge(s_segsum, 16)
            for b in range(BLOCKS):
                nc.gpsimd.indirect_dma_start(sum_node[:, b, :], None, seg_sum[:, :],
                                             bass.IndirectOffsetOnAxis(end_idx[:, b:b + 1], 0)
                                             ).then_inc(s_sumnode, 16)

        @block.tensor
        def _(pe):
            def turn7(a, order):
                pe.wait_ge(s_ask0, order)
                for c in range(CH):
                    last = nc.tensor.transpose(PS[c // 4][:, c % 4 * P:c % 4 * P + P], a[:, c, :], ident[:, :])
                last.then_inc(s_pe0, 1)

            def count_below(order):
                pe.wait_ge(s_ask0, order)
                for half in range(2):
                    for c in range(CH):
                        last = nc.tensor.matmul(PS[2 + half][:, 0:HP], onesb[:, :], gbf[:, c, half * HP:half * HP + HP],
                                                start=(c == 0), stop=(c == CH - 1))
                last.then_inc(s_pe0, 1)

            def pick(a, order):
                pe.wait_ge(s_ask0, order)
                for half in range(2):
                    for c in range(CH):
                        last = nc.tensor.matmul(PS[2 + half][:, 0:HP], a[:, c, :], sel[:, c, half * HP:half * HP + HP],
                                                start=(c == 0), stop=(c == CH - 1))
                last.then_inc(s_pe0, 1)

            turn7(hiF, 1)
            count_below(2)
            pick(dstF, 3)
            pick(srcF, 4)

            def histogram(i):
                for q in range(2):
                    pe.wait_ge(s_oh8, 2 * i + q + 1)
                    nc.tensor.matmul(PS[4][:, 0:HB * BLOCKS], onesb[:, :], oh8[q], start=first(i) and q == 0,
                                     stop=False, skip_group_check=True).then_inc(s_hist, 1)
            repeat(pe, STEPS // 2, histogram)

            def turn_group(a, to):
                for q in range(4):
                    last = nc.tensor.transpose(to[:, q * P:q * P + P], a[:, q * P:q * P + P], ident[:, :])
                return last

            pe.wait_ge(s_w[0], 16 * 6)

            def turn_h(i):
                pe.wait_ge(s_put, i + 1)
                if not first(i):
                    pe.wait_ge(s_e0c, i)
                turn_group(group, PS[7]).then_inc(s_t, 1)

            def hidden(i):
                pe.wait_ge(s_tc, i + 1)
                nc.tensor.matmul(PS[6][0:64, :], W0_1, hT, start=True, stop=True).then_inc(s_m0, 1)

            def result(i):
                pe.wait_ge(s_r0, i + 1)
                for q in range(4):
                    last = nc.tensor.matmul(PS[7][:, q * P:q * P + P], rT[0:65, q * P:q * P + P], W0_2,
                                            start=True, stop=True)
                last.then_inc(s_e0, 1)

            def segment(i, h, oh_ready, row_ready, row_count, used, done):
                pe.wait_ge(oh_ready, 2 * i + h + 1)
                pe.wait_ge(row_ready[h], row_count)
                if not first(i):
                    pe.wait_ge(used, 2 * i - 1 + h)
                for q in range(H):
                    last = nc.tensor.matmul(seg_ps(h, q), onehot[:, h * H + q, :], rows[:, h * H + q, 0:129],
                                            start=True, stop=True)
                last.then_inc(done, 1)

            def place(i):
                pe.wait_ge(s_oh8, STEPS + i + 1)
                if not first(i):
                    pe.wait_ge(s_placed, i)
                ahead = PS[4][:, 0:R * BLOCKS].rearrange("p (t h) -> p t h", h=BLOCKS)
                nc.tensor.matmul(ahead, below[:, :], ohp, start=True, stop=False, skip_group_check=True)
                for t in range(R - 1):
                    nc.tensor.matmul(ahead[:, t + 1:R, :], onesb[:, :],
                                     ohp[:, t:t + 1, :].to_broadcast([P, R - 1 - t, BLOCKS]),
                                     start=False, stop=(t == R - 2), skip_group_check=True)
                for t in range(R):
                    last = nc.tensor.matmul(PS[5][:, 0:BLOCKS], onesb[:, :], ohp[:, t, :], start=(t == 0),
                                            stop=(t == R - 1))
                last.then_inc(s_ahead, 1)

            def sum0(i):
                segment(i, 0, s_oh0, s_row, landed(0, i + 1), s_acc0, s_seg0)
                place(i)
                segment(i, 1, s_oh0, s_row, landed(0, i + 1), s_acc0, s_seg0)

            def sum0_mlp0(i):
                turn_h(i)
                segment(i, 0, s_oh0, s_row, landed(0, i + 1), s_acc0, s_seg0)
                hidden(i)
                place(i)
                segment(i, 1, s_oh0, s_row, landed(0, i + 1), s_acc0, s_seg0)
                result(i)
            repeat(pe, GROUPS, sum0_mlp0)
            repeat(pe, ITERS, sum0, begin=GROUPS)

            turn7(posT.rearrange("p (c e) -> p c e", e=P), 5)
            pick(posF, 6)
            count_below(7)

            pe.wait_ge(s_w[1], 16 * 13)
            nc.tensor.transpose(PS[7][:, 0:P], W1_2, ident[:, :]).then_inc(s_fold, 1)
            pe.wait_ge(s_folded, 1)
            nc.tensor.matmul(PS[6][:, 0:D], tw[:, 0:D], U1b, start=True, stop=True)
            nc.tensor.matmul(PS[6][:, D:2 * D], b1_2.to_broadcast([P, P]), U1b, start=True, stop=True
                             ).then_inc(s_fold, 1)
            pe.wait_ge(s_folded, 2)

            def turn_next(k, i):
                pe.wait_ge(s_put, GROUPS * k + i + 1)
                turn_group(group, PS[7]).then_inc(s_t, 1)

            def project(k, weights, width, used):
                def body(i):
                    pe.wait_ge(s_tc, GROUPS * k + i + 1)
                    for half in range(2):
                        if not first(i):
                            pe.wait_ge(used, 2 * i - 1 + half)
                        for q in (2 * half, 2 * half + 1):
                            last = nc.tensor.matmul(PS[2 + q][:, 0:width], hT[:, q * P:q * P + P], weights,
                                                    start=True, stop=True)
                        last.then_inc(s_p, 1)
                    if i is not GROUPS - 1:
                        turn_next(k, i + 1)
                turn_next(k, 0)
                repeat(pe, GROUPS - 1, body)
                body(GROUPS - 1)
            project(1, W1abu.rearrange("p a f -> p (a f)"), 3 * D, s_p1c)

            def edges(i):
                for (_, h), before in halves(i):
                    _, blocks = nc.values_load_multi_w_load_instructions(
                        regs[0:1, bass.ds(R * i + h * H, H)], engines=[mybir.EngineType.PE], min_val=0,
                        max_val=BLOCKS - 1, skip_runtime_bounds_check_because=IN_RANGE)
                    pe.wait_ge(s_oh1, 2 * i + h + 1)
                    pe.wait_ge(s_edge[h], landed(0, i + 1))
                    if before:
                        pe.wait_ge(s_turnedc, 2 * i + h)
                    for q in range(H):
                        nc.tensor.transpose(turn_ps(q)[:, 0:P], onehot[:, h * H + q, :], ident[:, :])
                        last = nc.tensor.transpose(turn_ps(q)[:, P:2 * P], edge[:, h * H + q, :], ident[:, :])
                    last.then_inc(s_turn, 1)
                    pe.wait_ge(s_turnedc, 2 * i + h + 1)
                    if not first(i):
                        pe.wait_ge(s_sum1, 2 * i - 1 + h)
                    for q in range(H):
                        nc.tensor.matmul(pre_ps(h, q), turned[:, q, 1, :], W1c, start=True, stop=False)
                        last = nc.tensor.matmul(pre_ps(h, q), turned[:, q, 0, :],
                                                BT[:, bass.ds(blocks[q], 1), :].rearrange("p a f -> p (a f)"),
                                                start=False, stop=True)
                    last.then_inc(s_pre, 1)
            repeat(pe, ITERS, edges)

            def segment2(i, u, oh_ready, rows_ready, rows_count, used, done):
                n, h = U * i + u, u % 2
                pe.wait_ge(oh_ready, n + 1)
                pe.wait_ge(rows_ready, rows_count)
                if not (first(i) and u < 2):
                    pe.wait_ge(used, n - 1)
                for q in range(H):
                    last = nc.tensor.matmul(seg_ps(h, q), onehot[:, h * H + q, :],
                                            (rows, mrow)[u // 2][:, h * H + q, 0:129], start=True, stop=True)
                last.then_inc(done, 1)

            def sum1(i):
                for u in range(U):
                    pe.wait_ge(s_oh1d, U * i + u + 1)
                    segment2(i, u, s_oh1s, s_edge[u], loaded(i + 1, u), s_acc1, s_seg1)
            repeat(pe, ITERS2, sum1)

            def update(i):
                if i is not GROUPS:
                    pe.wait_ge(s_put1, i + 1)
                    turn_group(group, PS[7]).then_inc(s_u1, 1)
                if not first(i):
                    pe.wait_ge(s_z1, i)
                    turn_group(zgroup, PS[5]).then_inc(s_u3, 1)
                if i is not GROUPS:
                    pe.wait_ge(s_u1c, i + 1)
                    for q in range(4):
                        last = nc.tensor.matmul(PS[6][:, q * P:q * P + P], hT[:, q * P:q * P + P], W2U,
                                                start=True, stop=True)
                    last.then_inc(s_u2, 1)
                if not first(i):
                    pe.wait_ge(s_u3c, i)
                    for q in range(4):
                        last = nc.tensor.matmul(PS[4][:, q * P:q * P + P], rT[:, q * P:q * P + P], U2w,
                                                start=True, stop=True)
                    last.then_inc(s_u4, 1)
            repeat(pe, GROUPS, update, peel=2)
            update(GROUPS)
            for k in range(2):
                pe.wait_ge(s_bn, k + 1)
                nc.tensor.matmul(PS[0][:, 0:D], ones[:, :], lnp[:, 0, :], start=True, stop=True).then_inc(s_bnsum, 1)

            pe.wait_ge(s_w[2], 48)
            nc.tensor.transpose(PS[7][:, 0:P], WA[:, 0, :], ident[:, :]).then_inc(s_fold2, 1)
            pe.wait_ge(s_folded2, 1)
            nc.tensor.matmul(PS[6][:, 0:2], tw[:, 0:D], WA[:, 3, 0:2], start=True, stop=True).then_inc(s_fold2, 1)
            pe.wait_ge(s_folded2, 2)
            waf = WA[:, :, :].rearrange("p a f -> p (a f)")
            project(2, waf[:, 0:130], 130, s_p2c)

            def weigh(i, u):
                segment2(i, u, s_oh2, s_scaled, U * i + u + 1, s_acc2, s_seg2)

            def attend(i):
                for u in range(U):
                    n, h = U * i + u, u % 2
                    pe.wait_ge(s_mx, n + 1)
                    if not (first(i) and u == 0):
                        pe.wait_ge(s_negm, n)
                    nc.tensor.transpose(PS[6][0:1, 0:P], lm[:, 1 - h, H:H + 1], ident[:, :]).then_inc(s_mxt, 1)
                    if u:
                        weigh(i, u - 1)
                    elif not first(i):
                        weigh(i - 1, U - 1)
                    pe.wait_ge(s_mnew, n + 1)
                    nc.tensor.matmul(PS[6][:, 256:257], ones[0:1, :], m_run[0:1, h:h + 1], start=True, stop=True
                                     ).then_inc(s_mbc, 1)
            repeat(pe, ITERS2, attend)
            weigh(ITERS2 - 1, U - 1)
            pe.wait_ge(s_mcol, 1)
            nc.tensor.matmul(PS[5][:, 0:NB], m_col.to_broadcast([P, P]), ident[:, 0:NB], start=True, stop=True
                             ).then_inc(s_mrow, 1)

            pe.wait_ge(s_folded3, 1)
            project(3, waf[:, 0:136], 136, s_p3c)
            pe.wait_ge(s_cum, 1)
            nc.tensor.matmul(PS[6][:, 0:BLOCKS], upto, cnt_dst[:, 0:BLOCKS], start=True, stop=True)
            nc.tensor.matmul(PS[6][:, 64:64 + BLOCKS], ones[:, :], cnt_dst[:, 0:BLOCKS], start=True, stop=True
                             ).then_inc(s_cump, 1)
            def pick3(i):
                for h in range(2):
                    n = 2 * i + h
                    pe.wait_ge(s_oh3, n + 1)
                    if not (first(i) and h == 0):
                        pe.wait_ge(s_turned3, n)
                    for q in range(H):
                        last = nc.tensor.transpose(PS[6 + q // 4][:, q % 4 * P:q % 4 * P + P], onehot[:, h * H + q, :],
                                                   ident[:, :])
                    last.then_inc(s_turn3, 1)
                    pe.wait_ge(s_turned3, n + 1)
                    if not first(i):
                        pe.wait_ge(s_took3, n - 1)
                    for q in range(H):
                        last = nc.tensor.matmul(spread_ps(h, q)[:, 0], tw[:, q * P:q * P + P], SN[:, :, 0:4],
                                                start=True, stop=True)
                    last.then_inc(s_sel3, 1)
            repeat(pe, ITERS3, pick3)
            for k, w in enumerate((4, 8, 4)):
                pe.wait_ge(s_carry, 2 * k + 1)
                nc.tensor.transpose(PS[5][0:w, 0:P], last_v[:, 0:w], ident[:, :])
                nc.tensor.transpose(PS[5][0:w, P:2 * P], last_c[:, 0:w], ident[:, :]).then_inc(s_carryp, 1)
                pe.wait_ge(s_carry, 2 * k + 2)
                nc.tensor.transpose(PS[5][:, 256:256 + w], carry_row[0:w, 0:P], ident[0:w, 0:w]).then_inc(s_carryp, 1)

        @block.scalar
        def _(act):
            done = Tally(act, s_act)

            def step(ins):
                done(ins)
                done.wait()

            def norm_begin(k, after):
                act.wait_ge(s_st, after)
                nc.scalar.activation(small[:, 2, :], small[:, 1, :], ACT.Sqrt).then_inc(s_sd, 1)
                act.wait_ge(s_nm, k + 1)
                if k:
                    act.wait_ge(s_tab[k - 1], 16)
                act.sem_inc(s_idleA, 1)

            def norm_group(k, g):
                for q in range(4):
                    b = bass.ds(4 * g + q, 1)
                    last = nc.scalar.activation(Hn[:, b, :].rearrange("p a f -> p (a f)"),
                                                X[:, b, :].rearrange("p a f -> p (a f)"), ACT.Relu,
                                                bias=small[:, 4, b], scale=small[:, 3, b])
                last.then_inc(s_h[k], 1)

            def norm_h(k, after):
                norm_begin(k, after)
                with act.Fori(0, GROUPS) as g:
                    norm_group(k, g)

            def norm_project(k, give):
                def turned_h(i):
                    act.wait_ge(s_t, GROUPS * k + i + 1)
                    nc.scalar.activation(hT, PS[7][:, :], ACT.Copy).then_inc(s_tc, 1)

                def body(g):
                    if not first(g):
                        turned_h(g - 1)
                    norm_group(k, g)
                    if not first(g):
                        give(g - 1)
                repeat(act, GROUPS, body)
                turned_h(GROUPS - 1)
                give(GROUPS - 1)

            def load(dest, source, k):
                act.dma_start(dest, source).then_inc(s_w[k], 16)

            def row(v):
                return v.partition_broadcast(P)

            load(W0_1, L0_gnn_W1, 0)
            load(WA[0:64, 1, :], L0_gnn_W2, 0)
            load(WA[64:65, 1, :], L0_gnn_b2.rearrange("(a f) -> a f", a=1), 0)
            load(b0_1, L0_gnn_b1.rearrange("(f a) -> f a", a=1), 0)
            load(g0, row(L0_gnn_gamma), 0)
            load(be0, row(L0_gnn_beta), 0)

            norm_h(0, 1)

            def mlp0(i):
                act.wait_ge(s_t, i + 1)
                nc.scalar.activation(hT, PS[7][:, :], ACT.Copy).then_inc(s_tc, 1)
                act.wait_ge(s_m0, i + 1)
                if not first(i):
                    act.wait_ge(s_e0, i)
                nc.scalar.activation(rT[0:64, :], PS[6][0:64, :], ACT.Relu, bias=b0_1).then_inc(s_r0, 1)
            act.wait_ge(s_w[0], 96)
            act.wait_ge(s_ones0, 1)
            repeat(act, GROUPS, mlp0)

            act.wait_ge(s_diff, 1)
            nc.scalar.activation(ACC[:, :, 0:D], ACC[:, :, 0:D], ACT.Square).then_inc(s_diffa, 1)
            act.wait_ge(s_diff, 2)
            step(nc.scalar.activation(small[:, 5, :], small[:, 5, :], ACT.Sqrt))
            nc.scalar.activation(small[:, 5, :], small[:, 5, :], ACT.Tanh).then_inc(s_diffa, 1)
            act.wait_ge(s_st, 2)
            nc.scalar.activation(small[:, 2, :], small[:, 1, :], ACT.Sqrt).then_inc(s_sd, 1)

            act.wait_ge(s_wdone[0], 1)
            for k in range(3):
                load(WA[:, k, :], (L1_gnn_W1[0:D, :], L1_gnn_W1[D:2 * D, :], L1_gnn_U1[0:D, :])[k], 1)
            load(W1c, L1_gnn_W1[2 * D:3 * D, :], 1)
            load(b1bc, row(L1_gnn_b1), 1)
            load(ub1bc, row(L1_gnn_ub1), 1)
            load(W1_2, L1_gnn_W2, 1)
            load(U1b, L1_gnn_U1[D:2 * D, :], 1)
            load(U2w, L1_gnn_U2, 1)
            load(ub2bc, row(L1_gnn_ub2), 1)
            load(g1, row(L1_gnn_gamma), 1)
            load(be1, row(L1_gnn_beta), 1)
            load(b1_2, L1_gnn_b2.rearrange("(f a) -> f a", a=1), 1)
            norm_h(1, 3)
            act.wait_ge(s_fold, 1)
            nc.scalar.activation(tw[:, 0:D], PS[7][:, 0:D], ACT.Copy).then_inc(s_folded, 1)
            act.wait_ge(s_fold, 2)
            nc.scalar.activation(WA[:, 12:14, :].rearrange("p a f -> p (a f)"), PS[6][:, 0:2 * D], ACT.Copy
                                 ).then_inc(s_folded, 1)

            def project1(i):
                act.wait_ge(s_t, GROUPS * 1 + i + 1)
                nc.scalar.activation(hT, PS[7][:, :], ACT.Copy).then_inc(s_tc, 1)
                for half in range(2):
                    act.wait_ge(s_p, 2 * i + half + 1)
                    act.sem_inc(s_idleA, 1)
                    for q in (2 * half, 2 * half + 1):
                        last = nc.scalar.activation(Hn[:, bass.ds(4 * i + q, 1), :].rearrange("p a f -> p (a f)"),
                                                    PS[2 + q][:, 0:D], ACT.Copy)
                    last.then_inc(s_p1a, 1)
            repeat(act, GROUPS, project1)

            def softplus_tail(v):
                o = lnp[:, 0:v.shape[1], :]
                step(nc.scalar.activation(o, v, ACT.Abs))
                step(nc.scalar.activation(o, o, ACT.Exp, scale=-1.0))
                return nc.scalar.activation(o, o, ACT.Ln, bias=1.0)

            nc.scalar.preload_act_table_set("natural_log_exp_and_others")

            def edges(i):
                for h in range(2):
                    act.wait_ge(s_turn, 2 * i + h + 1)
                    if not (first(i) and h == 0):
                        act.wait_ge(s_pre, 2 * i + h)
                    for bank, n in enumerate((512, 512, 256)):
                        last = nc.scalar.activation(tw[:, 512 * bank:512 * bank + n], PS[bank][:, 0:n], ACT.Copy)
                    last.then_inc(s_turnedc, 1)
                    act.wait_ge(s_sum1, 2 * i + h + 1)
                    if not (first(i) and h == 0):
                        act.wait_ge(s_msg, 2 * i + h)
                    softplus_tail(rows[:, h * H:h * H + H, 0:D]).then_inc(s_ln, 1)
            repeat(act, ITERS, edges, done)

            for h in range(2):
                act.wait_ge(s_sent[h], landed(0, ITERS))
            act.wait_ge(s_tables, 3)
            repeat(act, ITERS2, lambda i: message_rows(act, mybir.EngineType.Activation, i, 1))
            nc.scalar.preload_act_table_set("natural_log_exp_and_others")

            def update(i):
                if i is not GROUPS:
                    act.wait_ge(s_u1, i + 1)
                    nc.scalar.activation(hT, PS[7][:, :], ACT.Copy).then_inc(s_u1c, 1)
                if not first(i):
                    act.wait_ge(s_u3, i)
                    nc.scalar.activation(rT, PS[5][:, :], ACT.Copy).then_inc(s_u3c, 1)
                if i is not GROUPS:
                    act.wait_ge(s_zin, i + 1)
                    act.sem_inc(s_idleA, 1)
                    softplus_tail(CT[:, bass.ds(4 * i, 4), :]).then_inc(s_zl, 1)
            repeat(act, GROUPS, update, done, peel=2)
            update(GROUPS)
            act.wait_ge(s_bn, 3)
            nc.scalar.activation(lnp[:, 1, :], lnp[:, 1, :], ACT.Sqrt).then_inc(s_bnsd, 1)

            act.wait_ge(s_wdone[1], 1)
            load(WA[:, 0, :], L2_gnn_W, 2)
            for k in range(2):
                load(WA[:, 3, k:k + 1], L2_gnn_attn[0, k * D:(k + 1) * D].rearrange("(f a) -> f a", a=1), 2)
            norm_begin(2, 4)
            act.wait_ge(s_fold2, 1)
            nc.scalar.activation(tw[:, 0:D], PS[7][:, 0:D], ACT.Copy).then_inc(s_folded2, 1)
            act.wait_ge(s_fold2, 2)
            nc.scalar.activation(WA[:, 1, 0:2], PS[6][:, 0:2], ACT.Copy).then_inc(s_folded2, 1)

            def project2(i):
                for half in range(2):
                    act.wait_ge(s_p, 2 * GROUPS + 2 * i + half + 1)
                    act.sem_inc(s_idleA, 1)
                    for q in (2 * half, 2 * half + 1):
                        last = nc.scalar.activation(ACC[:, bass.ds(4 * i + q, 1), :].rearrange("p a f -> p (a f)"),
                                                    PS[2 + q][:, 0:130], ACT.Copy)
                    last.then_inc(s_p2c, 1)
            norm_project(2, project2)

            nc.scalar.preload_act_table_set("natural_log_exp_and_others")

            def attend(i):
                for u in range(U):
                    n, h, ring_of = U * i + u, u % 2, (rows, mrow)[u // 2]
                    act.wait_ge(s_mbc, n + 1)
                    nc.scalar.activation(m_all[:, h:h + 1], PS[6][:, 256:257], ACT.Copy)
                    nc.scalar.activation(negm[:, h:h + 1], PS[6][:, 256:257], ACT.Copy, scale=-1.0).then_inc(s_negm, 1)
                    act.wait_ge(s_negm, n + 1)
                    nc.scalar.activation(fade[:, h:h + 1], m_all[:, 1 - h:2 - h], ACT.Exp, bias=negm[:, h:h + 1])
                    nc.scalar.activation(wgt[:, h * H:h * H + H], lm[:, h, 0:H], ACT.Exp,
                                         bias=negm[:, h:h + 1]).then_inc(s_wgt, 1)
                    act.wait_ge(s_wgt, n + 1)
                    for j in range(h * H, h * H + H):
                        last = nc.scalar.activation(ring_of[:, j, 0:129], ring_of[:, j, 0:129], ACT.Copy,
                                                    scale=wgt[:, j:j + 1])
                    last.then_inc(s_scaled, 1)
                    nc.scalar.activation(history[:, bass.ds(n, 1)], m_all[:, h:h + 1], ACT.Copy).then_inc(s_hmax, 1)
            repeat(act, ITERS2, attend)
            act.wait_ge(s_fin2, 1)
            nc.scalar.activation(small[:, 6, :], small[:, 6, :], ACT.Exp).then_inc(s_fin2a, 1)
            act.wait_ge(s_fin2, 2)
            nc.scalar.activation(BT[:, :, :], BT[:, :, :], ACT.Exp).then_inc(s_fin2a, 1)

            act.wait_ge(s_wdone[2], 1)
            load(WA[:, 0, :], L3_gnn_weight, 3)
            for k in range(2):
                load(WA[:, 2 + k, :].rearrange("p (h c) -> p h c", h=4),
                     L3_gnn_att[0, :, 32 * k:32 * k + 32].partition_broadcast(P), 3)
            norm_begin(3, 5)

            def project3(i):
                for half in range(2):
                    act.wait_ge(s_p, 4 * GROUPS + 2 * i + half + 1)
                    act.sem_inc(s_idleA, 1)
                    for q in (2 * half, 2 * half + 1):
                        nc.scalar.activation(BT[:, bass.ds(4 * i + q, 1), :].rearrange("p a f -> p (a f)"),
                                             PS[2 + q][:, 0:D], ACT.Copy)
                        last = nc.scalar.activation(SN[:, bass.ds(4 * i + q, 1), :].rearrange("p a f -> p (a f)"),
                                                    PS[2 + q][:, D:D + 8], ACT.Copy)
                    last.then_inc(s_p3c, 1)
            norm_project(3, project3)

            def pick3(i):
                for h in range(2):
                    act.wait_ge(s_turn3, 2 * i + h + 1)
                    if not (first(i) and h == 0):
                        act.wait_ge(s_sel3, 2 * i + h)
                    nc.scalar.activation(tw[:, 0:512], PS[6][:, :], ACT.Copy)
                    nc.scalar.activation(tw[:, 512:640], PS[7][:, 0:P], ACT.Copy).then_inc(s_turned3, 1)
            repeat(act, ITERS3, pick3)
            act.wait_ge(s_alpha, 1)
            nc.scalar.activation(SI[:, 0:SC, :], SI[:, 0:SC, :], ACT.Exp).then_inc(s_alphae, 1)

        @block.vector
        def _(dve):
            done = Tally(dve, s_dve)

            def step(ins):
                done(ins)
                done.wait()

            v = nc.vector

            v.memset(accw[:, 0:1792].bitcast(I32), 0)
            v.memset(posT, 0.0)
            step(v.memset(accw[:, 1792:6760], 0.0))
            v.memset(srcL[:, CH - 1, :], NOKEY).then_inc(s_pad, 1)
            v.memset(dstL[:, CH - 1, :], NOKEY).then_inc(s_pad, 1)
            v.memset(ones[:, :], 1.0)
            v.memset(onesb[:, :], 1.0)
            v.memset(rT[64:65, :], 1.0).then_inc(s_ones0, 1)
            dve.wait_ge(s_const, 2)
            v.tensor_copy(iota[:, :], tmpp.bitcast(I32))
            step(v.tensor_copy(lane[:, :], count_i[:, :]))
            v.tensor_scalar(ident[:, :], iota[:, 0:P], lane[:, 0:1], None, ALU.is_equal)
            v.tensor_scalar(below[:, :], iota[:, 0:P], lane[:, 0:1], None, ALU.is_gt)
            for c in range(CH):
                step(v.tensor_scalar(lanes[:, c:c + 1], lane[:, :], float(c * P), None, ALU.add))

            dve.wait_ge(s_edges, 96)
            v.tensor_copy(srcF[:, :, :], srcL[:, :, :])
            v.tensor_copy(dstF[:, :, :], dstL[:, :, :])
            v.tensor_scalar(last_i, dstL[:, :, P - 1], 7, None, ALU.logical_shift_right)
            step(v.tensor_scalar(srcL, srcL, 7, None, ALU.logical_shift_right))
            v.tensor_copy(last_b, last_i)
            step(v.tensor_copy(hiF, srcL))
            v.tensor_tensor(rise, last_b, lanes[:, :], ALU.add).then_inc(s_ask0, 1)
            dve.wait_ge(s_pe0, 1)
            v.tensor_copy(hiT[:, 0:512], PS[0][:, :])
            step(v.tensor_copy(hiT[:, 512:896], PS[1][:, 0:384]))

            def pairs(pe_count, order):
                for c in range(CH):
                    last = v.tensor_scalar(gbf[:, c, :], iota[:, :], rise[:, c:c + 1], None, ALU.is_gt)
                last.then_inc(s_ask0, 1)
                dve.wait_ge(s_pe0, pe_count)
                for half in range(2):
                    step(v.tensor_scalar(kpair[:, half * HP:half * HP + HP], PS[2 + half][:, 0:HP],
                                         float(TILES - 1), None, ALU.min))
                step(v.tensor_tensor(bpair, iota[:, :], kpair, ALU.subtract))
                step(v.tensor_copy(regs[order:order + 1, 0:PAIRS], bpair[order:order + 1, :]))
                step(v.tensor_scalar(tmpp, kpair, float(P), float(LASTBASE), ALU.mult, ALU.min))
                step(v.tensor_copy(regs[order + 32:order + 33, 0:PAIRS], tmpp[order + 32:order + 33, :]))

            pairs(2, 0)
            for c in range(CH):
                last = v.tensor_scalar(sel[:, c, :], kpair, lanes[:, c:c + 1], None, ALU.is_equal)
            last.then_inc(s_ask0, 1)
            dve.wait_ge(s_pe0, 3)
            for half in range(2):
                v.tensor_copy(pay[:, half * HP:half * HP + HP, 0], PS[2 + half][:, 0:HP])
            step(v.tensor_scalar(tmpp, bpair, float(P), None, ALU.mult))
            step(v.tensor_tensor(dst_rel[:, 0:PAIRS], pay[:, :, 0], tmpp, ALU.subtract))
            v.memset(junk_hi[:, 0:1], 0.0).then_inc(s_ask0, 1)
            dve.wait_ge(s_pe0, 4)
            for half in range(2):
                step(v.tensor_copy(pay[:, half * HP:half * HP + HP, 1], PS[2 + half][:, 0:HP]))
            v.tensor_scalar(src_idx[:, 0:PAIRS], pay[:, :, 1], float(N - 1), None, ALU.min).then_inc(s_tables, 1)

            def stats(A, after):
                with dve.Fori(0, NB // GROUPS) as g:
                    for q in range(GROUPS):
                        b = bass.ds(GROUPS * g + q, 1)
                        last = v.bn_stats(st[:, b, :].rearrange("p a f -> p (a f)"),
                                          A[:, b, :].rearrange("p a f -> p (a f)"))
                    last.then_inc(s_bns, 1)
                dve.wait_ge(s_bns, NB // GROUPS * after)
                v.tensor_tensor(small[:, 0, :], st[:, :, 1], st[:, :, 4], ALU.add)
                v.tensor_tensor(small[:, 1, :], st[:, :, 2], st[:, :, 5], ALU.add)
                step(v.tensor_tensor(small[:, 2, :], st[:, :, 1], st[:, :, 4], ALU.subtract))
                step(v.tensor_tensor(small[:, 2, :], small[:, 2, :], small[:, 2, :], ALU.mult))
                v.tensor_scalar(small[:, 0, :], small[:, 0, :], 0.5, None, ALU.mult)
                step(v.tensor_scalar(small[:, 2, :], small[:, 2, :], 0.25, EPS, ALU.mult, ALU.add))
                v.scalar_tensor_tensor(small[:, 1, :], small[:, 1, :], 1.0 / D, small[:, 2, :], ALU.mult, ALU.add
                                       ).then_inc(s_st, 1)
                dve.wait_ge(s_sd, after)
                step(v.reciprocal(small[:, 3, :], small[:, 2, :]))
                step(v.scalar_tensor_tensor(small[:, 4, :], small[:, 0, :], -1.0, small[:, 3, :], ALU.mult, ALU.mult))

            def norm_ready():
                v.memset(small[:, 14, 0:1], 0.0).then_inc(s_nm, 1)

            dve.wait_ge(s_x, 32)
            stats(X, 1)
            norm_ready()

            def block_rows(to, at, n):
                v.tensor_tensor(to, iota[:, 0:BLOCKS].unsqueeze(1).to_broadcast([P, n, BLOCKS]),
                                hiT[:, bass.ds(at, n)].unsqueeze(2).to_broadcast([P, n, BLOCKS]),
                                ALU.is_equal).then_inc(s_oh8, 1)

            def histogram(i):
                for q in range(2):
                    if not first(i):
                        dve.wait_ge(s_hist, 2 * i + q - 1)
                    block_rows(oh8[q], HB * (2 * i + q), HB)
            repeat(dve, STEPS // 2, histogram)
            dve.wait_ge(s_hist, STEPS)
            step(v.tensor_reduce(cnt_hi, PS[4][:, 0:HB * BLOCKS].rearrange("p (t h) -> p h t", h=BLOCKS), AX, ALU.add))
            step(v.memset(junk_hi, 1.0))
            step(v.tensor_tensor_scan(cum_hi, junk_hi, cnt_hi, 0.0, ALU.mult, ALU.add))
            step(v.tensor_tensor(base_hi, cum_hi, cnt_hi, ALU.subtract))

            def put(A, i, sem_put, turned_sem, k=0):
                if not first(i):
                    dve.wait_ge(turned_sem, GROUPS * k + i)
                v.tensor_scalar(group.rearrange("p (a f) -> p a f", a=4), A[:, bass.ds(4 * i, 4), 0:D], 1.0, None,
                                ALU.mult).then_inc(sem_put, 1)

            v.memset(rows[:, :, D:ROW], 1.0)
            step(v.memset(ACC[:, :, :], 0.0))

            def block_numbers_at(at, reg_row=64):
                return nc.values_load_multi_w_load_instructions(
                    regs[reg_row:reg_row + 1, bass.ds(at, H)], engines=[mybir.EngineType.DVE],
                    min_val=0, max_val=BLOCKS - 1, skip_runtime_bounds_check_because=IN_RANGE)[1]

            def sum_blocks(i, h, seg, acc, reg_row):
                blocks = block_numbers_at(R * i + h * H, reg_row)
                dve.wait_ge(seg, 2 * i + h + 1)
                for q in range(H):
                    to = ACC[:, bass.ds(blocks[q], 1), 0:129].rearrange("p a f -> p (a f)")
                    last = v.tensor_tensor(to, to, seg_ps(h, q), ALU.add)
                    if q < H - 1:
                        step(last)
                last.then_inc(acc, 1)
                dve.wait_ge(acc, 2 * i + h + 1)

            def one_hots(h, keys, ready):
                v.tensor_tensor(onehot[:, h * H:h * H + H, :], iota[:, 0:P].unsqueeze(1).to_broadcast([P, H, P]),
                                keys.unsqueeze(2).to_broadcast([P, H, P]), ALU.is_equal).then_inc(ready, 1)

            def place(i):
                dve.wait_ge(s_ahead, i + 1)
                step(v.tensor_tensor(tpos, PS[4][:, 0:R * BLOCKS].rearrange("p (t h) -> p t h", h=BLOCKS),
                                     base_hi.unsqueeze(1).to_broadcast([P, R, BLOCKS]), ALU.add))
                done(v.tensor_tensor(base_hi, base_hi, PS[5][:, 0:BLOCKS], ALU.add))
                step(v.tensor_tensor(tpos, tpos, ohp, ALU.mult))
                v.tensor_reduce(posT[:, bass.ds(R * i, R)], tpos, AX, ALU.add).then_inc(s_placed, 1)
                dve.wait_ge(s_placed, i + 1)

            def sum0(i):
                block_rows(ohp, R * i, R)
                for (_, h), before in halves(i):
                    one_hots(h, dst_rel[:, bass.ds(R * i + h * H, H)], s_oh0)
                    if before:
                        sum_blocks(*before, s_seg0, s_acc0, 0)
                place(i)

            def sum0_mlp0(i):
                dve.wait_ge(s_h[0], i + 1)
                put(Hn, i, s_put, s_t)
                sum0(i)
                dve.wait_ge(s_e0, i + 1)
                v.tensor_scalar(BT[:, bass.ds(4 * i, 4), :].rearrange("p a f -> p (a f)"), PS[7][:, :], 0.2, None,
                                ALU.mult).then_inc(s_e0c, 1)
            repeat(dve, GROUPS, sum0_mlp0, done, peel=2)
            repeat(dve, ITERS, sum0, done, begin=GROUPS)
            sum_blocks(ITERS - 1, 1, s_seg0, s_acc0, 0)

            step(v.tensor_copy(cnt_dst, ACC[:, :, D]))
            step(v.tensor_scalar(small[:, 5, :], cnt_dst, 1.0, None, ALU.max))
            step(v.reciprocal(small[:, 5, :], small[:, 5, :]))
            step(v.tensor_tensor(ACC[:, :, 0:D], ACC[:, :, 0:D], spread(small[:, 5, :], NB), ALU.mult))
            v.tensor_tensor(ACC[:, :, 0:D], ACC[:, :, 0:D], Hn[:, :, :], ALU.subtract).then_inc(s_diff, 1)
            dve.wait_ge(s_diffa, 1)
            v.tensor_reduce(small[:, 5, :], ACC[:, :, 0:D], AX, ALU.add).then_inc(s_diff, 1)
            dve.wait_ge(s_diffa, 2)
            step(v.tensor_tensor(BT[:, :, :], BT[:, :, :], spread(small[:, 5, :], NB), ALU.mult))
            step(v.tensor_tensor(BT[:, :, :], BT[:, :, :], Hn[:, :, :], ALU.add))
            stats(BT, 2)
            step(v.tensor_tensor(BT[:, :, :], BT[:, :, :], spread(small[:, 3, :], NB), ALU.mult))
            step(v.tensor_tensor(BT[:, :, :], BT[:, :, :], spread(small[:, 4, :], NB), ALU.add))
            step(v.tensor_tensor(BT[:, :, :], BT[:, :, :], over(g0, NB), ALU.mult))
            step(v.tensor_tensor(BT[:, :, :], BT[:, :, :], over(be0, NB), ALU.add))
            step(v.tensor_tensor(X[:, :, :], X[:, :, :], BT[:, :, :], ALU.add))
            v.memset(small[:, 14, 0:1], 0.0).then_inc(s_wdone[0], 1)
            v.memset(small[:, 14, 1:2], 0.0).then_inc(s_xnew[0], 1)

            stats(X, 3)
            norm_ready()

            for c in range(CH):
                last = v.tensor_scalar(sel[:, c, :], kpair, lanes[:, c:c + 1], None, ALU.is_equal)
            last.then_inc(s_ask0, 1)
            dve.wait_ge(s_pe0, 5)
            v.tensor_copy(posF[:, 0:4, :].rearrange("p c e -> p (c e)"), PS[0][:, :])
            v.tensor_copy(posF[:, 4:7, :].rearrange("p c e -> p (c e)"), PS[1][:, 0:384]).then_inc(s_ask0, 1)
            dve.wait_ge(s_pe0, 6)
            step(v.tensor_scalar(tmpp, dst_rel[:, 0:PAIRS], -1.0, None, ALU.is_gt))
            step(v.tensor_scalar(bpair, dst_rel[:, 0:PAIRS], float(P), None, ALU.is_lt))
            step(v.tensor_tensor(tmpp, tmpp, bpair, ALU.mult))
            step(v.tensor_scalar(bpair, tmpp, float(-NOWHERE), float(NOWHERE), ALU.mult, ALU.add))
            for half in range(2):
                part = slice(half * HP, half * HP + HP)
                step(v.tensor_tensor(tmpp[:, part], tmpp[:, part], PS[2 + half][:, 0:HP], ALU.mult))
            step(v.tensor_tensor(tmpp, tmpp, bpair, ALU.add))
            step(v.tensor_copy(pos_idx[:, 0:PAIRS], tmpp))
            v.memset(junk_hi[:, 0:1], 0.0).then_inc(s_tables, 1)

            for c in range(CH):
                step(v.tensor_scalar(xlast[:, c:c + 1], lanes[:, c:c + 1], float(P), float(P - 1), ALU.mult, ALU.add))
                step(v.tensor_scalar(junk_hi, cum_hi, xlast[:, c:c + 1], None, ALU.is_le))
                step(v.tensor_reduce(last_b[:, c:c + 1], junk_hi, AX, ALU.add))
            step(v.tensor_tensor(rise, last_b, lanes[:, :], ALU.add))
            pairs(7, 64)
            v.memset(regs[64:65, PAIRS:W2], BLOCKS - 1)
            v.memset(regs[96:97, PAIRS:W2], 0)
            v.memset(s_shift[:, PAIRS:W2], -30000.0)
            v.memset(first_block[:, 2 * ITERS:], BLOCKS - 1)
            v.tensor_copy(first_block[:, 0:2 * ITERS], bpair.rearrange("p (n q) -> p n q", q=H)[:, :, 0])
            step(v.tensor_scalar(tmpp, kpair, float(TILES - 1), None, ALU.is_equal))
            step(v.tensor_scalar(junk_hi[:, 0:1], lane[:, 0:1], float(P - REST), -30000.0, ALU.is_lt, ALU.mult))
            step(v.tensor_scalar(tmpp, tmpp, junk_hi[:, 0:1], None, ALU.mult))
            step(v.scalar_tensor_tensor(s_shift[:, 0:PAIRS], bpair, float(P), tmpp, ALU.mult, ALU.add))

            step(v.memset(group[:, 0:1], 0.0))

            def project1(i):
                dve.wait_ge(s_h[1], i + 1)
                put(Hn, i, s_put, s_t, 1)
                if not first(i):
                    take1(i - 1)

            def take1(i):
                for half in range(2):
                    dve.wait_ge(s_p1a, 2 * i + half + 1)
                    for q in (2 * half, 2 * half + 1):
                        at = bass.ds(4 * i + q, 1)
                        v.tensor_tensor(BT[:, at, :].rearrange("p a f -> p (a f)"), PS[2 + q][:, D:2 * D], b1bc, ALU.add)
                        last = v.tensor_tensor(CT[:, at, :].rearrange("p a f -> p (a f)"), PS[2 + q][:, 2 * D:3 * D],
                                               ub1bc, ALU.add)
                    last.then_inc(s_p1c, 1)
            repeat(dve, GROUPS, project1)
            take1(GROUPS - 1)
            step(v.memset(mrow[:, :, D:ROW], 1.0))

            def edges(i):
                for (_, h), before in halves(i):
                    if before:
                        one_hots(h, dst_rel[:, bass.ds(R * i + h * H, H)], s_oh1)
                        messages_of(*before)
                    dve.wait_ge(s_row[h], landed(1, i + 1))
                    dve.wait_ge(s_pre, 2 * i + h + 1)
                    v.tensor_tensor(rows[:, h * H:h * H + 4, 0:D], rows[:, h * H:h * H + 4, 0:D],
                                    PS[3 + 2 * h][:, :].rearrange("p (q f) -> p q f", f=D), ALU.add)
                    v.tensor_tensor(rows[:, h * H + 4, 0:D], rows[:, h * H + 4, 0:D], pre_ps(h, 4), ALU.add
                                    ).then_inc(s_sum1, 1)

            def messages_of(i, h):
                part = slice(h * H, h * H + H)
                if not first(i):
                    dve.wait_ge(s_sent[h], landed(0, i))
                v.tensor_scalar(mrow[:, part, D + 1:D + 3], pay[:, bass.ds(R * i + h * H, H), :], 1.0, None, ALU.mult)
                dve.wait_ge(s_sum1, 2 * i + h + 1)
                dve.wait_ge(s_ln, 2 * i + h + 1)
                v.scalar_tensor_tensor(mrow[:, part, 0:D], rows[:, part, 0:D], 0.0, lnp[:, :, :], ALU.max, ALU.add
                                       ).then_inc(s_msg, 1)
            one_hots(0, dst_rel[:, 0:H], s_oh1)
            v.memset(ACC[:, :, :], 0.0)
            dve.wait_ge(s_tab[1], 16)
            step(v.memset(ACC2, 0.0))
            repeat(dve, ITERS, edges)
            messages_of(ITERS - 1, 1)

            dve.wait_ge(s_msg, 2 * ITERS)
            v.memset(small[:, 14, 0:1], 0.0).then_inc(s_tables, 1)

            def add_up(i, u, acc, faded):
                n, h = U * i + u, u % 2
                blocks = block_numbers_at(H * n)

                def add(q):
                    to = (ACC2 if not faded and (h + q) % 2 else ACC)[:, bass.ds(blocks[q], 1), 0:129].rearrange(
                        "p a f -> p (a f)")
                    if q == 0 and faded:
                        done(v.scalar_tensor_tensor(to, to, fade[:, h:h + 1], seg_ps(h, 0), ALU.mult, ALU.add))
                    elif q < H - 1:
                        done(v.tensor_tensor(to, to, seg_ps(h, q), ALU.add))
                    else:
                        v.tensor_tensor(to, to, seg_ps(h, q), ALU.add).then_inc(acc, 1)
                return add

            def add_last(seg, acc, faded):
                for u in (U - 2, U - 1):
                    add = add_up(ITERS2 - 1, u, acc, faded)
                    dve.wait_ge(seg, U * ITERS2 - U + u + 1)
                    for q in range(H):
                        add(q)
                        if q < H - 1:
                            done.wait()
                    dve.wait_ge(acc, U * ITERS2 - U + u + 1)

            def two_before(i, u):
                return (i, u - 2) if u >= 2 else None if first(i) else (i - 1, u + 2)

            def sum1(i):
                for u in range(U):
                    n, h = U * i + u, u % 2
                    part = slice(h * H, h * H + H)
                    ring_of = (rows, mrow)[u // 2]
                    dve.wait_ge(s_edge[u], loaded(i + 1, u))
                    if not (first(i) and u < 2):
                        dve.wait_ge(s_oh1s, n - 1)
                    v.tensor_tensor(key[:, part], ring_of[:, part, D + 2], s_shift[:, bass.ds(H * n, H)], ALU.subtract)
                    v.tensor_scalar(payS[:, bass.ds(H * n, H), :], ring_of[:, part, D + 1:D + 3], 1.0, None, ALU.mult
                                    ).then_inc(s_took, 1)
                    before = two_before(i, u)
                    if before:
                        add = add_up(*before, s_acc1, False)
                        dve.wait_ge(s_seg1, n - 1)
                        if not (first(i) and u == 2):
                            dve.wait_ge(s_acc1, n - 2)
                    for q in range(H):
                        if before:
                            if q > 1:
                                done.wait(but=1)
                            add(q)
                        if q == 0:
                            dve.wait_ge(s_took, n + 1)
                        if q < OH_DVE:
                            last = v.tensor_scalar(onehot[:, h * H + q, :], iota[:, 0:P],
                                                   key[:, h * H + q:h * H + q + 1], None, ALU.is_equal)
                            if q == OH_DVE - 1:
                                last.then_inc(s_oh1d, 1)
            repeat(dve, ITERS2, sum1, done, peel=2)
            dve.wait_ge(s_acc1, U * ITERS2 - 2)
            add_last(s_seg1, s_acc1, False)
            step(v.tensor_tensor(ACC[:, 0:BLOCKS, 0:129], ACC[:, 0:BLOCKS, 0:129], ACC2, ALU.add))

            cnt_src = small[:, 8, :]
            step(v.tensor_copy(cnt_src, ACC[:, :, D]))

            def terms(i):
                for q in range(4):
                    to = CT[:, bass.ds(4 * i + q, 1), :].rearrange("p a f -> p (a f)")
                    last = v.scalar_tensor_tensor(to, b2Ubc, cnt_src[:, bass.ds(4 * i + q, 1)], to, ALU.mult, ALU.add)
                done(last)

            def update(i):
                if i is not GROUPS:
                    at = CT[:, bass.ds(4 * i, 4), :].rearrange("p a f -> p (a f)")
                    dve.wait_ge(s_u2, i + 1)
                    done.wait()
                    v.tensor_tensor(at, at, PS[6][:, :], ALU.add).then_inc(s_zin, 1)
                    if i is not GROUPS - 1:
                        put(ACC, i + 1, s_put1, s_u1)
                if not first(i):
                    dve.wait_ge(s_u4, i)
                    v.tensor_tensor(BT[:, bass.ds(4 * i - 4, 4), :], PS[4][:, :].rearrange("p (a f) -> p a f", a=4),
                                    over(ub2bc, 4), ALU.add).then_inc(s_u4c, 1)
                if i is not GROUPS:
                    dve.wait_ge(s_zin, i + 1)
                    dve.wait_ge(s_zl, i + 1)
                    if not first(i):
                        dve.wait_ge(s_u3, i)
                    v.scalar_tensor_tensor(zgroup, at, 0.0, lnp[:, 0:4, :].rearrange("p a f -> p (a f)"), ALU.max,
                                           ALU.add).then_inc(s_z1, 1)
                    if i is not GROUPS - 1:
                        terms(i + 1)
            put(ACC, 0, s_put1, s_u1)
            terms(0)
            repeat(dve, GROUPS - 1, update, done)
            update(GROUPS - 1)
            update(GROUPS)
            dve.wait_ge(s_u4c, GROUPS)

            real = small[:, 9, 0:1]
            step(v.tensor_scalar(real, lane[:, :], float(TAIL), None, ALU.is_lt))

            def node_mean(A, order):
                step(v.tensor_scalar(A[:, BLOCKS - 1, :], A[:, BLOCKS - 1, :], real, None, ALU.mult))
                v.tensor_reduce(lnp[:, 0, :], A[:, 0:BLOCKS, :].rearrange("p b f -> p f b"), AX, ALU.add).then_inc(s_bn, 1)
                dve.wait_ge(s_bnsum, order)

            node_mean(BT, 1)
            step(v.tensor_scalar(lnp[:, 2, :], PS[0][:, 0:D], 1.0 / N, None, ALU.mult))
            step(v.tensor_tensor(BT[:, :, :], BT[:, :, :], over(lnp[:, 2, :], NB), ALU.subtract))
            step(v.tensor_tensor(CT[:, :, :], BT[:, :, :], BT[:, :, :], ALU.mult))
            node_mean(CT, 2)
            v.tensor_scalar(lnp[:, 1, :], PS[0][:, 0:D], 1.0 / N, EPS, ALU.mult, ALU.add).then_inc(s_bn, 1)
            dve.wait_ge(s_bnsd, 1)
            step(v.reciprocal(lnp[:, 1, :], lnp[:, 1, :]))
            step(v.tensor_tensor(lnp[:, 1, :], lnp[:, 1, :], g1, ALU.mult))
            step(v.tensor_tensor(BT[:, :, :], BT[:, :, :], over(lnp[:, 1, :], NB), ALU.mult))
            step(v.tensor_tensor(BT[:, :, :], BT[:, :, :], over(be1, NB), ALU.add))
            step(v.tensor_tensor(X[:, :, :], X[:, :, :], BT[:, :, :], ALU.add))
            v.memset(small[:, 14, 0:1], 0.0).then_inc(s_wdone[1], 1)
            v.memset(small[:, 14, 1:2], 0.0).then_inc(s_xnew[1], 1)

            step(v.tensor_copy(dst_idx[:, 0:PAIRS], payS[:, 0:PAIRS, 0]))
            step(v.tensor_tensor(src_relS[:, 0:PAIRS], payS[:, 0:PAIRS, 1], s_shift[:, 0:PAIRS], ALU.subtract))
            step(v.tensor_scalar(maskS[:, 0:PAIRS], src_relS[:, 0:PAIRS], -1.0, None, ALU.is_gt))
            step(v.tensor_scalar(payS[:, 0:PAIRS, 0], src_relS[:, 0:PAIRS], float(P), None, ALU.is_lt))
            step(v.tensor_tensor(maskS[:, 0:PAIRS], maskS[:, 0:PAIRS], payS[:, 0:PAIRS, 0], ALU.mult))
            step(v.tensor_scalar(maskS[:, 0:PAIRS], maskS[:, 0:PAIRS], -1.0, BIG, ALU.add, ALU.mult))
            v.memset(dst_idx[:, PAIRS:W2], 0)
            v.memset(src_relS[:, PAIRS:W2], -1.0)
            v.memset(maskS[:, PAIRS:W2], -BIG)
            v.memset(small[:, 14, 0:1], 0.0).then_inc(s_tables, 1)
            v.memset(scan_idx, 0)
            v.memset(scan_dst, NOKEY)
            v.memset(scan_prev, -1).then_inc(s_scanfree, 1)
            stats(X, 4)
            norm_ready()

            def project2(i):
                dve.wait_ge(s_h[2], i + 1)
                put(Hn, i, s_put, s_t, 2)
            repeat(dve, GROUPS, project2)
            dve.wait_ge(s_p2c, 2 * GROUPS)
            step(v.tensor_copy(small[:, 8, :], ACC[:, :, D]))
            v.memset(ACC[:, :, D], 1.0).then_inc(s_store2, 1)
            step(v.memset(small[:, 10:12, :], 0.0))
            v.memset(lm[:, 0, H:H + 1], -BIG)
            step(v.memset(m_all[:, 1:2], -BIG))
            dve.wait_ge(s_tab[2], 16)
            step(v.memset(ACC[:, :, :], 0.0))
            dve.wait_ge(s_sc2, 32)

            def block_scores(i, u):
                n, h = U * i + u, u % 2
                blocks = block_numbers_at(H * n)

                def score(q):
                    done(v.scalar_tensor_tensor(lnp[:, q, :], iota[:, 0:P], src_relS[:, bass.ds(H * n + q, 1)],
                                                BT[:, bass.ds(blocks[q], 1), :].rearrange("p a f -> p (a f)"),
                                                ALU.is_equal, ALU.mult, accum_out=sv[:, h * H + q:h * H + q + 1]))
                return score

            def attend(i):
                for u in range(U):
                    n, h = U * i + u, u % 2
                    part = slice(h * H, h * H + H)
                    before = two_before(i, u)
                    done.wait()
                    dve.wait_ge(s_row[u], landed(2, i + 1, u))
                    done(v.tensor_tensor(sv[:, part], sv[:, part], (rows, mrow)[u // 2][:, part, D + 1], ALU.add))
                    if before:
                        dve.wait_ge(s_seg2, n - 1)
                    one_hots(h, src_relS[:, bass.ds(H * n, H)], s_oh2)
                    done.wait()
                    step(v.scalar_tensor_tensor(lm[:, h, 0:H], sv[:, part], 0.2, sv[:, part], ALU.mult, ALU.max))
                    step(v.tensor_tensor(lm[:, h, 0:H], lm[:, h, 0:H], maskS[:, bass.ds(H * n, H)], ALU.add))
                    v.tensor_reduce(lm[:, 1 - h, H:H + 1], lm[:, h, :], AX, ALU.max).then_inc(s_mx, 1)
                    score = block_scores(i, u + 1)
                    if before:
                        add = add_up(*before, s_acc2, True)
                    for q in range(H):
                        if before:
                            if q:
                                done.wait(but=1)
                            add(q)
                        score(q)
                    if before:
                        dve.wait_ge(s_acc2, n - 1)
                    dve.wait_ge(s_mxt, n + 1)
                    v.tensor_reduce(m_run[0:1, h:h + 1], PS[6][0:1, 0:P], AX, ALU.max).then_inc(s_mnew, 1)
            score = block_scores(0, 0)
            for q in range(H):
                score(q)
            repeat(dve, ITERS2, attend, done, peel=2)
            add_last(s_seg2, s_acc2, True)
            dve.wait_ge(s_hmax, U * ITERS2)
            by_half = ctw[:, 0:U * ITERS2]
            step(v.tensor_scalar(by_half, first_block[:, :], lane[:, 0:1], None, ALU.is_le))
            step(v.tensor_scalar(by_half, by_half, -1.0, BIG, ALU.add, ALU.mult))
            step(v.tensor_tensor(by_half, by_half, history, ALU.add))
            v.tensor_reduce(m_col, by_half, AX, ALU.max).then_inc(s_mcol, 1)
            dve.wait_ge(s_mrow, 1)
            step(v.tensor_copy(m_block, PS[5][:, 0:NB]))

            step(v.tensor_scalar(small[:, 6, :], m_block, -1.0, m_all[:, 1:2], ALU.mult, ALU.add))
            v.tensor_scalar(small[:, 6, :], small[:, 6, :], 87.0, 0.0, ALU.min, ALU.max).then_inc(s_fin2, 1)
            dve.wait_ge(s_fin2a, 1)
            step(v.scalar_tensor_tensor(small[:, 6, :], small[:, 6, :], 9e-15, ACC[:, :, D], ALU.mult, ALU.add))
            step(v.reciprocal(small[:, 6, :], small[:, 6, :]))
            step(v.tensor_tensor(BT[:, :, :], ACC[:, :, 0:D], spread(small[:, 6, :], NB), ALU.mult))
            step(v.tensor_scalar(CT[:, :, :], BT[:, :, :], 0.0, None, ALU.max))
            v.tensor_scalar(BT[:, :, :], BT[:, :, :], 0.0, None, ALU.min).then_inc(s_fin2, 1)
            dve.wait_ge(s_fin2a, 2)
            step(v.scalar_tensor_tensor(CT[:, :, :], BT[:, :, :], -1.0, CT[:, :, :], ALU.add, ALU.add))
            step(v.tensor_tensor(X[:, :, :], X[:, :, :], CT[:, :, :], ALU.add))
            v.memset(small[:, 14, 0:1], 0.0).then_inc(s_wdone[2], 1)
            v.memset(small[:, 14, 1:2], 0.0).then_inc(s_xnew[2], 1)

            stats(X, 5)
            norm_ready()
            v.memset(fill, 0.0).then_inc(s_zero, 1)
            dve.wait_ge(s_w[3], 48)
            for k in range(2):
                step(v.tensor_tensor(WA[:, 4, :], WA[:, 0, :], WA[:, 2 + k, :], ALU.mult))
                step(v.tensor_reduce(WA[:, 1, 4 * k:4 * k + 4], WA[:, 4, :].rearrange("p (h c) -> p h c", h=4), AX,
                                     ALU.add))
            v.memset(small[:, 14, 0:1], 0.0).then_inc(s_folded3, 1)

            def project3(i):
                dve.wait_ge(s_h[3], i + 1)
                put(Hn, i, s_put, s_t, 3)
            repeat(dve, GROUPS, project3)

            v.tensor_scalar(upto, iota[:, 0:P], lane[:, 0:1], None, ALU.is_ge).then_inc(s_cum, 1)
            dve.wait_ge(s_cump, 1)
            nodes = slice(0, BLOCKS)
            total, cum, has = small[:, 10, nodes], small[:, 11, nodes], small[:, 5, nodes]
            start_f, end_f, one_row = small[:, 2, nodes], small[:, 3, nodes], small[:, 4, nodes]
            step(v.memset(one_row, 1.0))
            step(v.tensor_copy(total, PS[6][:, 64:64 + BLOCKS]))
            step(v.tensor_tensor_scan(cum, one_row, total, 0.0, ALU.mult, ALU.add))
            step(v.tensor_tensor(cum, cum, total, ALU.subtract))
            step(v.tensor_tensor(end_f, PS[6][:, 0:BLOCKS], cum, ALU.add))
            step(v.tensor_tensor(start_f, end_f, cnt_dst[:, nodes], ALU.subtract))
            step(v.tensor_scalar(end_f, end_f, -1.0, 0.0, ALU.add, ALU.max))
            step(v.tensor_copy(end_idx[:, nodes], end_f))
            step(v.tensor_scalar(has, cnt_dst[:, nodes], 1.0, None, ALU.min))
            step(v.tensor_tensor(start_f, start_f, has, ALU.mult))
            step(v.tensor_scalar(end_f, has, float(-NOWHERE), float(NOWHERE), ALU.mult, ALU.add))
            step(v.tensor_tensor(start_f, start_f, end_f, ALU.add))
            step(v.tensor_copy(start_idx[:, nodes], start_f))

            dve.wait_ge(s_scan, 64)
            dve.wait_ge(s_prev, 48)
            step(v.tensor_tensor(cont, scan_dst, scan_prev, ALU.is_equal))
            step(v.tensor_scalar(contneg, cont, -1.0, 1e38, ALU.add, ALU.mult))
            step(v.tensor_reduce(all_cont, cont, AX, ALU.min))
            dve.wait_ge(s_p3c, 2 * GROUPS)
            step(v.memset(mrow_flat[:, 416:1248], 0.0))

            for part, op, by in ((lo3, ALU.bitwise_and, P - 1), (hi3, ALU.logical_shift_right, 7)):
                step(v.tensor_scalar(part_i, scan_idx[:, SG // 2:SG], by, None, op))
                step(v.tensor_copy(part, part_i))

            def select(i, h):
                dve.wait_ge(s_sel3, 2 * i + h + 1)
                done.wait()
                for q in range(0, H, 2):
                    n = min(2, H - q)
                    last = v.tensor_tensor(picked[:, q:q + n], spread_ps(h, q, n),
                                           hi_oh[:, h * H + q:h * H + q + n, :].unsqueeze(3).to_broadcast([P, n, NB, 4]),
                                           ALU.mult)
                last.then_inc(s_took3, 1)
                dve.wait_ge(s_took3, 2 * i + h + 1)
                done(v.tensor_reduce(SI[:, bass.ds(SG // 2 + R * i + h * H, H), :],
                                     picked.rearrange("p q b f -> p q f b"), AX, ALU.add))

            def take(i):
                for (_, h), before in halves(i):
                    shape = [P, H, NB]
                    v.tensor_tensor(hi_oh[:, h * H:h * H + H, :], iota[:, 0:NB].unsqueeze(1).to_broadcast(shape),
                                    hi3[:, bass.ds(R * i + h * H, H)].unsqueeze(2).to_broadcast(shape), ALU.is_equal)
                    one_hots(h, lo3[:, bass.ds(R * i + h * H, H)], s_oh3)
                    if before:
                        select(*before)
                    dve.wait_ge(s_row[h], landed(3, i + 1))
                    v.tensor_scalar(SI[:, bass.ds(R * i + h * H, H), :], g4[:, h * H:h * H + H, :], 1.0, None, ALU.mult
                                    ).then_inc(s_got3, 1)
            repeat(dve, ITERS3, take, done, peel=2)
            select(ITERS3 - 1, 1)
            done.wait()
            dve.wait_ge(s_got3, 2 * ITERS3)

            def segments(to, of, w, factor, whole, op0, op1, start, order):
                for c in range(w):
                    step(v.tensor_tensor_scan(to[:, :, c], factor, of[:, 0:SC, c], start, op0, op1))
                step(v.tensor_copy(last_v[:, 0:w], to[:, SC - 1, :]))
                v.tensor_copy(last_c[:, 0:w], whole.to_broadcast([P, w])).then_inc(s_carry, 1)
                dve.wait_ge(s_carryp, 2 * order + 1)
                step(v.tensor_copy(carry_row[0:w, P:3 * P], PS[5][0:w, 0:2 * P]))
                step(v.tensor_tensor_scan(carry_row[0:w, P:2 * P], carry_row[0:w, 2 * P:3 * P], carry_row[0:w, P:2 * P],
                                          start, op0, op1))
                step(v.memset(carry_row[0:w, 0:1], start))
                v.tensor_scalar(carry_row[0:w, 1:P], carry_row[0:w, P:2 * P - 1], 1.0, None, ALU.mult
                                ).then_inc(s_carry, 1)
                dve.wait_ge(s_carryp, 2 * order + 2)
                step(v.tensor_copy(last_v[:, 0:w], PS[5][:, 256:256 + w]))
                for c in range(w):
                    step(v.tensor_tensor_scan(to[:, :, c], factor, of[:, 0:SC, c], last_v[:, c:c + 1], op0, op1))

            step(v.tensor_scalar(all_neg, all_cont, -1.0, 1e38, ALU.add, ALU.mult))
            segments(MX, SI, 4, contneg, all_neg, ALU.add, ALU.max, -1e38, 0)
            v.memset(small[:, 14, 0:1], 0.0).then_inc(s_scanned, 1)
            dve.wait_ge(s_mxnode, 16 * BLOCKS)
            target = SN[:, :, 4:8]
            step(v.tensor_tensor(mx_node, mx_node, target, ALU.add))
            step(v.tensor_copy(fill_node[:, :, 0:4], target))
            v.scalar_tensor_tensor(fill_node[:, :, 4:8], mx_node, 0.2, mx_node, ALU.mult, ALU.max).then_inc(s_fill, 1)
            dve.wait_ge(s_fillback, 16)
            segments(FO, fill, 8, cont, all_cont, ALU.mult, ALU.add, 0.0, 1)
            edges_si = SI[:, 0:SC, :]
            step(v.tensor_tensor(edges_si, edges_si, FO[:, :, 0:4], ALU.add))
            step(v.scalar_tensor_tensor(edges_si, edges_si, 0.2, edges_si, ALU.mult, ALU.max))
            step(v.tensor_tensor(edges_si, edges_si, FO[:, :, 4:8], ALU.subtract))
            v.tensor_scalar(edges_si, edges_si, 0.0, None, ALU.min).then_inc(s_alpha, 1)
            dve.wait_ge(s_alphae, 1)
            dve.wait_ge(s_segmax, 16)
            segments(MX, SI, 4, cont, all_cont, ALU.mult, ALU.add, 0.0, 2)
            v.memset(small[:, 14, 0:1], 0.0).then_inc(s_scanned, 1)
            dve.wait_ge(s_sumnode, 16 * BLOCKS)
            step(v.tensor_scalar(mx_node, sum_node, 1e-16, None, ALU.add))
            step(v.reciprocal(mx_node, mx_node))
            step(v.tensor_tensor(sum_node, sum_node, mx_node, ALU.mult))
            step(v.tensor_tensor(sum_node[:, nodes, :], sum_node[:, nodes, :], has.unsqueeze(2).to_broadcast([P, BLOCKS, 4]),
                                 ALU.mult))
            heads = BT[:, :, :].rearrange("p b (h c) -> p (b h) c", h=4)
            step(v.tensor_tensor(heads, heads, sum_node.rearrange("p b h -> p (b h)").unsqueeze(2)
                                 .to_broadcast([P, NB * 4, 32]), ALU.mult))
            step(v.tensor_tensor(X[:, :, :], X[:, :, :], BT[:, :, :], ALU.add))
            v.memset(small[:, 14, 1:2], 0.0).then_inc(s_xnew[3], 1)


_INS = ['x', 'src', 'dst', 'edge_attr_128', 'L0_gnn_W1', 'L0_gnn_b1', 'L0_gnn_W2', 'L0_gnn_b2', 'L0_gnn_gamma', 'L0_gnn_beta', 'L1_gnn_W1', 'L1_gnn_b1', 'L1_gnn_W2', 'L1_gnn_b2', 'L1_gnn_U1', 'L1_gnn_ub1', 'L1_gnn_U2', 'L1_gnn_ub2', 'L1_gnn_gamma', 'L1_gnn_beta', 'L2_gnn_W', 'L2_gnn_attn', 'L3_gnn_weight', 'L3_gnn_att']
_OUTS = [((6250, 128), 'float32')]


def kernel(**inputs):
    import numpy as _np
    import concourse.bacc as _bacc
    from concourse import mybir as _mybir
    from concourse.bass_utils import run_bass_kernel_spmd as _run

    nc = _bacc.Bacc("TRN2", target_bir_lowering=False, num_devices=1)
    arrays, args = {}, {}
    for name in _INS:
        a = _np.ascontiguousarray(inputs[name])
        arrays[f"in_{name}_dram"] = a
        args[name] = nc.dram_tensor(f"in_{name}_dram", a.shape, _mybir.dt.from_np(a.dtype), kind="ExternalInput").ap()
    for i, (shape, dtype) in enumerate(_OUTS):
        dt = _mybir.dt.from_np(_np.dtype(dtype))
        args["out"] = nc.dram_tensor(f"out_{i}_dram", shape, dt, kind="ExternalOutput").ap()
    gnn_kernel(nc, **args)
    r = _run(nc, [arrays], core_ids=[0])
    return r.results[0]["out_0_dram"]
```
